# Optimizing a Trainium2 kernel written in Bass

```python
import numpy as np
import jax
import jax.numpy as jnp

def _softmax(x, axis=-1):
    return jax.nn.softmax(x, axis=axis)

def _gelu(x):
    return jax.nn.gelu(x, approximate=True)

def _silu(x):
    return jax.nn.silu(x)

def _sigmoid(x):
    return jax.nn.sigmoid(x)

def _layernorm(x, axis=-1, eps=1e-05):
    m = jnp.mean(x, axis=axis, keepdims=True)
    v = jnp.var(x, axis=axis, keepdims=True)
    return (x - m) / jnp.sqrt(v + eps)

def _scatter_add(tgt, idx, src, axis=0):
    return tgt.at[idx].add(src)

def _segment_sum(src, seg, n):
    return jax.ops.segment_sum(src, seg, n)
kernel_name = 'mk_decoder_postln_d1_seqx_r4_614424'

def setup_inputs(seed: int=0):
    np.random.seed(seed)
    _w = jnp.asarray

    def _rec_inputs():
        import jax
        import jax.numpy as jnp
        _rk = jax.random.key(seed)
        x = -0.0003929 + 0.9999 * jax.random.normal(jax.random.fold_in(_rk, 1), (2, 512, 512), jnp.float32)
        _lenS = 512 - jax.random.randint(jax.random.fold_in(_rk, 7), (2,), 0, max(1, 512 // 4) + 1, jnp.int32)
        _lenS2 = 1024 - jax.random.randint(jax.random.fold_in(_rk, 8), (2,), 0, max(1, 1024 // 4) + 1, jnp.int32)
        _ctx_1024P = jax.random.normal(jax.random.fold_in(_rk, 11), (2, 16, 256), jnp.float32)
        _ctx_1024c = jax.random.dirichlet(jax.random.fold_in(_rk, 511), 0.3 * jnp.ones((16,), jnp.float32), (2, 1024))
        _ctx_1024t = jnp.einsum('bsk,bkd->bsd', _ctx_1024c, _ctx_1024P)
        _ctx_1024t = _ctx_1024t * jax.lax.rsqrt(jnp.mean(jnp.square(_ctx_1024t)) + 1e-12) * 0.953939
        ctx_1024 = -0.000494167 + 1.00018 * (_ctx_1024t + 0.3 * jax.random.normal(jax.random.fold_in(_rk, 611), (2, 1024, 256), jnp.float32))
        _validS = jnp.arange(512)[None, :] < _lenS[:, None]
        _validS2 = jnp.arange(1024)[None, :] < _lenS2[:, None]
        _causal = jnp.tril(jnp.ones((512, 512), dtype=bool))
        mask_BxS2_bf1 = jnp.ones((2, 1024), dtype=bool)
        return (x, ctx_1024, mask_BxS2_bf1)
    x, ctx_1024, mask_BxS2_bf1 = _rec_inputs()

    def _L0_attn_setup():
        import jax, jax.numpy as jnp
        import numpy as np
        D_MODEL = 512
        N_HEADS = 32
        HEAD_DIM = D_MODEL // N_HEADS
        B, T = (4, 1024)

        def _reference_tuple_inner(x, W_in, W_out, log_A, W_dt, b_dt):
            Bsz, Tlen, D = x.shape
            H, hd = log_A.shape
            xp = jnp.einsum('btd,ed->bte', x, W_in)
            dt = jax.nn.softplus(jnp.einsum('btd,hd->bth', xp, W_dt) + b_dt)
            A_cont = -jnp.exp(log_A)
            a = jnp.exp(dt[..., None] * A_cont)
            xh = xp.reshape(Bsz, Tlen, H, hd)

            def combine(c1, c2):
                a1, u1 = c1
                a2, u2 = c2
                return (a1 * a2, a2 * u1 + u2)
            _, ys = jax.lax.associative_scan(combine, (a, xh), axis=1)
            s = ys[:, -1]
            y = jnp.einsum('btd,ed->bte', ys.reshape(Bsz, Tlen, D), W_out)
            return (y, s)
        key = jax.random.key(seed)
        ks = jax.random.split(key, 6)
        return {'x': jax.random.normal(ks[0], (B, T, D_MODEL), dtype=jnp.float32), 'W_in': jax.random.normal(ks[1], (D_MODEL, D_MODEL), dtype=jnp.float32) * (1.0 / np.sqrt(D_MODEL)), 'W_out': jax.random.normal(ks[2], (D_MODEL, D_MODEL), dtype=jnp.float32) * (1.0 / np.sqrt(D_MODEL)), 'log_A': jax.random.normal(ks[3], (N_HEADS, HEAD_DIM), dtype=jnp.float32) * 0.02, 'W_dt': jax.random.normal(ks[4], (N_HEADS, D_MODEL), dtype=jnp.float32) * (1.0 / np.sqrt(D_MODEL)), 'b_dt': jax.random.normal(ks[5], (N_HEADS,), dtype=jnp.float32) * 0.02}
    _L0_attn_all = _L0_attn_setup()
    _L0_attn_in = {k: v for k, v in _L0_attn_all.items() if k in ('W_in', 'W_out', 'log_A', 'W_dt', 'b_dt')}
    del _L0_attn_all

    def _L0_xattn_setup():
        import jax, jax.numpy as jnp
        import numpy as np
        N_HEADS = 16
        N_KV_HEADS = 8
        HEAD_DIM = 128
        D_TEXT = 512
        D_VISION = 256
        GROUPS = N_HEADS // N_KV_HEADS
        key = jax.random.key(seed)
        ks = jax.random.split(key, 6)
        B, T_text, T_vis = (4, 512, 144)
        text_hidden = jax.random.normal(ks[0], (B, T_text, D_TEXT), dtype=jnp.float32)
        vision_tokens = jax.random.normal(ks[1], (B, T_vis, D_VISION), dtype=jnp.float32)
        vision_mask = jnp.ones((B, T_vis), dtype=bool)
        s = 0.02
        Wq = jax.random.normal(ks[2], (D_TEXT, N_HEADS * HEAD_DIM), dtype=jnp.float32) * s
        Wk = jax.random.normal(ks[3], (D_VISION, N_KV_HEADS * HEAD_DIM), dtype=jnp.float32) * s
        Wv = jax.random.normal(ks[4], (D_VISION, N_KV_HEADS * HEAD_DIM), dtype=jnp.float32) * s
        Wo = jax.random.normal(ks[5], (N_HEADS * HEAD_DIM, D_TEXT), dtype=jnp.float32) * s
        return {'text_hidden': text_hidden, 'vision_tokens': vision_tokens, 'vision_mask': vision_mask, 'Wq': Wq, 'Wk': Wk, 'Wv': Wv, 'Wo': Wo}
    _L0_xattn_all = _L0_xattn_setup()
    _L0_xattn_in = {k: v for k, v in _L0_xattn_all.items() if k in ('Wq', 'Wk', 'Wv', 'Wo')}
    del _L0_xattn_all

    def _L0_ffn_setup():
        import jax, jax.numpy as jnp
        import numpy as np
        B, S, D = (2, 512, 512)
        H, KV, HD = (16, 4, 128)
        E, F, TOPK = (8, 1024, 2)
        THETA = 1000000.0
        EPS = 1e-05

        def rmsnorm(x, w):
            var = jnp.mean(jnp.square(x), axis=-1, keepdims=True)
            return x * jax.lax.rsqrt(var + EPS) * w

        def rope_cos_sin(seq_len):
            inv_freq = 1.0 / THETA ** (jnp.arange(0, HD, 2, dtype=jnp.float32) / HD)
            ang = jnp.arange(seq_len, dtype=jnp.float32)[:, None] * inv_freq[None, :]
            return (jnp.cos(ang)[None, :, None, :], jnp.sin(ang)[None, :, None, :])

        def apply_rope(x, cos, sin):
            x1, x2 = jnp.split(x, 2, axis=-1)
            return jnp.concatenate([x1 * cos - x2 * sin, x2 * cos + x1 * sin], axis=-1)

        def attention(x, wq, wk, wv, wo):
            b, s, _ = x.shape
            q = (x @ wq).reshape(b, s, H, HD)
            k = (x @ wk).reshape(b, s, KV, HD)
            v = (x @ wv).reshape(b, s, KV, HD)
            cos, sin = rope_cos_sin(s)
            q = apply_rope(q, cos, sin)
            k = apply_rope(k, cos, sin)
            rep = H // KV
            k = jnp.repeat(k, rep, axis=2)
            v = jnp.repeat(v, rep, axis=2)
            scores = jnp.einsum('bqhd,bkhd->bhqk', q, k) / np.sqrt(HD)
            causal = jnp.tril(jnp.ones((s, s), dtype=bool))
            scores = jnp.where(causal[None, None], scores, jnp.finfo(scores.dtype).min)
            probs = jax.nn.softmax(scores, axis=-1)
            out = jnp.einsum('bhqk,bkhd->bqhd', probs, v).reshape(b, s, H * HD)
            return out @ wo

        def moe(x, gate_w, w1, w3, w2):
            b, s, d = x.shape
            xt = x.reshape(b * s, d)
            logits = xt @ gate_w
            topv, topi = jax.lax.top_k(logits, TOPK)
            probs = jax.nn.softmax(topv, axis=-1)
            w = jnp.zeros_like(logits)
            for kk in range(TOPK):
                w = w + jax.nn.one_hot(topi[:, kk], E, dtype=logits.dtype) * probs[:, kk:kk + 1]
            out = jnp.zeros_like(xt)
            for e in range(E):
                h = jax.nn.silu(xt @ w1[e]) * (xt @ w3[e])
                out = out + w[:, e:e + 1] * (h @ w2[e])
            return out.reshape(b, s, d)
        key = jax.random.key(seed)
        ks = jax.random.split(key, 10)
        init = lambda k, shape: jax.random.normal(k, shape, jnp.float32) * 0.02
        return {'hidden_states': jax.random.normal(ks[0], (B, S, D), jnp.float32), 'norm1_w': jnp.ones((D,), jnp.float32), 'norm2_w': jnp.ones((D,), jnp.float32), 'wq': init(ks[1], (D, H * HD)), 'wk': init(ks[2], (D, KV * HD)), 'wv': init(ks[3], (D, KV * HD)), 'wo': init(ks[4], (H * HD, D)), 'gate_w': init(ks[5], (D, E)), 'w1': init(ks[6], (E, D, F)), 'w3': init(ks[7], (E, D, F)), 'w2': init(ks[8], (E, F, D))}
    _L0_ffn_all = _L0_ffn_setup()
    _L0_ffn_in = {k: v for k, v in _L0_ffn_all.items() if k in ('norm1_w', 'norm2_w', 'wq', 'wk', 'wv', 'wo', 'gate_w', 'w1', 'w3', 'w2')}
    del _L0_ffn_all
    return {'x': x, 'ctx_1024': ctx_1024, 'mask_BxS2_bf1': mask_BxS2_bf1, 'L0_attn_W_in': _L0_attn_in['W_in'], 'L0_attn_W_out': _L0_attn_in['W_out'], 'L0_attn_log_A': _L0_attn_in['log_A'], 'L0_attn_W_dt': _L0_attn_in['W_dt'], 'L0_attn_b_dt': _L0_attn_in['b_dt'], 'L0_xattn_Wq': _L0_xattn_in['Wq'], 'L0_xattn_Wk': _L0_xattn_in['Wk'], 'L0_xattn_Wv': _L0_xattn_in['Wv'], 'L0_xattn_Wo': _L0_xattn_in['Wo'], 'L0_ffn_norm1_w': _L0_ffn_in['norm1_w'], 'L0_ffn_norm2_w': _L0_ffn_in['norm2_w'], 'L0_ffn_wq': _L0_ffn_in['wq'], 'L0_ffn_wk': _L0_ffn_in['wk'], 'L0_ffn_wv': _L0_ffn_in['wv'], 'L0_ffn_wo': _L0_ffn_in['wo'], 'L0_ffn_gate_w': _L0_ffn_in['gate_w'], 'L0_ffn_w1': _L0_ffn_in['w1'], 'L0_ffn_w3': _L0_ffn_in['w3'], 'L0_ffn_w2': _L0_ffn_in['w2']}

def reference(x, ctx_1024, mask_BxS2_bf1, L0_attn_W_in, L0_attn_W_out, L0_attn_log_A, L0_attn_W_dt, L0_attn_b_dt, L0_xattn_Wq, L0_xattn_Wk, L0_xattn_Wv, L0_xattn_Wo, L0_ffn_norm1_w, L0_ffn_norm2_w, L0_ffn_wq, L0_ffn_wk, L0_ffn_wv, L0_ffn_wo, L0_ffn_gate_w, L0_ffn_w1, L0_ffn_w3, L0_ffn_w2):
    import jax
    import jax.numpy as jnp

    def _L0_attn_ref(x, W_in, W_out, log_A, W_dt, b_dt):
        import jax, jax.numpy as jnp
        import numpy as np
        D_MODEL = 512
        N_HEADS = 32
        HEAD_DIM = D_MODEL // N_HEADS
        B, T = (4, 1024)

        def _reference_tuple_inner(x, W_in, W_out, log_A, W_dt, b_dt):
            Bsz, Tlen, D = x.shape
            H, hd = log_A.shape
            xp = jnp.einsum('btd,ed->bte', x, W_in)
            dt = jax.nn.softplus(jnp.einsum('btd,hd->bth', xp, W_dt) + b_dt)
            A_cont = -jnp.exp(log_A)
            a = jnp.exp(dt[..., None] * A_cont)
            xh = xp.reshape(Bsz, Tlen, H, hd)

            def combine(c1, c2):
                a1, u1 = c1
                a2, u2 = c2
                return (a1 * a2, a2 * u1 + u2)
            _, ys = jax.lax.associative_scan(combine, (a, xh), axis=1)
            s = ys[:, -1]
            y = jnp.einsum('btd,ed->bte', ys.reshape(Bsz, Tlen, D), W_out)
            return (y, s)
        return _reference_tuple_inner(x, W_in, W_out, log_A, W_dt, b_dt)[0]

    def _L0_xattn_ref(text_hidden, vision_tokens, vision_mask, Wq, Wk, Wv, Wo):
        import jax, jax.numpy as jnp
        import numpy as np
        N_HEADS = 16
        N_KV_HEADS = 8
        HEAD_DIM = 128
        D_TEXT = 512
        D_VISION = 256
        GROUPS = N_HEADS // N_KV_HEADS
        B, T_text, _ = text_hidden.shape
        T_vis = vision_tokens.shape[1]
        scale = jnp.float32(np.sqrt(HEAD_DIM))
        q = (text_hidden @ Wq).reshape(B, T_text, N_HEADS, HEAD_DIM).transpose(0, 2, 1, 3)
        k = (vision_tokens @ Wk).reshape(B, T_vis, N_KV_HEADS, HEAD_DIM).transpose(0, 2, 1, 3)
        v = (vision_tokens @ Wv).reshape(B, T_vis, N_KV_HEADS, HEAD_DIM).transpose(0, 2, 1, 3)
        k = jnp.repeat(k, GROUPS, axis=1)
        v = jnp.repeat(v, GROUPS, axis=1)
        scores = jnp.einsum('bhtd,bhsd->bhts', q, k) / scale
        mask = vision_mask[:, None, None, :]
        scores = jnp.where(mask, scores, -jnp.inf)
        attn = jax.nn.softmax(scores, axis=-1)
        attn = jnp.nan_to_num(attn, nan=0.0)
        out = jnp.einsum('bhts,bhsd->bhtd', attn, v)
        out = out.transpose(0, 2, 1, 3).reshape(B, T_text, N_HEADS * HEAD_DIM)
        return out @ Wo

    def _L0_ffn_ref(hidden_states, norm1_w, norm2_w, wq, wk, wv, wo, gate_w, w1, w3, w2):
        import jax, jax.numpy as jnp
        import numpy as np
        B, S, D = (2, 512, 512)
        H, KV, HD = (16, 4, 128)
        E, F, TOPK = (8, 1024, 2)
        THETA = 1000000.0
        EPS = 1e-05

        def rmsnorm(x, w):
            var = jnp.mean(jnp.square(x), axis=-1, keepdims=True)
            return x * jax.lax.rsqrt(var + EPS) * w

        def rope_cos_sin(seq_len):
            inv_freq = 1.0 / THETA ** (jnp.arange(0, HD, 2, dtype=jnp.float32) / HD)
            ang = jnp.arange(seq_len, dtype=jnp.float32)[:, None] * inv_freq[None, :]
            return (jnp.cos(ang)[None, :, None, :], jnp.sin(ang)[None, :, None, :])

        def apply_rope(x, cos, sin):
            x1, x2 = jnp.split(x, 2, axis=-1)
            return jnp.concatenate([x1 * cos - x2 * sin, x2 * cos + x1 * sin], axis=-1)

        def attention(x, wq, wk, wv, wo):
            b, s, _ = x.shape
            q = (x @ wq).reshape(b, s, H, HD)
            k = (x @ wk).reshape(b, s, KV, HD)
            v = (x @ wv).reshape(b, s, KV, HD)
            cos, sin = rope_cos_sin(s)
            q = apply_rope(q, cos, sin)
            k = apply_rope(k, cos, sin)
            rep = H // KV
            k = jnp.repeat(k, rep, axis=2)
            v = jnp.repeat(v, rep, axis=2)
            scores = jnp.einsum('bqhd,bkhd->bhqk', q, k) / np.sqrt(HD)
            causal = jnp.tril(jnp.ones((s, s), dtype=bool))
            scores = jnp.where(causal[None, None], scores, jnp.finfo(scores.dtype).min)
            probs = jax.nn.softmax(scores, axis=-1)
            out = jnp.einsum('bhqk,bkhd->bqhd', probs, v).reshape(b, s, H * HD)
            return out @ wo

        def moe(x, gate_w, w1, w3, w2):
            b, s, d = x.shape
            xt = x.reshape(b * s, d)
            logits = xt @ gate_w
            topv, topi = jax.lax.top_k(logits, TOPK)
            probs = jax.nn.softmax(topv, axis=-1)
            w = jnp.zeros_like(logits)
            for kk in range(TOPK):
                w = w + jax.nn.one_hot(topi[:, kk], E, dtype=logits.dtype) * probs[:, kk:kk + 1]
            out = jnp.zeros_like(xt)
            for e in range(E):
                h = jax.nn.silu(xt @ w1[e]) * (xt @ w3[e])
                out = out + w[:, e:e + 1] * (h @ w2[e])
            return out.reshape(b, s, d)
        attn_out = attention(rmsnorm(hidden_states, norm1_w), wq, wk, wv, wo)
        h = hidden_states + attn_out
        out = h + moe(rmsnorm(h, norm2_w), gate_w, w1, w3, w2)
        return out
    x = _layernorm(x + _L0_attn_ref(x, L0_attn_W_in, L0_attn_W_out, L0_attn_log_A, L0_attn_W_dt, L0_attn_b_dt), axis=-1)
    x = _layernorm(x + _L0_xattn_ref(x, ctx_1024, mask_BxS2_bf1, L0_xattn_Wq, L0_xattn_Wk, L0_xattn_Wv, L0_xattn_Wo), axis=-1)
    x = _layernorm(x + _L0_ffn_ref(x, L0_ffn_norm1_w, L0_ffn_norm2_w, L0_ffn_wq, L0_ffn_wk, L0_ffn_wv, L0_ffn_wo, L0_ffn_gate_w, L0_ffn_w1, L0_ffn_w3, L0_ffn_w2), axis=-1)
    return x

_drawn_inputs = setup_inputs


def setup_inputs(seed=0):
    import zlib

    import numpy as np

    out = dict(_drawn_inputs(seed))
    spreads = {'L0_ffn_norm1_w': (1.0, 0.6), 'L0_ffn_norm2_w': (1.0, 0.6)}
    factors = {'L0_attn_log_A': 7.991,
     'L0_attn_b_dt': 8.0,
     'L0_xattn_Wq': 7.4,
     'L0_xattn_Wk': 7.255,
     'L0_ffn_wq': 7.16,
     'L0_ffn_wk': 7.912}
    for name, (base, spread) in spreads.items():
        noise = np.random.default_rng([zlib.crc32(name.encode()), seed]).standard_normal(out[name].shape)
        drawn = base * np.exp(spread * noise) if base else spread * noise
        out[name] = jnp.asarray(drawn.astype(out[name].dtype))
    for name, factor in factors.items():
        out[name] = (out[name] * factor).astype(out[name].dtype)
    return out
```

```python
from contextlib import ExitStack

import concourse.bass as bass
import numpy as np
from concourse import mybir

F32 = mybir.dt.float32
F16 = mybir.dt.float16
U8 = mybir.dt.uint8
U32 = mybir.dt.uint32
I32 = mybir.dt.int32
ALU = mybir.AluOpType
ACT = mybir.ActivationFunctionType
AX_X = mybir.AxisListType.X

P = 128
B, S, D = 2, 512, 512
T = B * S
NT = T // P
TPB = S // P
DC = D // P
S2, DCTX = 1024, 256
HD = 128
EPS = 1e-5
NEG = -1e30
PSCALE = 1024.0
SCORE_SCALE = float(1.0 / np.sqrt(HD))
E, F = 8, 1024
FC = F // P
CAP = 384
CTL = CAP // P
PAIRS = ((0, 0), (0, 1), (1, 0))


def wait_from(eng, sem, count):
    if isinstance(count, int) and count <= 0:
        return
    eng.wait_ge(sem, count)


def phase_semaphores(nc, phase):
    held = []

    def end():
        nc.clear_and_free_semaphores(held)
        nc.all_engine_barrier()

    phase.callback(end)

    def sem(name):
        held.append(nc.alloc_semaphore(name=name))
        return held[-1]

    return sem


def stand_apart(eng, passed):
    eng.sem_inc(passed, 1)


def split_banks(nc, sem, jobs, bank, ident, name):
    tr_done, hi_done, lo_done = sem(name + "_tr_done"), sem(name + "_hi_done"), sem(name + "_lo_done")
    nb = len(bank)

    def pe_job(pe, n):
        wait, blocks, _, _ = jobs[n]
        pe.wait_ge(*wait)
        if n >= nb:
            pe.wait_ge(lo_done, n - nb + 1)
        for src, off, rows, cols in blocks:
            last = nc.tensor.transpose(bank[n % nb][0:cols, off:off + rows], src, ident[0:rows, 0:rows])
        last.then_inc(tr_done, 1)

    def act_job(act, n):
        _, _, hi, _ = jobs[n]
        act.wait_ge(tr_done, n + 1)
        nc.scalar.copy(hi[0], hi[1](bank[n % nb])).then_inc(hi_done, 1)

    def dve_job(dve, n):
        _, _, hi, lo = jobs[n]
        dve.wait_ge(hi_done, n + 1)
        nc.vector.tensor_tensor(lo[0], lo[1](bank[n % nb]), hi[0], ALU.subtract).then_inc(lo_done, 1)

    return pe_job, act_job, dve_job, lo_done


def phase_ssm(nc, X, XT, CT, XG, x, ctxt, mask, W_in, W_out, log_A, W_dt, b_dt, consts, rope_in):
    identF, causal, maskb, flag, ropeC, ropeS = consts
    with ExitStack() as st:
        sem = phase_semaphores(nc, st)

        def sb(name, shape, dt):
            return st.enter_context(nc.sbuf_tensor(name, shape, dt))

        def pb(name, shape):
            return st.enter_context(nc.psum_tensor(name, shape, F32))

        win = sb("win", [P, DC, D], F32)
        wout = sb("wout", [P, DC, D], F32)
        wdt = sb("wdt", [32, D], F32)
        winT = sb("winT", [P, 2, DC, D], F16)
        woutT = sb("woutT", [P, 2, DC, D], F16)
        wdtT = sb("wdtT", [P, 2, DC, 32], F16)
        wdtR = sb("wdtR", [P, 2, DC, 32, 16], F16)
        ctx_in = sb("ctx_in", [P, 8, DCTX], F32)
        xp = sb("xp", [P, DC, T], F32)
        XPT = sb("XPT", [P, 2, DC, T], F16)
        logA = sb("logA", [P, DC], F32)
        negA = sb("negA", [P, DC], F32)
        bdt = sb("bdt", [P, DC], F32)
        zb = sb("zb", [P, 2, S], F32)
        za = sb("za", [P, 2, S], F32)
        dtb = sb("dtb", [P, 2, S], F32)
        dec = sb("dec", [P, 2, S], F32)
        ys = sb("ys", [P, 2, S], F32)
        mask_in = sb("mask_in", [P, B * S2], U8)
        anyv = sb("anyv", [P, B], F32)
        zeros = sb("zeros", [P, 2048], F32)
        zeros_done, zeroed = sem("zeros_done"), sem("zeroed")
        bank = [pb(f"bank{i}", [P, 512]) for i in range(8)]

        x_in = [sem(f"x_in{b}") for b in range(B)]
        tables_in, w_in, c_in, small_in = sem("tables_in"), sem("w_in"), sem("c_in"), sem("small_in")
        ident_zero, ident_done, causal_zero, causal_done = (sem("ident_zero"), sem("ident_done"),
                                                            sem("causal_zero"), sem("causal_done"))
        maskb_done, any_done, flag_done = sem("maskb_done"), sem("any_done"), sem("flag_done")
        rep_done, expA_done, negA_done = sem("rep_done"), sem("expA_done"), sem("negA_done")
        xp_ready, xp_hi, xp_f32, xp_lo = sem("xp_ready"), sem("xp_hi"), sem("xp_f32"), sem("xp_lo")
        z_ready, zb_done, za_abs, za_exp, za_ln = (sem("z_ready"), sem("zb_done"), sem("za_abs"),
                                                   sem("za_exp"), sem("za_ln"))
        dt_done, dec_done, scan_done, ys_hi, ys_lo = (sem("dt_done"), sem("dec_done"), sem("scan_done"),
                                                      sem("ys_hi"), sem("ys_lo"))
        y_ready, y_added = sem("y_ready"), sem("y_added")

        YST = XT
        whole = lambda ap: ap[:, :]

        jobs = []
        for k in range(DC):
            jobs.append(((w_in, 16), [(win[:, m, k * P:(k + 1) * P], m * P, P, P) for m in range(DC)],
                         (winT[:, 0, k, :], whole), (winT[:, 1, k, :], whole)))
        for i in range(NT):
            as4 = lambda ap: ap[:, :].rearrange("p (k t) -> p k t", k=DC)
            jobs.append(((x_in[i // TPB], 16), [(X[:, i, k * P:(k + 1) * P], k * P, P, P) for k in range(DC)],
                         (XT[:, 0, :, i * P:(i + 1) * P], as4), (XT[:, 1, :, i * P:(i + 1) * P], as4)))
        as_dt = lambda ap: ap[:, 0:DC * 32].rearrange("p (k h) -> p k h", k=DC)
        jobs.append(((w_in, 32), [(wdt[:, k * P:(k + 1) * P], k * 32, 32, P) for k in range(DC)],
                     (wdtT[:, 0, :, :], as_dt), (wdtT[:, 1, :, :], as_dt)))
        first_jobs = len(jobs)
        late = []
        for k in range(DC):
            late.append(((w_in, 48), [(wout[:, m, k * P:(k + 1) * P], m * P, P, P) for m in range(DC)],
                         (woutT[:, 0, k, :], whole), (woutT[:, 1, k, :], whole)))
        ctx_jobs = len(late)
        for i in range(8):
            pair = lambda ap: ap[:, :].rearrange("p (c t) -> p c t", c=2)
            late.append(((c_in, 16 * (i // 4 + 1)),
                         [(ctx_in[:, 2 * (i % 4) + j, c * P:(c + 1) * P], c * 2 * P + j * P, P, P) for c in range(2) for j in range(2)],
                         (CT[:, 0, :, i * 2 * P:(i + 1) * 2 * P], pair), (CT[:, 1, :, i * 2 * P:(i + 1) * 2 * P], pair)))
        tr_pe, tr_act, tr_dve, tr_lo = split_banks(nc, sem, jobs, bank[0:4], identF, "first")
        late_pe, late_act, late_dve, late_lo = split_banks(nc, sem, late, bank[4:6], identF, "late")

        block = st.enter_context(nc.Block())

        @block.sync
        def _(sp):
            sp.dma_start(win[:], W_in.rearrange("(m p) d -> p m d", p=P)).then_inc(w_in, 16)
            for b in range(B):
                sp.dma_start(X[:, b * TPB:(b + 1) * TPB, :], x[b].rearrange("(t p) d -> p t d", p=P)).then_inc(x_in[b], 16)
            sp.wait_ge(w_in, 16)
            sp.dma_start(wdt[:], W_dt).then_inc(w_in, 16)
            sp.wait_ge(w_in, 32)
            sp.dma_start(wout[:], W_out.rearrange("(m p) d -> p m d", p=P)).then_inc(w_in, 16)
            sp.dma_start(ropeC[:], rope_in[0]).then_inc(tables_in, 16)
            sp.dma_start(ropeS[:], rope_in[1]).then_inc(tables_in, 16)
            sp.dma_start(mask_in[:], mask.rearrange("b s -> (b s)").partition_broadcast(P)).then_inc(tables_in, 16)
            for b in range(B):
                if b:
                    sp.wait_ge(late_lo, ctx_jobs + 4)
                sp.dma_start(ctx_in[:], ctxt[b].rearrange("(t p) d -> p t d", p=P)).then_inc(c_in, 16)
            sp.wait_ge(zeros_done, 1)
            xg = XG.rearrange("(n p r) d -> n p (r d)", p=P, r=4)
            for i in range(E * CAP // (4 * P)):
                sp.dma_start(xg[i], zeros[:]).then_inc(zeroed, 16)
            sp.wait_ge(zeroed, 16 * (E * CAP // (4 * P)))

        @block.gpsimd
        def _(pool):
            nc.gpsimd.memset(identF[:], 0.0).then_inc(ident_zero, 1)
            nc.gpsimd.memset(zeros[:], 0.0).then_inc(zeros_done, 1)
            pool.wait_ge(ident_zero, 1)
            nc.gpsimd.affine_select(out=identF[:], in_=identF[:], compare_op=ALU.not_equal, fill=1.0, base=0,
                                    pattern=[[-1, P]], channel_multiplier=1).then_inc(ident_done, 1)
            nc.gpsimd.memset(causal[:], 0.0).then_inc(causal_zero, 1)
            pool.wait_ge(causal_zero, 1)
            nc.gpsimd.affine_select(out=causal[:, S - P:S], in_=causal[:, S - P:S], compare_op=ALU.is_ge, fill=NEG,
                                    base=0, pattern=[[-1, P]], channel_multiplier=1).then_inc(causal_done, 1)
            pool.wait_ge(causal_done, 1)
            pool.wait_ge(tr_lo, first_jobs)
            for hl in range(2):
                last = nc.gpsimd.tensor_copy(wdtR[:, hl, :, :, :], wdtT[:, hl, :, :].unsqueeze(3).broadcast_to([P, DC, 32, 16]))
                last.then_inc(rep_done, 1)

        @block.tensor
        def _(pe):
            pe.wait_ge(ident_done, 1)
            for n in range(len(jobs)):
                tr_pe(pe, n)
            pe.wait_ge(tr_lo, first_jobs)
            for n in range(2 * DC):
                m, b = n % DC, n // DC
                if n >= 2:
                    pe.wait_ge(xp_lo, n - 1)
                for i, (hw, hx) in enumerate(PAIRS):
                    for k in range(DC):
                        last = nc.tensor.matmul(bank[6 + n % 2][:, :], winT[:, hw, k, m * P:(m + 1) * P],
                                                XT[:, hx, k, b * S:(b + 1) * S], start=(i + k == 0),
                                                stop=(i == 2 and k == DC - 1))
                last.then_inc(xp_ready, 1)
            for n in range(len(late)):
                late_pe(pe, n)
            pe.wait_ge(rep_done, 2)
            pe.wait_ge(late_lo, len(late))
            for n in range(2 * DC):
                m, b = n % DC, n // DC
                pe.wait_ge(xp_lo, DC * (b + 1))
                if n >= 2:
                    pe.wait_ge(za_abs, n - 1)
                    pe.wait_ge(zb_done, n - 1)
                for i, (hw, hx) in enumerate(PAIRS):
                    for k in range(DC):
                        last = nc.tensor.matmul(bank[n % 2][:, :],
                                                wdtR[:, hw, k, m * 8:(m + 1) * 8, :].rearrange("p h c -> p (h c)"),
                                                XPT[:, hx, k, b * S:(b + 1) * S], start=(i + k == 0),
                                                stop=(i == 2 and k == DC - 1))
                last.then_inc(z_ready, 1)
            for i in range(NT):
                pe.wait_ge(ys_lo, DC * (i // TPB + 1))
                if i >= 2:
                    pe.wait_ge(y_added, i - 1)
                for q, (hy, hw) in enumerate(PAIRS):
                    for k in range(DC):
                        last = nc.tensor.matmul(bank[2 + i % 2][:, :], YST[:, hy, k, i * P:(i + 1) * P],
                                                woutT[:, hw, k, :], start=(q + k == 0), stop=(q == 2 and k == DC - 1))
                last.then_inc(y_ready, 1)

        @block.scalar
        def _(act):
            act.dma_start(logA[:], log_A.rearrange("(m h) c -> (h c) m", m=DC), allow_slow_non_contiguous=True).then_inc(small_in, 16)
            for h in range(8):
                act.dma_start(bdt[h * 16:(h + 1) * 16, :],
                              b_dt.rearrange("(m h) -> h m", h=8)[h].partition_broadcast(16),
                              allow_slow_non_contiguous=True).then_inc(small_in, 16)
            for n in range(len(jobs)):
                tr_act(act, n)
            for n in range(2 * DC):
                m, b = n % DC, n // DC
                act.wait_ge(xp_ready, n + 1)
                nc.scalar.copy(XPT[:, 0, m, b * S:(b + 1) * S], bank[6 + n % 2][:, :]).then_inc(xp_hi, 1)
                nc.scalar.copy(xp[:, m, b * S:(b + 1) * S], bank[6 + n % 2][:, :]).then_inc(xp_f32, 1)
            for n in range(len(late)):
                late_act(act, n)
            act.wait_ge(small_in, 144)
            nc.scalar.activation(logA[:], logA[:], ACT.Exp).then_inc(expA_done, 1)
            for n in range(2 * DC):
                m = n % DC
                act.wait_ge(z_ready, n + 1)
                act.wait_ge(zb_done, n + 1)
                if n >= 2:
                    act.wait_ge(dt_done, n - 1)
                nc.scalar.activation(za[:, n % 2, :], bank[n % 2][:, :], ACT.Abs, bias=bdt[:, m:m + 1]).then_inc(za_abs, 1)
                act.wait_ge(za_abs, n + 1)
                nc.scalar.activation(za[:, n % 2, :], za[:, n % 2, :], ACT.Exp, scale=-1.0).then_inc(za_exp, 1)
                act.wait_ge(za_exp, n + 1)
                nc.scalar.activation(za[:, n % 2, :], za[:, n % 2, :], ACT.Ln, bias=1.0).then_inc(za_ln, 1)
                act.wait_ge(dt_done, n + 1)
                act.wait_ge(negA_done, 1)
                if n >= 2:
                    act.wait_ge(scan_done, n - 1)
                nc.scalar.activation(dec[:, n % 2, :], dtb[:, n % 2, :], ACT.Exp, scale=negA[:, m:m + 1]).then_inc(dec_done, 1)
                act.wait_ge(scan_done, n + 1)
                nc.scalar.copy(YST[:, 0, m, (n // DC) * S:(n // DC + 1) * S], ys[:, n % 2, :]).then_inc(ys_hi, 1)

        @block.vector
        def _(dve):
            for n in range(len(jobs)):
                tr_dve(dve, n)
            for n in range(2 * DC):
                m, b = n % DC, n // DC
                dve.wait_ge(xp_hi, n + 1)
                dve.wait_ge(xp_f32, n + 1)
                nc.vector.tensor_tensor(XPT[:, 1, m, b * S:(b + 1) * S], xp[:, m, b * S:(b + 1) * S],
                                        XPT[:, 0, m, b * S:(b + 1) * S], ALU.subtract).then_inc(xp_lo, 1)
            for n in range(len(late)):
                late_dve(dve, n)
            dve.wait_ge(tables_in, 48)
            nc.vector.tensor_scalar(maskb[:].rearrange("p b s -> p (b s)"), mask_in[:], -1.0, -NEG, ALU.add,
                                    ALU.mult).then_inc(maskb_done, 1)
            for b in range(B):
                last = nc.vector.tensor_reduce(anyv[:, b:b + 1], mask_in[:, b * S2:(b + 1) * S2], AX_X, ALU.max)
            last.then_inc(any_done, 1)
            dve.wait_ge(any_done, 1)
            nc.vector.tensor_scalar(flag[:], anyv[:], PSCALE, None, ALU.mult).then_inc(flag_done, 1)
            dve.wait_ge(expA_done, 1)
            nc.vector.tensor_scalar(negA[:], logA[:], -1.0, None, ALU.mult).then_inc(negA_done, 1)
            for n in range(2 * DC):
                m, b = n % DC, n // DC
                dve.wait_ge(z_ready, n + 1)
                if n >= 1:
                    dve.wait_ge(scan_done, n)
                nc.vector.tensor_scalar(zb[:, n % 2, :], bank[n % 2][:, :], bdt[:, m:m + 1], 0.0, ALU.add,
                                        ALU.max).then_inc(zb_done, 1)
                dve.wait_ge(zb_done, n + 1)
                dve.wait_ge(za_ln, n + 1)
                if n >= 2:
                    dve.wait_ge(dec_done, n - 1)
                nc.vector.tensor_tensor(dtb[:, n % 2, :], zb[:, n % 2, :], za[:, n % 2, :], ALU.add).then_inc(dt_done, 1)
                dve.wait_ge(dec_done, n + 1)
                if n >= 2:
                    dve.wait_ge(ys_lo, n - 1)
                    dve.wait_ge(ys_hi, n - 1)
                nc.vector.tensor_tensor_scan(ys[:, n % 2, :], dec[:, n % 2, :], xp[:, m, b * S:(b + 1) * S], 0.0,
                                             ALU.mult, ALU.add).then_inc(scan_done, 1)
                dve.wait_ge(ys_hi, n + 1)
                nc.vector.tensor_tensor(YST[:, 1, m, b * S:(b + 1) * S], ys[:, n % 2, :],
                                        YST[:, 0, m, b * S:(b + 1) * S], ALU.subtract).then_inc(ys_lo, 1)
            for i in range(NT):
                dve.wait_ge(y_ready, i + 1)
                nc.vector.tensor_tensor(X[:, i, :], bank[2 + i % 2][:, :], X[:, i, :], ALU.add).then_inc(y_added, 1)


def phase_norm(nc, name, X, identF, XT=None, norm_w=None, layer=True, out=None, keep=None, add=None,
               rows=None, fetch=()):
    with ExitStack() as st:
        sem = phase_semaphores(nc, st)

        def sb(n, shape, dt):
            return st.enter_context(nc.sbuf_tensor(f"{name}_{n}", shape, dt))

        stats = sb("stats", [P, NT, 6], F32)
        mv = sb("mv", [P, NT, 2], F32)
        ve = sb("ve", [P, NT], F32)
        half = sb("half", [P, 1], F32)
        rstd = sb("rstd", [P, NT], F32)
        sq = sb("sq", [P, 2, D], F32)
        ms = sb("ms", [P, NT], F32)
        me = sb("me", [P, NT], F32)
        rr = sb("rr", [P, NT], F32)
        wb = sb("wb", [P, D], F32)
        XR = 4 if rows is None else NT
        xw = sb("xw", [P, 4, D], F32) if rows is None else rows
        bank = [st.enter_context(nc.psum_tensor(f"{name}_bank{i}", [P, 512], F32)) for i in range(4)]

        s = lambda n: sem(f"{name}_{n}")
        half_done, w_in, stats_done, mv_done, ve_done, rstd_done, ln_done = (
            s("half_done"), s("w_in"), s("stats_done"), s("mv_done"), s("ve_done"), s("rstd_done"), s("ln_done"))
        ms_done, me_done, rr_done, xr_done, xw_done, out_done = (
            s("ms_done"), s("me_done"), s("rr_done"), s("xr_done"), s("xw_done"), s("out_done"))
        rms, fetched = norm_w is not None, s("fetched")
        jobs = []
        if XT is not None:
            for i in range(NT):
                src = xw[:, i % XR] if rms else X[:, i]
                as4 = lambda ap: ap[:, :].rearrange("p (k t) -> p k t", k=DC)
                jobs.append(((xw_done if rms else ln_done, i + 1),
                             [(src[:, k * P:(k + 1) * P], k * P, P, P) for k in range(DC)],
                             (XT[:, 0, :, i * P:(i + 1) * P], as4), (XT[:, 1, :, i * P:(i + 1) * P], as4)))
        tr_pe, tr_act, tr_dve, tr_lo = split_banks(nc, sem, jobs, bank, identF, name)

        block = st.enter_context(nc.Block())

        @block.sync
        def _(sp):
            for dst, src in fetch:
                sp.dma_start(dst, src).then_inc(fetched, 16)
            if rms:
                sp.dma_start(wb[:], norm_w.partition_broadcast(P)).then_inc(w_in, 16)
                sp.wait_ge(w_in, 16)
            if out is not None:
                for i in range(NT):
                    sp.wait_ge(ln_done, i + 1)
                    sp.dma_start(out[i // TPB, (i % TPB) * P:(i % TPB + 1) * P, :], X[:, i, :]).then_inc(out_done, 16)
                sp.wait_ge(out_done, 16 * NT)
            if fetch:
                sp.wait_ge(fetched, 16 * len(fetch))

        @block.gpsimd
        def _(pool):
            nc.gpsimd.memset(half[:], -0.5).then_inc(half_done, 1)
            pool.wait_ge(half_done, 1)
            if rms:
                pool.wait_ge(w_in, 16)
            for i in range(NT if layer else 0):
                pool.wait_ge(mv_done, i + 1)
                nc.gpsimd.tensor_scalar(ve[:, i:i + 1], mv[:, i, 1:2], EPS, 1.0, ALU.add, ALU.mult).then_inc(ve_done, 1)
                pool.wait_ge(ve_done, i + 1)
                nc.gpsimd.tensor_tensor(rstd[:, i:i + 1], ve[:, i:i + 1], half[:], ALU.pow).then_inc(rstd_done, 1)
            for i in range(NT + 1 if rms else 0):
                if i < NT:
                    pool.wait_ge(ms_done, i + 1)
                    nc.gpsimd.tensor_scalar(me[:, i:i + 1], ms[:, i:i + 1], 1.0 / D, EPS, ALU.mult, ALU.add).then_inc(me_done, 1)
                    pool.wait_ge(me_done, i + 1)
                    nc.gpsimd.tensor_tensor(rr[:, i:i + 1], me[:, i:i + 1], half[:], ALU.pow).then_inc(rr_done, 1)
                if i >= 1:
                    row = (i - 1) % XR
                    pool.wait_ge(xr_done, i)
                    if keep is not None:
                        nc.gpsimd.tensor_copy(keep[:, i - 1, :], X[:, i - 1, :])
                    if add is not None:
                        nc.gpsimd.tensor_tensor(X[:, i - 1, :], X[:, i - 1, :], add[:, i - 1, :], ALU.add)
                    nc.gpsimd.tensor_tensor(xw[:, row, :], xw[:, row, :], wb[:], ALU.mult).then_inc(xw_done, 1)

        @block.tensor
        def _(pe):
            for n in range(len(jobs)):
                tr_pe(pe, n)

        @block.scalar
        def _(act):
            if rms:
                for i in range(NT):
                    if layer:
                        act.wait_ge(ln_done, i + 1)
                    if i >= 2:
                        act.wait_ge(ms_done, i - 1)
                    nc.scalar.activation(sq[:, i % 2, :], X[:, i, :], ACT.Square, accum_out=ms[:, i:i + 1]).then_inc(ms_done, 1)
                    if i >= 1:
                        row = i - 1
                        act.wait_ge(rr_done, row + 1)
                        if row >= 4:
                            act.wait_ge(tr_lo, row - 3)
                        nc.scalar.activation(xw[:, row % XR, :], X[:, row, :], ACT.Copy, scale=rr[:, row:row + 1]).then_inc(xr_done, 1)
                    if i >= 2:
                        tr_act(act, i - 2)
                act.wait_ge(rr_done, NT)
                act.wait_ge(tr_lo, NT - 4)
                nc.scalar.activation(xw[:, (NT - 1) % XR, :], X[:, NT - 1, :], ACT.Copy,
                                     scale=rr[:, NT - 1:NT]).then_inc(xr_done, 1)
                tr_act(act, NT - 2)
                tr_act(act, NT - 1)
            else:
                for i in range(len(jobs)):
                    tr_act(act, i)

        @block.vector
        def _(dve):
            if layer:
                for i in range(NT):
                    nc.vector.bn_stats(stats[:, i, :], X[:, i, :]).then_inc(stats_done, 1)
                    dve.wait_ge(stats_done, i + 1)
                    nc.vector.bn_aggr(mv[:, i, :], stats[:, i, :]).then_inc(mv_done, 1)
                for i in range(NT):
                    dve.wait_ge(rstd_done, i + 1)
                    dve.wait_ge(mv_done, i + 1)
                    nc.vector.tensor_scalar(X[:, i, :], X[:, i, :], mv[:, i, 0:1], rstd[:, i:i + 1], ALU.subtract,
                                            ALU.mult).then_inc(ln_done, 1)
            for n in range(len(jobs)):
                tr_dve(dve, n)


def attention(nc, name, X, XT, KVT, identF, Wq, Wk, Wv, Wo, kv_heads, groups, keys, mask_of, flag, rope):
    NS = groups * TPB
    NBLK = keys // P
    NB = -(-NBLK // 4)
    KC = KVT.shape[2]
    WQ, WKV = DC * groups * HD, KC * HD
    causal = rope is not None
    JP, JO = 6, TPB
    JT = JP + JO
    NJ = 2 if causal else 1
    TAIL = 4
    if causal:
        proj = [("q", g) for g in range(groups)] + [("k", 0), ("v", 0)]
        slots = {0: ([("proj", 0)], []), 1: ([("proj", 1)], []), 2: ([("proj", 2)], []), 4: ([("proj", 3)], []),
                 5: ([("proj", 4)], []), 6: ([("proj", 5)], []), 8: ([("wo", 0)], []), 10: ([("wo", 1)], []),
                 12: ([("wo", 2)], []), 14: ([("wo", 3)], [])}
    else:
        proj = [("q", 0), ("q", 1), ("k", 0), ("k", 1), ("v", 0), ("v", 1)]
        slots = {0: ([("proj", 0)], []), 1: ([("proj", 1)], []), 2: ([("proj", 2)], []),
                 3: ([("proj", 3)], [("proj", 4)]), 4: ([("proj", 5)], []), 5: ([("wo", 0)], []),
                 6: ([("wo", 1)], []), 7: ([("wo", 2)], [("wo", 3)])}
    assert len(proj) == JP
    last_proj_slot = max(j for j, l in slots.items() if any(k == "proj" for k, _ in l[0] + l[1]))
    first_piece = last_proj_slot + 1

    def jobs_before(h):
        return JP if isinstance(h, int) and h == 0 else 2 * JP + JT * (h - 1)

    def projections_before(h):
        return jobs_before(h) if isinstance(h, int) and h <= 1 else jobs_before(h) - JO

    def slot_jobs(h, j, first, last, late=None):
        out, k = [], 0
        for jj in range(NS):
            for place, jobs in enumerate(slots.get(jj, ([], []))):
                for kind, i in jobs:
                    if kind == "wo" and first or kind == "proj" and last:
                        continue
                    if jj == j and late in (None, place):
                        out.append((kind, i, jobs_before(h) + k, k % NJ))
                    k += 1
        return out

    with ExitStack() as st:
        sem = phase_semaphores(nc, st)

        def sb(n, shape, dt):
            return st.enter_context(nc.sbuf_tensor(f"{name}_{n}", shape, dt))

        def pb(n, shape):
            return st.enter_context(nc.psum_tensor(f"{name}_{n}", shape, F32))

        WPraw = sb("WPraw", [P, WQ + 2 * WKV], F32)
        WP = sb("WP", [P, 2, WQ + 2 * WKV], F16)
        WOraw = sb("WOraw", [P, groups, D], F32)
        WO = sb("WO", [P, 2, groups, D], F16)
        QT = [sb(f"QT{b}", [P, 2, groups, S], F16) for b in range(B)]
        KT = [sb(f"KT{b}", [P, 2, keys], F16) for b in range(B)]
        V = [sb(f"V{b}", [P, 2, NBLK, HD], F16) for b in range(B)]
        OT = [sb(f"OT{b}", [P, 2, groups, S], F16) for b in range(B)]
        SC = [sb(f"SC{i}", [P, keys], F32) for i in range(2)]
        PN = [sb(f"PN{i}", [P, keys], F32) for i in range(2)]
        PT = [sb(f"PT{i}", [P, 2, NBLK, S], F16) for i in range(2)]
        mn = sb("mn", [P, 4], F32)
        sm = sb("sm", [P, 4], F32)
        rc = sb("rc", [P, 4], F32)
        rA = [sb(f"rA{i}", [P, S if causal else 1], F32) for i in range(2)]
        rB = [sb(f"rB{i}", [P, S if causal else 1], F32) for i in range(2)]
        psS = [pb(f"psS{i}", [P, NB * 512]) for i in range(2)]
        psT = [pb(f"psT{i}", [P, 512]) for i in range(2)]
        psO = pb("psO", [P, 512])
        psJ = [pb(f"psJ{i}", [P, 512]) for i in range(NJ)]

        s = lambda n: sem(f"{name}_{n}")
        wp_in, wp_hi, wp_done = s("wp_in"), s("wp_hi"), s("wp_done")
        wo_in, wo_hi, wo_done = s("wo_in"), s("wo_hi"), s("wo_done")
        scores_ready, masked, exp_done, recip_done, norm_done = (
            s("scores_ready"), s("masked"), s("exp_done"), s("recip_done"), s("norm_done"))
        tr_ready, tr_hi, tr_lo = s("tr_ready"), s("tr_hi"), s("tr_lo")
        pv_ready, o_hi, o_lo = s("pv_ready"), s("o_hi"), s("o_lo")
        job_ready, job_hi, job_free = s("job_ready"), s("job_hi"), s("job_free")
        rope_added, rope_hi, rope_done = s("rope_added"), s("rope_hi"), s("rope_done")

        pool_passed, dve_passed = s("pool_passed"), s("dve_passed")
        wp_pieces = [(WP[:, :, c:c + 512], WPraw[:, c:c + 512]) for c in range(0, WQ + 2 * WKV, 512)]
        wo_pieces = [(WO[:, :, g, :], WOraw[:, g, :]) for g in range(groups)]
        NWP, NWO = len(wp_pieces), len(wo_pieces)

        def step_pieces(kv, b, j, last_kv):
            i = j - first_piece
            if b == 0 and not last_kv and 0 <= i < NWP:
                return "wp", i, (kv + 1) * NWP + i
            if b == 1 and j < NWO:
                return "wo", j, kv * NWO + j
            return None

        wq_v = WP[:, :, 0:WQ].rearrange("p l (k g c) -> p l k g c", k=DC, g=groups)
        wk_v = WP[:, :, WQ:WQ + WKV].rearrange("p l (k c) -> p l k c", k=KC)
        wv_v = WP[:, :, WQ + WKV:].rearrange("p l (k c) -> p l k c", k=KC)

        def width(t):
            return (t + 1) * P if causal else keys

        def blocks(t, i):
            return range(4 * i, min(4 * i + 4, width(t) // P))

        block = st.enter_context(nc.Block())

        def halves(emit):
            for b in range(B):
                emit(b, 0, b, b == 0, False)
            yield 1, kv_heads - 1
            for b in range(B):
                emit(2 * (kv_heads - 1) + b, kv_heads - 1, b, False, b == B - 1)

        @block.sync
        def _(sp):
            def load_kv(kv):
                wait_from(sp, wp_done, kv * NWP)
                sp.dma_start(WPraw[:, 0:WQ].rearrange("p (k c) -> p k c", k=DC),
                             Wq[:, bass.ds(kv * (groups * HD), groups * HD)].rearrange("(k p) c -> p k c", p=P)).then_inc(wp_in, 16)
                sp.dma_start(WPraw[:, WQ:WQ + WKV].rearrange("p (k c) -> p k c", k=KC),
                             Wk[:, bass.ds(kv * HD, HD)].rearrange("(k p) c -> p k c", p=P)).then_inc(wp_in, 16)
                sp.dma_start(WPraw[:, WQ + WKV:].rearrange("p (k c) -> p k c", k=KC),
                             Wv[:, bass.ds(kv * HD, HD)].rearrange("(k p) c -> p k c", p=P)).then_inc(wp_in, 16)
                wait_from(sp, wo_done, kv * NWO)
                sp.dma_start(WOraw[:], Wo[bass.ds(kv * (groups * HD), groups * HD), :].rearrange(
                    "(g p) d -> p g d", p=P)).then_inc(wo_in, 16)

            load_kv(0)
            with sp.Fori(1, kv_heads) as kv:
                load_kv(kv)

        @block.gpsimd
        def _(pool):
            def piece_low(what, i, n):
                (dst, src), hi_done, done = ((wp_pieces[i], wp_hi, wp_done) if what == "wp" else
                                             (wo_pieces[i], wo_hi, wo_done))
                pool.wait_ge(hi_done, n + 1)
                nc.gpsimd.tensor_tensor(dst[:, 1], src, dst[:, 0], ALU.subtract).then_inc(done, 1)

            def rope_sum(h, b, i, job):
                par = (b * (JP - 1) + i) % 2
                pool.wait_ge(job_free, job + 1)
                nc.gpsimd.tensor_tensor(rA[par][:], rA[par][:], rB[par][:], ALU.add).then_inc(rope_added, 1)

            def rope_low(h, b, i):
                r = (JP - 1) * h + i
                par = (b * (JP - 1) + i) % 2
                pool.wait_ge(rope_hi, r + 1)
                dst = QT[b][:, :, i, :] if proj[i][0] == "q" else KT[b][:, :, :]
                nc.gpsimd.tensor_tensor(dst[:, 1, :], rA[par][:], dst[:, 0, :], ALU.subtract).then_inc(rope_done, 1)

            def half(h, kv, b, first, last):
                for j in range(NS):
                    n = h * NS + j
                    pool.wait_ge(recip_done, n + 1)
                    wait_from(pool, tr_ready, (n - 1) * NB)
                    w = width(j % TPB)
                    stand_apart(pool, pool_passed)
                    nc.gpsimd.tensor_scalar(PN[j % 2][:, 0:w], SC[j % 2][:, 0:w], rc[:, j % 4:j % 4 + 1],
                                            PSCALE if flag is None else flag[:, b:b + 1], ALU.mult,
                                            ALU.mult).then_inc(norm_done, 1)
                    turned = [(i, job) for kind, i, job, _ in slot_jobs(h, j, first, last)
                              if causal and kind == "proj" and proj[i][0] != "v"]
                    for i, job in turned:
                        rope_sum(h + 1, 1 - b, i, job)
                    piece = step_pieces(kv, b, j, isinstance(kv, int) and kv == kv_heads - 1)
                    if piece:
                        piece_low(*piece)
                    for i, job in turned:
                        rope_low(h + 1, 1 - b, i)

            if causal:
                for i in range(JP - 1):
                    rope_sum(0, 0, i, i)
                    rope_low(0, 0, i)
            mid = halves(half)
            lo, hi = next(mid)
            with pool.Fori(lo, hi) as kv:
                for b in range(B):
                    half(kv * 2 + b, kv, b, False, False)
            for _ in mid:
                pass

        @block.tensor
        def _(pe):
            def project(h, b, i, job, bank):
                kind, a = proj[i]
                wait_from(pe, job_free, job - NJ + 1)
                if kind == "q":
                    for q, (hw, hx) in enumerate(PAIRS):
                        for k in range(DC):
                            last = nc.tensor.matmul(psJ[bank][:, :], wq_v[:, hw, k, a, :], XT[:, hx, k, b * S:(b + 1) * S],
                                                    start=(q + k == 0), stop=(q == 2 and k == DC - 1))
                elif kind == "k":
                    for q, (hw, hx) in enumerate(PAIRS):
                        for k in range(KC):
                            last = nc.tensor.matmul(psJ[bank][:, :], wk_v[:, hw, k, :],
                                                    KVT[:, hx, k, b * keys + a * 512:b * keys + a * 512 + 512],
                                                    start=(q + k == 0), stop=(q == 2 and k == KC - 1))
                else:
                    for m in range(4):
                        at = b * keys + (4 * a + m) * P
                        for q, (hw, hx) in enumerate(PAIRS):
                            for k in range(KC):
                                last = nc.tensor.matmul(psJ[bank][:, m * P:(m + 1) * P], KVT[:, hx, k, at:at + P],
                                                        wv_v[:, hw, k, :], start=(q + k == 0),
                                                        stop=(q == 2 and k == KC - 1))
                last.then_inc(job_ready, 1)

            def output(h, b, t, job, bank):
                pe.wait_ge(o_lo, (h + 1) * groups)
                wait_from(pe, job_free, job - NJ + 1)
                for g in range(groups):
                    for q, (ho, hw) in enumerate(PAIRS):
                        last = nc.tensor.matmul(psJ[bank][:, :], OT[b][:, ho, g, t * P:(t + 1) * P], WO[:, hw, g, :],
                                                start=(g + q == 0), stop=(g == groups - 1 and q == 2))
                last.then_inc(job_ready, 1)

            def scores(n, b, g, t, j):
                wait_from(pe, masked, n - 1)
                w = width(t)
                for c in range(0, w, 512):
                    cw = min(512, w - c)
                    for q, (hq, hk) in enumerate(PAIRS):
                        last = nc.tensor.matmul(psS[j % 2][:, c:c + cw], QT[b][:, hq, g, t * P:(t + 1) * P],
                                                KT[b][:, hk, c:c + cw], start=(q == 0), stop=(q == 2))
                last.then_inc(scores_ready, 1)

            def transposes(m, t, j):
                pe.wait_ge(norm_done, m + 1)
                for i in range(NB):
                    u = m * NB + i
                    wait_from(pe, tr_lo, u - 1)
                    for blk in blocks(t, i):
                        last = nc.tensor.transpose(psT[(j * NB + i) % 2][:, (blk % 4) * P:(blk % 4 + 1) * P],
                                                   PN[j % 2][:, blk * P:(blk + 1) * P], identF[:])
                    last.then_inc(tr_ready, 1)

            def values(head, steps, b, g):
                pe.wait_ge(tr_lo, steps * NB)
                wait_from(pe, o_lo, head)
                for blk in range(NBLK):
                    c = blk * P if causal else 0
                    for q, (hv, hp) in enumerate(PAIRS):
                        last = nc.tensor.matmul(psO[:, c:], V[b][:, hv, blk, :], PT[g % 2][:, hp, blk, c:],
                                                start=(blk + q == 0), stop=(blk == NBLK - 1 and q == 2))
                last.then_inc(pv_ready, 1)

            def jobs(h, kv, b, j, first, last, late):
                for kind, i, job, bank in slot_jobs(h, j, first, last, late):
                    if kind == "proj":
                        if b == 1 and i == 0:
                            pe.wait_ge(wp_done, (kv + 2) * NWP)
                        project(h + 1, 1 - b, i, job, bank)
                    else:
                        pe.wait_ge(wo_done, (kv + b) * NWO)
                        output(h - 1, 1 - b, i, job, bank)

            def half(h, kv, b, first, last):
                for j in range(NS + (TAIL if last else 0)):
                    n = h * NS + j
                    if j == 0:
                        pe.wait_ge(job_free, projections_before(h))
                        if causal:
                            pe.wait_ge(rope_done, (h + 1) * (JP - 1))
                    if j < NS:
                        scores(n, b, j // TPB, j % TPB, j)
                    jobs(h, kv, b, j, first, last, 0)
                    m = j - TAIL
                    if m % TPB == TPB - 1 and (m >= 0 or not first):
                        values(h * groups + m // TPB, n - TAIL + 1, b if m >= 0 else 1 - b, (m % NS) // TPB)
                    jobs(h, kv, b, j, first, last, 1)
                    m = j - 2
                    if m < NS and (m >= 0 or not first):
                        mj = m % NS
                        transposes(n - 2, mj % TPB, mj)

            pe.wait_ge(wp_done, NWP)
            for i in range(JP):
                project(0, 0, i, i, i % NJ)
            mid = halves(half)
            lo, hi = next(mid)
            with pe.Fori(lo, hi) as kv:
                for b in range(B):
                    half(kv * 2 + b, kv, b, False, False)
            for _ in mid:
                pass
            pe.wait_ge(wo_done, kv_heads * NWO)
            for t in range(TPB):
                h = 2 * kv_heads - 1
                output(h, 1, t, jobs_before(h) + JO + t, t % NJ)

        def job_view(i):
            kind, a = proj[i]
            if kind == "q":
                return lambda b, hl: QT[b][:, hl, a, :]
            if kind == "k":
                return lambda b, hl: KT[b][:, hl, a * 512:(a + 1) * 512]
            return lambda b, hl: V[b][:, hl, 4 * a:4 * a + 4, :].rearrange("p m c -> p (m c)")

        def plain(i):
            return not causal or proj[i][0] == "v"

        def plain_count(h, i):
            return h + 1 if causal else JP * h + i + 1

        @block.scalar
        def _(act):
            def job_high(h, b, i, job, bank):
                act.wait_ge(job_ready, job + 1)
                nc.scalar.copy(job_view(i)(b, 0), psJ[bank][:, :]).then_inc(job_hi, 1)

            def rope_high(h, b, i):
                r = (JP - 1) * h + i
                par = (b * (JP - 1) + i) % 2
                dst = QT[b][:, :, i, :] if proj[i][0] == "q" else KT[b][:, :, :]
                act.wait_ge(rope_added, r + 1)
                nc.scalar.copy(dst[:, 0, :], rA[par][:]).then_inc(rope_hi, 1)

            short = [] if causal else [j for j, l in slots.items() if l[0][0][0] == "proj" and proj[l[0][0][1]][0] != "q"]

            def piece_high(what, i):
                (dst, src), hi_done = (wp_pieces[i], wp_hi) if what == "wp" else (wo_pieces[i], wo_hi)
                nc.scalar.copy(dst[:, 0], src).then_inc(hi_done, 1)

            def jobs(h, b, j, first, last, late):
                for kind, i, job, bank in slot_jobs(h, j, first, last, late):
                    if kind == "proj" and plain(i):
                        job_high(h + 1, 1 - b, i, job, bank)

            def half(h, kv, b, first, last):
                for j in range(NS + (TAIL if last else 0)):
                    n = h * NS + j
                    if j in short:
                        jobs(h, b, j, first, last, 0)
                    if j < NS:
                        w = width(j % TPB)
                        act.wait_ge(masked, n + 1)
                        nc.scalar.activation(SC[j % 2][:, 0:w], SC[j % 2][:, 0:w], ACT.Exp,
                                             bias=mn[:, j % 4:j % 4 + 1], scale=-1.0,
                                             accum_out=sm[:, j % 4:j % 4 + 1]).then_inc(exp_done, 1)
                    if j not in short:
                        jobs(h, b, j, first, last, 0)
                    m = j - TAIL
                    if m % TPB == TPB - 1 and (m >= 0 or not first):
                        mb, mg = (b if m >= 0 else 1 - b), (m % NS) // TPB
                        act.wait_ge(pv_ready, h * groups + m // TPB + 1)
                        nc.scalar.activation(OT[mb][:, 0, mg, :], psO[:, :], ACT.Copy, scale=1.0 / PSCALE).then_inc(o_hi, 1)
                    jobs(h, b, j, first, last, 1)
                    m = j - 2
                    if m < NS and (m >= 0 or not first):
                        mj = m % NS
                        mt, mg = mj % TPB, mj // TPB
                        for i in range(NB):
                            u = (n - 2) * NB + i
                            bl = blocks(mt, i)
                            act.wait_ge(tr_ready, u + 1)
                            nc.scalar.copy(PT[mg % 2][:, 0, bl[0]:bl[-1] + 1, mt * P:(mt + 1) * P],
                                           psT[(mj * NB + i) % 2][:, 0:len(bl) * P].rearrange("p (k t) -> p k t", t=P)
                                           ).then_inc(tr_hi, 1)
                    piece = step_pieces(kv, b, j, last or isinstance(kv, int) and kv == kv_heads - 1)
                    if piece and piece[0] == "wp":
                        if piece[1] == 0:
                            act.wait_ge(wp_in, 48 * (kv + 2))
                            act.wait_ge(job_ready, jobs_before(h + 1) - (0 if first else JO))
                        piece_high(*piece[:2])
                    elif piece:
                        if piece[1] == 0:
                            act.wait_ge(wo_in, 16 * (kv + 1))
                            act.wait_ge(job_ready, jobs_before(h))
                        piece_high(*piece[:2])
                    for kind, i, job, _ in slot_jobs(h, j, first, last):
                        if causal and kind == "proj" and proj[i][0] != "v":
                            rope_high(h + 1, 1 - b, i)

            act.wait_ge(wp_in, 48)
            for i in range(NWP):
                piece_high("wp", i)
            for i in range(JP):
                if plain(i):
                    job_high(0, 0, i, i, i % NJ)
                else:
                    rope_high(0, 0, i)
            mid = halves(half)
            lo, hi = next(mid)
            with act.Fori(lo, hi) as kv:
                for b in range(B):
                    half(kv * 2 + b, kv, b, False, False)
            for _ in mid:
                pass

        @block.vector
        def _(dve):
            def job_low(h, b, i, job, bank):
                if plain(i):
                    dve.wait_ge(job_hi, plain_count(h, i))
                    dve.wait_ge(job_ready, job + 1)
                    nc.vector.tensor_tensor(job_view(i)(b, 1), psJ[bank][:, :], job_view(i)(b, 0),
                                            ALU.subtract).then_inc(job_free, 1)
                    return
                r = (JP - 1) * h + i
                par = (b * (JP - 1) + i) % 2
                dve.wait_ge(job_ready, job + 1)
                wait_from(dve, rope_done, r - 1)
                ropeC, ropeS = rope
                nc.vector.tensor_tensor(rA[par][:], psJ[bank][:, :], ropeC[:], ALU.mult)
                nc.vector.tensor_tensor(rB[par][64:128, :], psJ[bank][0:64, :], ropeS[0:64, :], ALU.mult)
                nc.vector.tensor_tensor(rB[par][0:64, :], psJ[bank][64:128, :], ropeS[64:128, :],
                                        ALU.mult).then_inc(job_free, 1)

            def output_add(h, b, t, job, bank):
                dve.wait_ge(job_ready, job + 1)
                nc.vector.tensor_tensor(X[:, b * TPB + t, :], psJ[bank][:, :], X[:, b * TPB + t, :], ALU.add).then_inc(job_free, 1)

            def jobs(h, b, j, first, last, late):
                for kind, i, job, bank in slot_jobs(h, j, first, last, late):
                    if kind == "proj":
                        job_low(h + 1, 1 - b, i, job, bank)
                    else:
                        output_add(h - 1, 1 - b, i, job, bank)

            def half(h, kv, b, first, last):
                for j in range(NS + (TAIL if last else 0)):
                    n = h * NS + j
                    if j < NS:
                        w = width(j % TPB)
                        dve.wait_ge(scores_ready, n + 1)
                        wait_from(dve, norm_done, n - 1)
                        stand_apart(dve, dve_passed)
                        nc.vector.tensor_tensor_reduce(out=SC[j % 2][:, 0:w], in0=psS[j % 2][:, 0:w],
                                                       in1=mask_of(b, j % TPB), scale=-SCORE_SCALE, scalar=3e38,
                                                       op0=ALU.add, op1=ALU.min,
                                                       accum_out=mn[:, j % 4:j % 4 + 1]).then_inc(masked, 1)
                    jobs(h, b, j, first, last, 0)
                    if j < NS:
                        dve.wait_ge(exp_done, n + 1)
                        nc.vector.reciprocal(rc[:, j % 4:j % 4 + 1], sm[:, j % 4:j % 4 + 1]).then_inc(recip_done, 1)
                    m = j - TAIL
                    if m % TPB == TPB - 1 and (m >= 0 or not first):
                        mb, mg = (b if m >= 0 else 1 - b), (m % NS) // TPB
                        dve.wait_ge(o_hi, h * groups + m // TPB + 1)
                        nc.vector.scalar_tensor_tensor(out=OT[mb][:, 1, mg, :], in0=psO[:, :], scalar=1.0 / PSCALE,
                                                       in1=OT[mb][:, 0, mg, :], op0=ALU.mult,
                                                       op1=ALU.subtract).then_inc(o_lo, 1)
                    jobs(h, b, j, first, last, 1)
                    m = j - 2
                    if m < NS and (m >= 0 or not first):
                        mj = m % NS
                        mt, mg = mj % TPB, mj // TPB
                        for i in range(NB):
                            u = (n - 2) * NB + i
                            bl = blocks(mt, i)
                            dve.wait_ge(tr_hi, u + 1)
                            dst = (slice(bl[0], bl[-1] + 1), slice(mt * P, (mt + 1) * P))
                            nc.vector.tensor_tensor(PT[mg % 2][:, 1, dst[0], dst[1]],
                                                    psT[(mj * NB + i) % 2][:, 0:len(bl) * P].rearrange("p (k t) -> p k t", t=P),
                                                    PT[mg % 2][:, 0, dst[0], dst[1]], ALU.subtract).then_inc(tr_lo, 1)

            for i, (dst, src) in enumerate(wp_pieces):
                dve.wait_ge(wp_hi, i + 1)
                nc.vector.tensor_tensor(dst[:, 1], src, dst[:, 0], ALU.subtract).then_inc(wp_done, 1)
            for i in range(JP):
                job_low(0, 0, i, i, i % NJ)
            mid = halves(half)
            lo, hi = next(mid)
            with dve.Fori(lo, hi) as kv:
                for b in range(B):
                    half(kv * 2 + b, kv, b, False, False)
            for _ in mid:
                pass
            for t in range(TPB):
                h = 2 * kv_heads - 1
                output_add(h, 1, t, jobs_before(h) + JO + t, t % NJ)


def w13_split_pieces(W13, W13raw):
    return [(W13[:, :, :, i // 2, (i % 2) * 512:(i % 2) * 512 + 512], W13raw[:, :, i // 2, (i % 2) * 512:(i % 2) * 512 + 512])
            for i in range(8)]


def phase_route(nc, XT, gate_w, W13, W13raw, wts, p12, slots, over):
    with ExitStack() as st:
        named = phase_semaphores(nc, st)
        sem = lambda n: named(f"route_{n}")

        def sb(n, shape, dt):
            return st.enter_context(nc.sbuf_tensor(f"route_{n}", shape, dt))

        GW = sb("GW", [P, DC, E], F32)
        GWP = sb("GWP", [P, 2, DC, E], F16)
        lg = sb("lg", [P, NT, E], F32)
        top = sb("top", [P, NT, 8], F32)
        idx = sb("idx", [P, NT, 8], U32)
        idf = sb("idf", [P, NT, 8], F32)
        dlt = sb("dlt", [P, NT], F32)
        ex = sb("ex", [P, NT], F32)
        ex1 = sb("ex1", [P, NT], F32)
        expert = sb("expert", [P, E], F32)
        base = sb("base", [P, E], F32)
        onehot = sb("onehot", [P, 2, NT, E], F32)
        picks = sb("picks", [P, NT, E], F16)
        before = sb("before", [P, NT + 1, E], F16)
        part = sb("part", [P, 2, NT, E], F32)
        rank = sb("rank", [P, NT, E], F32)
        slotf = sb("slotf", [P, 2, NT], F32)
        counts = sb("counts", [P, 1], F32)
        zero = sb("zero", [P, P], F32)
        earlier = sb("earlier", [P, P], F32)
        earlier16 = sb("earlier16", [P, P], F16)
        ones16 = sb("ones16", [P, P], F16)
        psL = st.enter_context(nc.psum_tensor("route_psL", [P, 512], F32))
        psR = st.enter_context(nc.psum_tensor("route_psR", [P, 512], F32))
        psC = st.enter_context(nc.psum_tensor("route_psC", [P, 512], F32))

        gw_in, gw_hi, gw_done, iota_done, zero_done, tri_done, mats_done = (
            sem("gw_in"), sem("gw_hi"), sem("gw_done"), sem("iota_done"), sem("zero_done"), sem("tri_done"), sem("mats_done"))
        logits_ready, dlt_done, ex_done, chain = sem("logits_ready"), sem("dlt_done"), sem("ex_done"), sem("chain")
        picks_done, rank_ready, w13_hi, w13_done = sem("picks_done"), sem("rank_ready"), sem("w13_hi"), sem("w13_done")
        pieces = w13_split_pieces(W13, W13raw)
        block = st.enter_context(nc.Block())

        @block.sync
        def _(sp):
            sp.dma_start(GW[:], gate_w.rearrange("(k p) e -> p k e", p=P)).then_inc(gw_in, 16)

        @block.gpsimd
        def _(pool):
            nc.gpsimd.iota(expert[:], pattern=[[1, E]], base=0, channel_multiplier=0,
                           allow_small_or_imprecise_dtypes=True).then_inc(iota_done, 1)
            nc.gpsimd.iota(base[:], pattern=[[CAP, E]], base=0, channel_multiplier=0,
                           allow_small_or_imprecise_dtypes=True).then_inc(iota_done, 1)
            nc.gpsimd.memset(zero[:], 0.0).then_inc(zero_done, 1)
            nc.gpsimd.memset(ones16[:], 1.0).then_inc(mats_done, 1)
            pool.wait_ge(zero_done, 1)
            nc.gpsimd.affine_select(out=earlier[:], in_=zero[:], compare_op=ALU.is_ge, fill=1.0, base=0,
                                    pattern=[[-1, P]], channel_multiplier=1).then_inc(tri_done, 1)
            pool.wait_ge(tri_done, 1)
            nc.gpsimd.tensor_copy(earlier16[:], earlier[:]).then_inc(mats_done, 1)

        @block.tensor
        def _(pe):
            pe.wait_ge(gw_done, 1)
            for i in range(NT):
                for q, (hx, hw) in enumerate(PAIRS):
                    for k in range(DC):
                        last = nc.tensor.matmul(psL[:, i * E:(i + 1) * E], XT[:, hx, k, i * P:(i + 1) * P], GWP[:, hw, k, :],
                                                start=(q + k == 0), stop=(q == 2 and k == DC - 1))
            last.then_inc(logits_ready, 1)
            pe.wait_ge(picks_done, 1)
            pe.wait_ge(mats_done, 2)
            nc.tensor.matmul(psR[:, 0:NT * E], earlier16[:], picks[:].rearrange("p t e -> p (t e)"), start=True, stop=False)
            nc.tensor.matmul(psR[:, 0:NT * E], ones16[:], before[:, 0:NT, :].rearrange("p t e -> p (t e)"),
                             start=False, stop=True)
            nc.tensor.matmul(psC[:, 0:E], ones16[:], before[:, NT, :], start=True, stop=True).then_inc(rank_ready, 1)

        @block.scalar
        def _(act):
            for dst, src in pieces:
                nc.scalar.copy(dst[:, 0], src).then_inc(w13_hi, 1)
            act.wait_ge(dlt_done, 1)
            nc.scalar.activation(ex[:], dlt[:], ACT.Exp).then_inc(ex_done, 1)

        @block.vector
        def _(dve):
            steps = [0]

            def chained(ins):
                steps[0] += 1
                ins.then_inc(chain, 1)
                dve.wait_ge(chain, steps[0])

            dve.wait_ge(gw_in, 16)
            nc.vector.tensor_copy(GWP[:, 0, :, :], GW[:]).then_inc(gw_hi, 1)
            dve.wait_ge(gw_hi, 1)
            nc.vector.tensor_tensor(GWP[:, 1, :, :], GW[:], GWP[:, 0, :, :], ALU.subtract).then_inc(gw_done, 1)
            dve.wait_ge(logits_ready, 1)
            chained(nc.vector.tensor_copy(lg[:].rearrange("p t e -> p (t e)"), psL[:, 0:NT * E]))
            for i in range(NT):
                last = nc.vector.max(top[:, i, :], lg[:, i, :])
            chained(last)
            for i in range(NT):
                last = nc.vector.max_index(idx[:, i, :], top[:, i, :], lg[:, i, :])
            chained(last)
            nc.vector.tensor_tensor(dlt[:], top[:, :, 1], top[:, :, 0], ALU.subtract).then_inc(dlt_done, 1)
            chained(nc.vector.tensor_copy(idf[:], idx[:]))
            dve.wait_ge(iota_done, 2)
            wide = [P, NT, E]
            for k in range(2):
                last = nc.vector.tensor_tensor(onehot[:, k], expert[:].unsqueeze(1).broadcast_to(wide),
                                               idf[:, :, k:k + 1].broadcast_to(wide), ALU.is_equal)
            chained(last)
            chained(nc.vector.tensor_tensor(picks[:], onehot[:, 0], onehot[:, 1], ALU.add))
            chained(nc.vector.memset(before[:, 0, :], 0.0))
            for i in range(NT):
                chained(nc.vector.tensor_tensor(before[:, i + 1, :], before[:, i, :], picks[:, i, :], ALU.add))
            nc.vector.tensor_copy(counts[:], expert[:, 0:1]).then_inc(picks_done, 1)
            dve.wait_ge(ex_done, 1)
            chained(nc.vector.tensor_scalar(ex1[:], ex[:], 1.0, None, ALU.add))
            chained(nc.vector.reciprocal(p12[:, 0, :], ex1[:]))
            chained(nc.vector.tensor_tensor(p12[:, 1, :], ex[:], p12[:, 0, :], ALU.mult))
            for k in range(2):
                last = nc.vector.tensor_tensor(part[:, k], onehot[:, k], p12[:, k, :].unsqueeze(2).broadcast_to(wide), ALU.mult)
            chained(last)
            chained(nc.vector.tensor_tensor(wts[:], part[:, 0], part[:, 1], ALU.add))
            dve.wait_ge(rank_ready, 1)
            chained(nc.vector.tensor_tensor(rank[:], psR[:, 0:NT * E].rearrange("p (t e) -> p t e", e=E),
                                            base[:].unsqueeze(1).broadcast_to(wide), ALU.add))
            for k in range(2):
                last = nc.vector.tensor_tensor(part[:, k], onehot[:, k], rank[:], ALU.mult)
            chained(last)
            chained(nc.vector.tensor_reduce(slotf[:], part[:], AX_X, ALU.add))
            chained(nc.vector.tensor_copy(slots[:], slotf[:]))
            chained(nc.vector.tensor_reduce(counts[:], psC[:, 0:E], AX_X, ALU.max))
            chained(nc.vector.tensor_scalar(over[:], counts[:], float(CAP), None, ALU.is_gt))
            for i, (dst, src) in enumerate(pieces):
                dve.wait_ge(w13_hi, i + 1)
                nc.vector.tensor_tensor(dst[:, 1], src, dst[:, 0], ALU.subtract).then_inc(w13_done, 1)


def phase_moe_routed(nc, X, XT, XW, scratch, XG, YG, w1, w3, w2, W13raw, W13, W2raw, W2, p12, slots):
    with ExitStack() as st:
        named = phase_semaphores(nc, st)
        sem = lambda n: named(f"rmoe_{n}")

        def sb(n, shape, dt):
            return st.enter_context(nc.sbuf_tensor(f"rmoe_{n}", shape, dt))

        def pb(n):
            return st.enter_context(nc.psum_tensor(f"rmoe_{n}", [P, 512], F32))

        XR = scratch[:, 0:CTL, :]
        YR = scratch[:, CTL:2 * CTL, :]
        XGT = sb("XGT", [P, 2, DC, CAP], F16)
        SG = [sb(f"SG{i}", [P, CAP], F32) for i in range(2)]
        HF = [sb(f"HF{i}", [P, CAP], F32) for i in range(2)]
        HT = sb("HT", [P, 2, FC, CAP], F16)
        ident = sb("ident", [P, P], F32)
        psG = [pb(f"psG{i}") for i in range(2)]
        psU = [pb(f"psU{i}") for i in range(2)]
        psY = [pb(f"psY{i}") for i in range(2)]
        psT = [pb(f"psT{i}") for i in range(2)]
        Y1, Y2 = XW, XT[:].rearrange("p l k t -> p (l k t)").bitcast(F32).rearrange("p (t d) -> p t d", d=D)

        ident_zero, ident_done = sem("ident_zero"), sem("ident_done")
        scattered, x_in = sem("scattered"), sem("x_in")
        w13_in, w2_in, w13_hi, w13_done, w2_hi, w2_done = (
            sem("w13_in"), sem("w2_in"), sem("w13_hi"), sem("w13_done"), sem("w2_hi"), sem("w2_done"))
        tr_ready, tr_hi, tr_lo = sem("tr_ready"), sem("tr_hi"), sem("tr_lo")
        up_ready, silu_done, h_done, h_hi, h_lo = (
            sem("up_ready"), sem("silu_done"), sem("h_done"), sem("h_hi"), sem("h_lo"))
        down_ready, y_copied = sem("down_ready"), sem("y_copied")
        y_stored = [sem(f"y_stored{r}") for r in range(CTL)]
        gathered = [sem(f"gathered{t}") for t in range(NT)]
        combined = sem("combined")
        w13_pieces = w13_split_pieces(W13, W13raw)
        w2_pieces = [(W2[:, :, i, :], W2raw[:, i, :]) for i in range(FC)]
        xg_v = XG.rearrange("(e r p) d -> e p r d", r=CTL, p=P)
        yg_v = YG.rearrange("(e r p) d -> e r p d", r=CTL, p=P)
        block = st.enter_context(nc.Block())

        def over_experts(eng, emit):
            emit(0, True, False)
            with eng.Fori(1, E - 1) as e:
                emit(e, False, False)
            emit(E - 1, False, True)

        @block.sync
        def _(sp):
            def load_rows(e):
                wait_from(sp, tr_ready, DC * e)
                sp.dma_start(XR, xg_v[bass.ds(e, 1)].rearrange("o p r d -> p (o r) d")).then_inc(x_in, 16)

            sp.wait_ge(scattered, 16 * 2 * NT)
            load_rows(0)

            def step(e, first, last):
                if not last:
                    load_rows(e + 1)
                    wait_from(sp, w13_done, 8 * e)
                    for i, w in enumerate((w1, w3)):
                        sp.dma_start(W13raw[:, i, :, :], w[bass.ds(e + 1, 1)].rearrange("o (k p) f -> p (o k) f", p=P)).then_inc(w13_in, 16)
                    sp.wait_ge(w2_done, FC * (e + 1))
                    sp.dma_start(W2raw[:], w2[bass.ds(e + 1, 1)].rearrange("o (k p) d -> p (o k) d", p=P)).then_inc(w2_in, 16)
                for r in range(CTL):
                    sp.wait_ge(y_copied, CTL * e + r + 1)
                    sp.dma_start(yg_v[bass.ds(e, 1), r].rearrange("o p d -> p (o d)"), YR[:, r, :]).then_inc(y_stored[r], 16)

            over_experts(sp, step)
            for r in range(CTL):
                sp.wait_ge(y_stored[r], 16 * E)

        @block.gpsimd
        def _(pool):
            for t in range(NT):
                for k in range(2):
                    pool.indirect_dma_start(out=XG, out_offset=bass.IndirectOffsetOnAxis(ap=slots[:, k, t:t + 1], axis=0),
                                            in_=XW[:, t, :], in_offset=None).then_inc(scattered, 16)
            nc.gpsimd.memset(ident[:], 0.0).then_inc(ident_zero, 1)
            pool.wait_ge(ident_zero, 1)
            nc.gpsimd.affine_select(out=ident[:], in_=ident[:], compare_op=ALU.not_equal, fill=1.0, base=0,
                                    pattern=[[-1, P]], channel_multiplier=1).then_inc(ident_done, 1)
            for r in range(CTL):
                pool.wait_ge(y_stored[r], 16 * E)
            pool.wait_ge(scattered, 16 * 2 * NT)
            for t in range(NT):
                for k, dst in enumerate((Y1, Y2)):
                    pool.indirect_dma_start(out=dst[:, t, :], out_offset=None, in_=YG,
                                            in_offset=bass.IndirectOffsetOnAxis(ap=slots[:, k, t:t + 1], axis=0)
                                            ).then_inc(gathered[t], 16)

        @block.tensor
        def _(pe):
            def transposes(e):
                pe.wait_ge(x_in, 16 * (e + 1))
                for k in range(DC):
                    wait_from(pe, tr_lo, DC * e + k - 1)
                    for r in range(CTL):
                        last = nc.tensor.transpose(psT[k % 2][:, r * P:(r + 1) * P], XR[:, r, k * P:(k + 1) * P], ident[:])
                    last.then_inc(tr_ready, 1)

            def step(e, first, last_e):
                if not first:
                    pe.wait_ge(w13_done, 8 * e)
                pe.wait_ge(tr_lo, DC * (e + 1))
                for f in range(FC):
                    n = e * FC + f
                    wait_from(pe, h_done, n - 1)
                    for w, bank in ((0, psG), (1, psU)):
                        for i, (hw, hx) in enumerate(PAIRS):
                            for k in range(DC):
                                last = nc.tensor.matmul(bank[f % 2][:, 0:CAP], W13[:, hw, w, k, f * P:(f + 1) * P],
                                                        XGT[:, hx, k, :], start=(i + k == 0),
                                                        stop=(i == 2 and k == DC - 1))
                    last.then_inc(up_ready, 1)
                if not last_e:
                    transposes(e + 1)
                pe.wait_ge(w2_done, (e + 1) * FC)
                pe.wait_ge(h_lo, (e + 1) * FC)
                for r in range(CTL):
                    y = r % 2
                    wait_from(pe, y_copied, e * CTL + r - 1 if r else e * CTL)
                    for i, (hh, hw) in enumerate(PAIRS):
                        for k in range(FC):
                            last = nc.tensor.matmul(psY[y][:, :], HT[:, hh, k, r * P:(r + 1) * P], W2[:, hw, k, :],
                                                    start=(i + k == 0), stop=(i == 2 and k == FC - 1))
                    last.then_inc(down_ready, 1)

            pe.wait_ge(ident_done, 1)
            transposes(0)
            over_experts(pe, step)

        @block.scalar
        def _(act):
            def rows_high(e):
                for k in range(DC):
                    act.wait_ge(tr_ready, DC * e + k + 1)
                    if k == 0:
                        wait_from(act, up_ready, FC * e)
                    nc.scalar.copy(XGT[:, 0, k, :], psT[k % 2][:, 0:CAP]).then_inc(tr_hi, 1)

            def step(e, first, last):
                wait_from(act, w2_in, 16 * e)
                wait_from(act, down_ready, CTL * e)
                for f in range(FC):
                    n = e * FC + f
                    act.wait_ge(up_ready, n + 1)
                    nc.scalar.activation(SG[f % 2][:], psG[f % 2][:, 0:CAP], ACT.Silu).then_inc(silu_done, 1)
                    dst, src = w2_pieces[f]
                    nc.scalar.copy(dst[:, 0], src).then_inc(w2_hi, 1)
                    act.wait_ge(h_done, n + 1)
                    nc.scalar.copy(HT[:, 0, f, :], HF[f % 2][:]).then_inc(h_hi, 1)
                if not last:
                    rows_high(e + 1)
                    act.wait_ge(w13_in, 32 * (e + 1))
                    for dst, src in w13_pieces:
                        nc.scalar.copy(dst[:, 0], src).then_inc(w13_hi, 1)

            rows_high(0)
            over_experts(act, step)

        @block.vector
        def _(dve):
            def rows_low(e):
                for k in range(DC):
                    dve.wait_ge(tr_hi, DC * e + k + 1)
                    nc.vector.tensor_tensor(XGT[:, 1, k, :], psT[k % 2][:, 0:CAP], XGT[:, 0, k, :], ALU.subtract).then_inc(tr_lo, 1)

            def step(e, first, last):
                for f in range(FC):
                    n = e * FC + f
                    dve.wait_ge(silu_done, n + 1)
                    wait_from(dve, h_lo, n - 1)
                    nc.vector.tensor_tensor(HF[f % 2][:], psU[f % 2][:, 0:CAP], SG[f % 2][:], ALU.mult).then_inc(h_done, 1)
                    dst, src = w2_pieces[f]
                    dve.wait_ge(w2_hi, n + 1)
                    nc.vector.tensor_tensor(dst[:, 1], src, dst[:, 0], ALU.subtract).then_inc(w2_done, 1)
                    dve.wait_ge(h_hi, n + 1)
                    nc.vector.tensor_tensor(HT[:, 1, f, :], HF[f % 2][:], HT[:, 0, f, :], ALU.subtract).then_inc(h_lo, 1)
                if not last:
                    rows_low(e + 1)
                for r in range(CTL):
                    if not last:
                        for i in range(3 * r, min(3 * r + 3, 8)):
                            dst, src = w13_pieces[i]
                            dve.wait_ge(w13_hi, 8 * e + i + 1)
                            nc.vector.tensor_tensor(dst[:, 1], src, dst[:, 0], ALU.subtract).then_inc(w13_done, 1)
                    dve.wait_ge(down_ready, CTL * e + r + 1)
                    wait_from(dve, y_stored[r], 16 * e)
                    nc.vector.tensor_copy(YR[:, r, :], psY[r % 2][:, :]).then_inc(y_copied, 1)

            rows_low(0)
            over_experts(dve, step)
            for t in range(NT):
                dve.wait_ge(gathered[t], 32)
                nc.vector.scalar_tensor_tensor(out=X[:, t, :], in0=Y1[:, t, :], scalar=p12[:, 0, t:t + 1],
                                               in1=X[:, t, :], op0=ALU.mult, op1=ALU.add).then_inc(combined, 1)
                dve.wait_ge(combined, 2 * t + 1)
                nc.vector.scalar_tensor_tensor(out=X[:, t, :], in0=Y2[:, t, :], scalar=p12[:, 1, t:t + 1],
                                               in1=X[:, t, :], op0=ALU.mult, op1=ALU.add).then_inc(combined, 1)


def phase_moe_dense(nc, X, XT, wts, w1, w3, w2, W13raw, W13, W2raw, W2, scratch):
    with ExitStack() as st:
        sem = phase_semaphores(nc, st)

        def sb(n, shape, dt):
            return st.enter_context(nc.sbuf_tensor(f"moe_{n}", shape, dt))

        def pb(n, shape):
            return st.enter_context(nc.psum_tensor(f"moe_{n}", shape, F32))

        SG = [sb(f"SG{i}", [P, S], F32) for i in range(2)]
        HF = [sb(f"HF{i}", [P, S], F32) for i in range(4)]
        HT = scratch[:].rearrange("p l t d -> p (l t d)").bitcast(F16).rearrange("p (l f t) -> p l f t", l=2, f=FC)
        psG = [pb(f"psG{i}", [P, 512]) for i in range(2)]
        psU = [pb(f"psU{i}", [P, 512]) for i in range(2)]
        psY = [pb(f"psY{i}", [P, 512]) for i in range(2)]

        s = lambda n: sem(f"moe_{n}")
        pool_passed = s("pool_passed")
        w13_in, w2_in = s("w13_in"), s("w2_in")
        w13_hi, w13_done, w2_hi, w2_done = s("w13_hi"), s("w13_done"), s("w2_hi"), s("w2_done")
        up_ready, silu_done, h_done, h_hi, h_split = s("up_ready"), s("silu_done"), s("h_done"), s("h_hi"), s("h_split")
        down_ready, added = s("down_ready"), s("added")
        UP = B * FC
        block = st.enter_context(nc.Block())

        def over_experts(eng, emit):
            emit(0, True, False)
            with eng.Fori(1, E - 1) as e:
                emit(e, False, False)
            emit(E - 1, False, True)

        @block.sync
        def _(sp):
            def load(e):
                wait_from(sp, w13_done, e * 8)
                for i, w in enumerate((w1, w3)):
                    sp.dma_start(W13raw[:, i, :, :], w[bass.ds(e, 1)].rearrange("o (k p) f -> p (o k) f", p=P)).then_inc(w13_in, 16)
                wait_from(sp, w2_done, e * 8)
                sp.dma_start(W2raw[:], w2[bass.ds(e, 1)].rearrange("o (k p) d -> p (o k) d", p=P)).then_inc(w2_in, 16)

            load(0)
            with sp.Fori(1, E) as e:
                load(e)

        @block.gpsimd
        def _(pool):
            def split_w13(e, i):
                at = (i // 2, slice((i % 2) * 512, (i % 2) * 512 + 512))
                stand_apart(pool, pool_passed)
                nc.gpsimd.tensor_copy(W13[:, 0, :, at[0], at[1]], W13raw[:, :, at[0], at[1]]).then_inc(w13_hi, 1)
                pool.wait_ge(w13_hi, e * 8 + i + 1)
                nc.gpsimd.tensor_tensor(W13[:, 1, :, at[0], at[1]], W13raw[:, :, at[0], at[1]],
                                        W13[:, 0, :, at[0], at[1]], ALU.subtract).then_inc(w13_done, 1)

            def split_w2(e, i):
                stand_apart(pool, pool_passed)
                nc.gpsimd.tensor_copy(W2[:, 0, i, :], W2raw[:, i, :]).then_inc(w2_hi, 1)
                pool.wait_ge(w2_hi, e * 8 + i + 1)
                nc.gpsimd.tensor_tensor(W2[:, 1, i, :], W2raw[:, i, :], W2[:, 0, i, :], ALU.subtract).then_inc(w2_done, 1)

            def expert_steps(e, first, last):
                for q in range(UP):
                    b, f = q // FC, q % FC
                    if q == 0:
                        pool.wait_ge(w2_in, 16 * (e + 1))
                        wait_from(pool, down_ready, e * NT)
                    if q < 8:
                        split_w2(e, q)
                    n = e * UP + q
                    pool.wait_ge(h_done, n + 1)
                    stand_apart(pool, pool_passed)
                    nc.gpsimd.tensor_copy(HT[:, 0, f, b * S:(b + 1) * S], HF[q % 4][:]).then_inc(h_hi, 1)
                    pool.wait_ge(h_hi, n + 1)
                    nc.gpsimd.tensor_tensor(HT[:, 1, f, b * S:(b + 1) * S], HF[q % 4][:], HT[:, 0, f, b * S:(b + 1) * S],
                                            ALU.subtract).then_inc(h_split, 1)
                if not last:
                    pool.wait_ge(w13_in, 32 * (e + 2))
                    pool.wait_ge(up_ready, (e + 1) * UP)
                    for i in range(8):
                        split_w13(e + 1, i)

            pool.wait_ge(w13_in, 32)
            for i in range(8):
                split_w13(0, i)
            over_experts(pool, expert_steps)

        @block.tensor
        def _(pe):
            def expert_steps(e, first, last_e):
                pe.wait_ge(w13_done, (e + 1) * 8)
                for q in range(UP):
                    n = e * UP + q
                    b, f = q // FC, q % FC
                    wait_from(pe, h_done, n - 1)
                    for w, bank in ((0, psG), (1, psU)):
                        for i, (hw, hx) in enumerate(PAIRS):
                            for k in range(DC):
                                last = nc.tensor.matmul(bank[q % 2][:, :], W13[:, hw, w, k, f * P:(f + 1) * P],
                                                        XT[:, hx, k, b * S:(b + 1) * S], start=(i + k == 0),
                                                        stop=(i == 2 and k == DC - 1))
                    last.then_inc(up_ready, 1)
                pe.wait_ge(w2_done, (e + 1) * 8)
                for t in range(NT):
                    if t % TPB == 0:
                        pe.wait_ge(h_split, e * UP + (t // TPB + 1) * FC)
                    wait_from(pe, added, e * NT + t - 1)
                    for i, (hh, hw) in enumerate(PAIRS):
                        for k in range(FC):
                            last = nc.tensor.matmul(psY[t % 2][:, :], HT[:, hh, k, t * P:(t + 1) * P], W2[:, hw, k, :],
                                                    start=(i + k == 0), stop=(i == 2 and k == FC - 1))
                    last.then_inc(down_ready, 1)

            over_experts(pe, expert_steps)

        @block.scalar
        def _(act):
            def expert_steps(e, first, last):
                for q in range(UP):
                    n = e * UP + q
                    act.wait_ge(up_ready, n + 1)
                    wait_from(act, h_done, n - 1)
                    nc.scalar.activation(SG[q % 2][:], psG[q % 2][:, :], ACT.Silu).then_inc(silu_done, 1)

            over_experts(act, expert_steps)

        @block.vector
        def _(dve):
            def expert_steps(e, first, last):
                for q in range(UP):
                    n = e * UP + q
                    dve.wait_ge(silu_done, n + 1)
                    wait_from(dve, h_split, n - 3)
                    nc.vector.tensor_tensor(HF[q % 4][:], psU[q % 2][:, :], SG[q % 2][:], ALU.mult).then_inc(h_done, 1)
                for t in range(NT):
                    dve.wait_ge(down_ready, e * NT + t + 1)
                    wait_from(dve, added, (e - 1) * NT + t + 1)
                    nc.vector.scalar_tensor_tensor(out=X[:, t, :], in0=psY[t % 2][:, :], scalar=wts[:, t, bass.ds(e, 1)],
                                                   in1=X[:, t, :], op0=ALU.mult, op1=ALU.add).then_inc(added, 1)

            over_experts(dve, expert_steps)


def decoder_layer(nc, x, ctxt, mask, W_in, W_out, log_A, W_dt, b_dt, xWq, xWk, xWv, xWo, norm1_w, norm2_w, wq, wk, wv, wo,
                  gate_w, w1, w3, w2, rope_in, XG, YG, out):
    with ExitStack() as st:
        def sb(name, shape, dt):
            return st.enter_context(nc.sbuf_tensor(name, shape, dt))

        X = sb("X", [P, NT, D], F32)
        XT = sb("XT", [P, 2, DC, T], F16)
        identF = sb("identF", [P, P], F32)
        causal = sb("causal", [P, S], F32)
        flag = sb("flag", [P, B], F32)
        ropeC = sb("ropeC", [P, S], F32)
        ropeS = sb("ropeS", [P, S], F32)

        with ExitStack() as cross:
            CT = cross.enter_context(nc.sbuf_tensor("CT", [P, 2, DCTX // P, B * S2], F16))
            maskb = cross.enter_context(nc.sbuf_tensor("maskb", [P, B, S2], F32))
            phase_ssm(nc, X, XT, CT, XG, x, ctxt, mask, W_in, W_out, log_A, W_dt, b_dt,
                      (identF, causal, maskb, flag, ropeC, ropeS), rope_in)
            phase_norm(nc, "n1", X, identF, XT=XT)
            attention(nc, "xa", X, XT, CT, identF, xWq, xWk, xWv, xWo, 8, 2, S2,
                      lambda b, t: maskb[:, b, :], flag, None)
        rows = sb("rows", [P, 2, NT, D], F32)
        XW = rows[:, 0]
        X2 = rows[:, 1]
        phase_norm(nc, "n2", X, identF, XT=XT, norm_w=norm1_w, keep=X2)
        attention(nc, "sa", X, XT, XT, identF, wq, wk, wv, wo, 4, 4, S,
                  lambda b, t: causal[:, S - (t + 1) * P:S], None, (ropeC, ropeS))
        W13raw = sb("W13raw", [P, 2, DC, F], F32)
        W13 = sb("W13", [P, 2, 2, DC, F], F16)
        W2raw = sb("W2raw", [P, FC, D], F32)
        W2 = sb("W2", [P, 2, FC, D], F16)
        wts = sb("wts", [P, NT, E], F32)
        p12 = sb("p12", [P, 2, NT], F32)
        slots = sb("slots", [P, 2, NT], U32)
        over = sb("over", [P, 1], I32)
        phase_norm(nc, "n3", X, identF, XT=XT, norm_w=norm2_w, layer=False, add=X2, rows=XW,
                   fetch=[(W13raw[:, 0], w1[0].rearrange("(k p) f -> p k f", p=P)),
                          (W13raw[:, 1], w3[0].rearrange("(k p) f -> p k f", p=P)),
                          (W2raw[:], w2[0].rearrange("(k p) d -> p k d", p=P))])
        phase_route(nc, XT, gate_w, W13, W13raw, wts, p12, slots, over)
        overfull = nc.values_load(over[0:1, 0:1], min_val=0, max_val=1)
        with nc.If(overfull < 1):
            phase_moe_routed(nc, X, XT, XW, X2, XG, YG, w1, w3, w2, W13raw, W13, W2raw, W2, p12, slots)
        with nc.Else():
            phase_moe_dense(nc, X, XT, wts, w1, w3, w2, W13raw, W13, W2raw, W2, rows)
        phase_norm(nc, "n4", X, identF, out=out)


def rope_tables():
    inv = (1.0 / np.float32(1e6) ** (np.arange(0, HD, 2, dtype=np.float32) / np.float32(HD))).astype(np.float32)
    ang = inv[:, None] * np.arange(S, dtype=np.float32)[None, :]
    c, s = np.cos(ang).astype(np.float32), np.sin(ang).astype(np.float32)
    return np.stack([np.concatenate([c, c]), np.concatenate([s, -s])])


_INS = ['x', 'ctx_1024', 'mask_BxS2_bf1', 'L0_attn_W_in', 'L0_attn_W_out', 'L0_attn_log_A', 'L0_attn_W_dt', 'L0_attn_b_dt',
        'L0_xattn_Wq', 'L0_xattn_Wk', 'L0_xattn_Wv', 'L0_xattn_Wo', 'L0_ffn_norm1_w', 'L0_ffn_norm2_w', 'L0_ffn_wq',
        'L0_ffn_wk', 'L0_ffn_wv', 'L0_ffn_wo', 'L0_ffn_gate_w', 'L0_ffn_w1', 'L0_ffn_w3', 'L0_ffn_w2']


def kernel(**inputs):
    import numpy as _np
    import concourse.bacc as _bacc
    from concourse import mybir as _mybir
    from concourse.bass_utils import run_bass_kernel_spmd as _run

    nc = _bacc.Bacc("TRN2", target_bir_lowering=False, num_devices=1)
    arrays, args = {}, []
    for name in _INS:
        a = _np.ascontiguousarray(inputs[name])
        arrays[f"in_{name}_dram"] = a
        args.append(nc.dram_tensor(f"in_{name}_dram", a.shape, _mybir.dt.from_np(a.dtype), kind="ExternalInput").ap())
    arrays["rope_dram"] = rope_tables()
    args.append(nc.dram_tensor("rope_dram", (2, HD, S), F32, kind="ExternalInput").ap())
    for name in ("expert_rows_dram", "expert_out_dram"):
        args.append(nc.dram_tensor(name, (E * CAP, D), F32).ap())
    args.append(nc.dram_tensor("out_0_dram", (B, S, D), F32, kind="ExternalOutput").ap())
    decoder_layer(nc, *args)
    r = _run(nc, [arrays], core_ids=[0])
    return r.results[0]["out_0_dram"]
```

```python
from contextlib import ExitStack

import concourse.bass as bass
import numpy as np
from concourse import mybir

F32 = mybir.dt.float32
F16 = mybir.dt.float16
U8 = mybir.dt.uint8
U32 = mybir.dt.uint32
I32 = mybir.dt.int32
ALU = mybir.AluOpType
ACT = mybir.ActivationFunctionType
AX_X = mybir.AxisListType.X

P = 128
B, S, D = 2, 512, 512
T = B * S
NT = T // P
TPB = S // P
DC = D // P
S2, DCTX = 1024, 256
HD = 128
EPS = 1e-5
NEG = -1e30
PSCALE = 1024.0
SCORE_SCALE = float(1.0 / np.sqrt(HD))
E, F = 8, 1024
FC = F // P
CAP = 384
CTL = CAP // P
PAIRS = ((0, 0), (0, 1), (1, 0))


def wait_from(eng, sem, count):
    if isinstance(count, int) and count <= 0:
        return
    eng.wait_ge(sem, count)


def phase_semaphores(nc, phase):
    held = []

    def end():
        nc.clear_and_free_semaphores(held)
        nc.all_engine_barrier()

    phase.callback(end)

    def sem(name):
        held.append(nc.alloc_semaphore(name=name))
        return held[-1]

    return sem


def stand_apart(eng, passed):
    eng.sem_inc(passed, 1)


def split_banks(nc, sem, jobs, bank, ident, name):
    tr_done, hi_done, lo_done = sem(name + "_tr_done"), sem(name + "_hi_done"), sem(name + "_lo_done")
    nb = len(bank)

    def pe_job(pe, n):
        wait, blocks, _, _ = jobs[n]
        pe.wait_ge(*wait)
        if n >= nb:
            pe.wait_ge(lo_done, n - nb + 1)
        for src, off, rows, cols in blocks:
            last = nc.tensor.transpose(bank[n % nb][0:cols, off:off + rows], src, ident[0:rows, 0:rows])
        last.then_inc(tr_done, 1)

    def act_job(act, n):
        _, _, hi, _ = jobs[n]
        act.wait_ge(tr_done, n + 1)
        nc.scalar.copy(hi[0], hi[1](bank[n % nb])).then_inc(hi_done, 1)

    def dve_job(dve, n):
        _, _, hi, lo = jobs[n]
        dve.wait_ge(hi_done, n + 1)
        nc.vector.tensor_tensor(lo[0], lo[1](bank[n % nb]), hi[0], ALU.subtract).then_inc(lo_done, 1)

    return pe_job, act_job, dve_job, lo_done


def phase_ssm(nc, X, XT, CT, XG, x, ctxt, mask, W_in, W_out, log_A, W_dt, b_dt, consts, rope_in):
    identF, causal, maskb, flag, ropeC, ropeS = consts
    with ExitStack() as st:
        sem = phase_semaphores(nc, st)

        def sb(name, shape, dt):
            return st.enter_context(nc.sbuf_tensor(name, shape, dt))

        def pb(name, shape):
            return st.enter_context(nc.psum_tensor(name, shape, F32))

        win = sb("win", [P, DC, D], F32)
        wout = sb("wout", [P, DC, D], F32)
        wdt = sb("wdt", [32, D], F32)
        winT = sb("winT", [P, 2, DC, D], F16)
        woutT = sb("woutT", [P, 2, DC, D], F16)
        wdtT = sb("wdtT", [P, 2, DC, 32], F16)
        wdtR = sb("wdtR", [P, 2, DC, 32, 16], F16)
        ctx_in = [win[:].rearrange("p m (r d) -> p (m r) d", d=DCTX), sb("ctx_in1", [P, 8, DCTX], F32)[:]]
        xp = sb("xp", [P, DC, T], F32)
        XPT = sb("XPT", [P, 2, DC, T], F16)
        logA = sb("logA", [P, DC], F32)
        negA = sb("negA", [P, DC], F32)
        bdt = sb("bdt", [P, DC], F32)
        zb = sb("zb", [P, 2 * DC, S], F32)
        za = sb("za", [P, 2 * DC, S], F32)
        ys = sb("ys", [P, DC, S], F32)
        stats = sb("stats", [P, NT, 6], F32)
        mv = sb("mv", [P, NT, 2], F32)
        ve = sb("ve", [P, NT], F32)
        half = sb("half", [P, 1], F32)
        rstd = sb("rstd", [P, NT], F32)
        mask_in = sb("mask_in", [P, B * S2], U8)
        anyv = sb("anyv", [P, B], F32)
        zeros = sb("zeros", [P, D], F32)
        zeros_done, zeroed = sem("zeros_done"), sem("zeroed")
        bank = [pb(f"bank{i}", [P, 512]) for i in range(8)]

        x_in = [sem(f"x_in{b}") for b in range(B)]
        tables_in, mask_done, w_in, small_in = sem("tables_in"), sem("mask_done"), sem("w_in"), sem("small_in")
        c_in = [sem(f"c_in{b}") for b in range(B)]
        ident_zero, ident_done, causal_zero, causal_done = (sem("ident_zero"), sem("ident_done"),
                                                            sem("causal_zero"), sem("causal_done"))
        maskb_done, any_done, flag_done = sem("maskb_done"), sem("any_done"), sem("flag_done")
        rep_hi, rep_lo, expA_done, negA_done = sem("rep_hi"), sem("rep_lo"), sem("expA_done"), sem("negA_done")
        xp_ready, xp_hi, xp_f32, xp_lo = sem("xp_ready"), sem("xp_hi"), sem("xp_f32"), sem("xp_lo")
        z_ready, zb_done, za_abs, za_exp, za_ln = (sem("z_ready"), sem("zb_done"), sem("za_abs"),
                                                   sem("za_exp"), sem("za_ln"))
        dt_done, dec_done, scan_done, ys_hi, ys_lo = (sem("dt_done"), sem("dec_done"), sem("scan_done"),
                                                      sem("ys_hi"), sem("ys_lo"))
        y_ready, y_added = sem("y_ready"), sem("y_added")
        half_done, stats_done, mv_done, ve_done, rstd_done, ln_done = (
            sem("half_done"), sem("stats_done"), sem("mv_done"), sem("ve_done"), sem("rstd_done"), sem("ln_done"))

        YST = XT
        whole = lambda ap: ap[:, :]

        jobs = []
        as4 = lambda ap: ap[:, :].rearrange("p (k t) -> p k t", k=DC)

        def rows_job(i, wait):
            return (wait, [(X[:, i, k * P:(k + 1) * P], k * P, P, P) for k in range(DC)],
                    (XT[:, 0, :, i * P:(i + 1) * P], as4), (XT[:, 1, :, i * P:(i + 1) * P], as4))

        for k in range(DC):
            jobs.append(((w_in, 16), [(win[:, m, k * P:(k + 1) * P], m * P, P, P) for m in range(DC)],
                         (winT[:, 0, k, :], whole), (winT[:, 1, k, :], whole)))
        jobs += [rows_job(i, (x_in[0], 16)) for i in range(TPB)]
        as_dt = lambda ap: ap[:, 0:DC * 32].rearrange("p (k h) -> p k h", k=DC)
        jobs.append(((w_in, 32), [(wdt[:, k * P:(k + 1) * P], k * 32, 32, P) for k in range(DC)],
                     (wdtT[:, 0, :, :], as_dt), (wdtT[:, 1, :, :], as_dt)))
        first_jobs = len(jobs)
        jobs += [rows_job(i, (x_in[1], 16)) for i in range(TPB, NT)]
        late = []
        for k in range(DC):
            late.append(((w_in, 48), [(wout[:, m, k * P:(k + 1) * P], m * P, P, P) for m in range(DC)],
                         (woutT[:, 0, k, :], whole), (woutT[:, 1, k, :], whole)))
        for i in range(8):
            pair = lambda ap: ap[:, :].rearrange("p (c t) -> p c t", c=2)
            late.append(((c_in[i // 4], 16),
                         [(ctx_in[i // 4][:, 2 * (i % 4) + j, c * P:(c + 1) * P], c * 2 * P + j * P, P, P)
                          for c in range(2) for j in range(2)],
                         (CT[:, 0, :, i * 2 * P:(i + 1) * 2 * P], pair), (CT[:, 1, :, i * 2 * P:(i + 1) * 2 * P], pair)))
        norm_jobs = [rows_job(i, (ln_done, i + 1)) for i in range(NT)]
        tr_pe, tr_act, tr_dve, tr_lo = split_banks(nc, sem, jobs, bank[0:4], identF, "first")
        late_pe, late_act, late_dve, late_lo = split_banks(nc, sem, late, bank[0:2], identF, "late")
        norm_pe, norm_act, norm_dve, norm_lo = split_banks(nc, sem, norm_jobs, bank[4:8], identF, "norm")

        block = st.enter_context(nc.Block())

        @block.sync
        def _(sp):
            sp.dma_start(win[:], W_in.rearrange("(m p) d -> p m d", p=P)).then_inc(w_in, 16)
            sp.dma_start(X[:, 0:TPB, :], x[0].rearrange("(t p) d -> p t d", p=P)).then_inc(x_in[0], 16)
            sp.wait_ge(w_in, 16)
            sp.dma_start(wdt[:], W_dt).then_inc(w_in, 16)
            sp.dma_start(X[:, TPB:NT, :], x[1].rearrange("(t p) d -> p t d", p=P)).then_inc(x_in[1], 16)
            sp.wait_ge(w_in, 32)
            sp.dma_start(wout[:], W_out.rearrange("(m p) d -> p m d", p=P)).then_inc(w_in, 16)
            sp.dma_start(mask_in[:], mask.rearrange("b s -> (b s)").partition_broadcast(P)).then_inc(mask_done, 16)
            sp.dma_start(ropeC[:], rope_in[0]).then_inc(tables_in, 16)
            sp.dma_start(ropeS[:], rope_in[1]).then_inc(tables_in, 16)
            sp.wait_ge(tr_lo, DC)
            for b in range(B):
                sp.dma_start(ctx_in[b], ctxt[b].rearrange("(t p) d -> p t d", p=P)).then_inc(c_in[b], 16)
            sp.wait_ge(zeros_done, 1)
            xg = XG.rearrange("(n p r) d -> n p r d", p=P, r=4)
            for i in range(E * CAP // (4 * P)):
                sp.dma_start(xg[i], zeros[:].unsqueeze(1).broadcast_to([P, 4, D])).then_inc(zeroed, 16)
            sp.wait_ge(zeroed, 16 * (E * CAP // (4 * P)))
            sp.wait_ge(tables_in, 32)

        @block.gpsimd
        def _(pool):
            nc.gpsimd.memset(identF[:], 0.0).then_inc(ident_zero, 1)
            pool.wait_ge(ident_zero, 1)
            nc.gpsimd.affine_select(out=identF[:], in_=identF[:], compare_op=ALU.not_equal, fill=1.0, base=0,
                                    pattern=[[-1, P]], channel_multiplier=1).then_inc(ident_done, 1)
            nc.gpsimd.memset(zeros[:], 0.0).then_inc(zeros_done, 1)
            nc.gpsimd.memset(causal[:], 0.0).then_inc(causal_zero, 1)
            pool.wait_ge(causal_zero, 1)
            nc.gpsimd.affine_select(out=causal[:, S - P:S], in_=causal[:, S - P:S], compare_op=ALU.is_ge, fill=NEG,
                                    base=0, pattern=[[-1, P]], channel_multiplier=1).then_inc(causal_done, 1)
            nc.gpsimd.memset(half[:], -0.5).then_inc(half_done, 1)
            pool.wait_ge(half_done, 1)
            for i in range(NT):
                pool.wait_ge(mv_done, i + 1)
                nc.gpsimd.tensor_scalar(ve[:, i:i + 1], mv[:, i, 1:2], EPS, 1.0, ALU.add, ALU.mult).then_inc(ve_done, 1)
                pool.wait_ge(ve_done, i + 1)
                nc.gpsimd.tensor_tensor(rstd[:, i:i + 1], ve[:, i:i + 1], half[:], ALU.pow).then_inc(rstd_done, 1)

        @block.tensor
        def _(pe):
            def project(b):
                for m in range(DC):
                    n = b * DC + m
                    if n >= 2:
                        pe.wait_ge(xp_lo, n - 1)
                    for i, (hw, hx) in enumerate(PAIRS):
                        for k in range(DC):
                            last = nc.tensor.matmul(bank[6 + n % 2][:, :], winT[:, hw, k, m * P:(m + 1) * P],
                                                    XT[:, hx, k, b * S:(b + 1) * S], start=(i + k == 0),
                                                    stop=(i == 2 and k == DC - 1))
                    last.then_inc(xp_ready, 1)

            def gates(b):
                pe.wait_ge(xp_lo, DC * (b + 1))
                for m in range(DC):
                    for i, (hw, hx) in enumerate(PAIRS):
                        for k in range(DC):
                            last = nc.tensor.matmul(bank[b * DC + m][:, :],
                                                    wdtR[:, hw, k, m * 8:(m + 1) * 8, :].rearrange("p h c -> p (h c)"),
                                                    XPT[:, hx, k, b * S:(b + 1) * S], start=(i + k == 0),
                                                    stop=(i == 2 and k == DC - 1))
                    last.then_inc(z_ready, 1)

            def output(i):
                pe.wait_ge(ys_lo, DC * (i // TPB + 1))
                if i >= 2:
                    pe.wait_ge(y_added, i - 1)
                for q, (hy, hw) in enumerate(PAIRS):
                    for k in range(DC):
                        last = nc.tensor.matmul(bank[2 + i % 2][:, :], YST[:, hy, k, i * P:(i + 1) * P],
                                                woutT[:, hw, k, :], start=(q + k == 0), stop=(q == 2 and k == DC - 1))
                last.then_inc(y_ready, 1)

            pe.wait_ge(ident_done, 1)
            for n in range(first_jobs):
                tr_pe(pe, n)
            pe.wait_ge(tr_lo, 2 * TPB)
            project(0)
            for n in range(first_jobs, len(jobs)):
                tr_pe(pe, n)
            pe.wait_ge(rep_hi, 1)
            pe.wait_ge(rep_lo, 1)
            pe.wait_ge(tr_lo, len(jobs))
            gates(0)
            project(1)
            gates(1)
            pe.wait_ge(za_abs, DC)
            pe.wait_ge(zb_done, DC)
            for n in range(DC):
                late_pe(pe, n)
            pe.wait_ge(late_lo, DC)
            for i in range(TPB):
                output(i)
            for n in range(DC, len(late)):
                late_pe(pe, n)
            pe.wait_ge(za_abs, 2 * DC)
            pe.wait_ge(zb_done, 2 * DC)
            for i in range(TPB, NT):
                output(i)
                norm_pe(pe, i - TPB)
            for n in range(TPB, NT):
                norm_pe(pe, n)

        @block.scalar
        def _(act):
            def split_xp(n):
                m, b = n % DC, n // DC
                act.wait_ge(xp_ready, n + 1)
                nc.scalar.copy(XPT[:, 0, m, b * S:(b + 1) * S], bank[6 + n % 2][:, :]).then_inc(xp_hi, 1)
                nc.scalar.copy(xp[:, m, b * S:(b + 1) * S], bank[6 + n % 2][:, :]).then_inc(xp_f32, 1)

            def gate_exp(n):
                act.wait_ge(z_ready, n + 1)
                act.wait_ge(zb_done, n + 1)
                nc.scalar.activation(za[:, n, :], bank[n][:, :], ACT.Abs, bias=bdt[:, n % DC:n % DC + 1]).then_inc(za_abs, 1)
                act.wait_ge(za_abs, n + 1)
                nc.scalar.activation(za[:, n, :], za[:, n, :], ACT.Exp, scale=-1.0).then_inc(za_exp, 1)

            def gate_ln(n):
                act.wait_ge(za_exp, n + 1)
                nc.scalar.activation(za[:, n, :], za[:, n, :], ACT.Ln, bias=1.0).then_inc(za_ln, 1)

            def decay(n):
                act.wait_ge(dt_done, n + 1)
                nc.scalar.activation(za[:, n, :], zb[:, n, :], ACT.Exp, scale=negA[:, n % DC:n % DC + 1]).then_inc(dec_done, 1)

            def scan_high(n):
                act.wait_ge(scan_done, n + 1)
                nc.scalar.copy(YST[:, 0, n % DC, (n // DC) * S:(n // DC + 1) * S], ys[:, n % DC, :]).then_inc(ys_hi, 1)

            act.dma_start(logA[:], log_A.rearrange("(m h) c -> (h c) m", m=DC), allow_slow_non_contiguous=True).then_inc(small_in, 16)
            for h in range(8):
                act.dma_start(bdt[h * 16:(h + 1) * 16, :],
                              b_dt.rearrange("(m h) -> h m", h=8)[h].partition_broadcast(16),
                              allow_slow_non_contiguous=True).then_inc(small_in, 16)
            for n in range(first_jobs):
                tr_act(act, n)
            act.wait_ge(tr_lo, first_jobs)
            nc.scalar.copy(wdtR[:, 0], wdtT[:, 0, :, :].unsqueeze(3).broadcast_to([P, DC, 32, 16])).then_inc(rep_hi, 1)
            for n in range(DC):
                split_xp(n)
            for n in range(first_jobs, len(jobs)):
                tr_act(act, n)
            act.wait_ge(small_in, 144)
            nc.scalar.activation(logA[:], logA[:], ACT.Exp).then_inc(expA_done, 1)
            act.wait_ge(negA_done, 1)
            for n in range(DC):
                gate_exp(n)
            for n in range(DC, DC + 2):
                split_xp(n)
            for n in range(DC):
                gate_ln(n)
            for n in range(DC + 2, 2 * DC):
                split_xp(n)
            for n in range(DC):
                decay(n)
            for n in range(DC):
                scan_high(n)
            for n in range(DC, 2 * DC):
                gate_exp(n)
            for n in range(DC):
                late_act(act, n)
            for n in range(DC, 2 * DC):
                gate_ln(n)
            for n in range(DC, 2 * DC):
                decay(n)
            for n in range(DC, 2 * DC):
                scan_high(n)
            for n in range(DC, len(late)):
                late_act(act, n)
            for n in range(NT):
                norm_act(act, n)

        @block.vector
        def _(dve):
            def xp_low(n):
                m, b = n % DC, n // DC
                dve.wait_ge(xp_hi, n + 1)
                dve.wait_ge(xp_f32, n + 1)
                nc.vector.tensor_tensor(XPT[:, 1, m, b * S:(b + 1) * S], xp[:, m, b * S:(b + 1) * S],
                                        XPT[:, 0, m, b * S:(b + 1) * S], ALU.subtract).then_inc(xp_lo, 1)

            def gate_max(n):
                dve.wait_ge(z_ready, n + 1)
                nc.vector.tensor_scalar(zb[:, n, :], bank[n][:, :], bdt[:, n % DC:n % DC + 1], 0.0, ALU.add,
                                        ALU.max).then_inc(zb_done, 1)

            def softplus(n):
                dve.wait_ge(zb_done, n + 1)
                dve.wait_ge(za_ln, n + 1)
                nc.vector.tensor_tensor(zb[:, n, :], zb[:, n, :], za[:, n, :], ALU.add).then_inc(dt_done, 1)

            def scan(n):
                m, b = n % DC, n // DC
                dve.wait_ge(dec_done, n + 1)
                if b:
                    dve.wait_ge(ys_hi, n - DC + 1)
                    dve.wait_ge(ys_lo, n - DC + 1)
                nc.vector.tensor_tensor_scan(ys[:, m, :], za[:, n, :], xp[:, m, b * S:(b + 1) * S], 0.0,
                                             ALU.mult, ALU.add).then_inc(scan_done, 1)

            def scan_low(n):
                m, b = n % DC, n // DC
                dve.wait_ge(ys_hi, n + 1)
                nc.vector.tensor_tensor(YST[:, 1, m, b * S:(b + 1) * S], ys[:, m, :],
                                        YST[:, 0, m, b * S:(b + 1) * S], ALU.subtract).then_inc(ys_lo, 1)

            def add(i):
                dve.wait_ge(y_ready, i + 1)
                nc.vector.tensor_tensor(X[:, i, :], bank[2 + i % 2][:, :], X[:, i, :], ALU.add).then_inc(y_added, 1)
                dve.wait_ge(y_added, i + 1)
                nc.vector.bn_stats(stats[:, i, :], X[:, i, :]).then_inc(stats_done, 1)
                dve.wait_ge(stats_done, i + 1)
                nc.vector.bn_aggr(mv[:, i, :], stats[:, i, :]).then_inc(mv_done, 1)

            def layer_norm(i):
                dve.wait_ge(rstd_done, i + 1)
                dve.wait_ge(mv_done, i + 1)
                nc.vector.tensor_scalar(X[:, i, :], X[:, i, :], mv[:, i, 0:1], rstd[:, i:i + 1], ALU.subtract,
                                        ALU.mult).then_inc(ln_done, 1)

            for n in range(first_jobs):
                tr_dve(dve, n)
            dve.wait_ge(tr_lo, first_jobs)
            nc.vector.tensor_copy(wdtR[:, 1], wdtT[:, 1, :, :].unsqueeze(3).broadcast_to([P, DC, 32, 16])).then_inc(rep_lo, 1)
            for n in range(DC):
                xp_low(n)
            for n in range(first_jobs, len(jobs)):
                tr_dve(dve, n)
            dve.wait_ge(expA_done, 1)
            nc.vector.tensor_scalar(negA[:], logA[:], -1.0, None, ALU.mult).then_inc(negA_done, 1)
            for n in range(DC):
                gate_max(n)
            for n in range(DC, DC + 2):
                xp_low(n)
            for n in range(DC):
                softplus(n)
            for n in range(DC + 2, 2 * DC):
                xp_low(n)
            for n in range(DC):
                scan(n)
            for n in range(DC):
                scan_low(n)
            for n in range(DC, 2 * DC):
                gate_max(n)
            for n in range(DC):
                late_dve(dve, n)
            for n in range(DC, 2 * DC):
                softplus(n)
            for n in range(DC, 2 * DC):
                scan(n)
            for n in range(DC, 2 * DC):
                scan_low(n)
            for i in range(TPB):
                add(i)
            for n in range(DC, len(late)):
                late_dve(dve, n)
            for i in range(TPB):
                layer_norm(i)
            for i in range(TPB, NT):
                add(i)
                if i > TPB:
                    layer_norm(i - 1)
                norm_dve(dve, i - TPB)
            layer_norm(NT - 1)
            dve.wait_ge(mask_done, 16)
            nc.vector.tensor_scalar(maskb[:].rearrange("p b s -> p (b s)"), mask_in[:], -1.0, -NEG, ALU.add,
                                    ALU.mult).then_inc(maskb_done, 1)
            for b in range(B):
                last = nc.vector.tensor_reduce(anyv[:, b:b + 1], mask_in[:, b * S2:(b + 1) * S2], AX_X, ALU.max)
            last.then_inc(any_done, 1)
            dve.wait_ge(any_done, 1)
            nc.vector.tensor_scalar(flag[:], anyv[:], PSCALE, None, ALU.mult).then_inc(flag_done, 1)
            for n in range(TPB, NT):
                norm_dve(dve, n)


def phase_norm(nc, name, X, identF, XT=None, norm_w=None, layer=True, out=None, keep=None, add=None,
               rows=None, fetch=()):
    with ExitStack() as st:
        sem = phase_semaphores(nc, st)

        def sb(n, shape, dt):
            return st.enter_context(nc.sbuf_tensor(f"{name}_{n}", shape, dt))

        stats = sb("stats", [P, NT, 6], F32)
        mv = sb("mv", [P, NT, 2], F32)
        ve = sb("ve", [P, NT], F32)
        half = sb("half", [P, 1], F32)
        rstd = sb("rstd", [P, NT], F32)
        sq = sb("sq", [P, 2, D], F32)
        ms = sb("ms", [P, NT], F32)
        me = sb("me", [P, NT], F32)
        rr = sb("rr", [P, NT], F32)
        wb = sb("wb", [P, D], F32)
        XR = 4 if rows is None else NT
        xw = sb("xw", [P, 4, D], F32) if rows is None else rows
        bank = [st.enter_context(nc.psum_tensor(f"{name}_bank{i}", [P, 512], F32)) for i in range(4)]

        s = lambda n: sem(f"{name}_{n}")
        half_done, w_in, stats_done, mv_done, ve_done, rstd_done, ln_done = (
            s("half_done"), s("w_in"), s("stats_done"), s("mv_done"), s("ve_done"), s("rstd_done"), s("ln_done"))
        ms_done, me_done, rr_done, xw_done, out_done = (
            s("ms_done"), s("me_done"), s("rr_done"), s("xw_done"), s("out_done"))
        rms, fetched = norm_w is not None, s("fetched")
        jobs = []
        if XT is not None:
            for i in range(NT):
                src = xw[:, i % XR] if rms else X[:, i]
                as4 = lambda ap: ap[:, :].rearrange("p (k t) -> p k t", k=DC)
                jobs.append(((xw_done if rms else ln_done, i + 1),
                             [(src[:, k * P:(k + 1) * P], k * P, P, P) for k in range(DC)],
                             (XT[:, 0, :, i * P:(i + 1) * P], as4), (XT[:, 1, :, i * P:(i + 1) * P], as4)))
        tr_pe, tr_act, tr_dve, tr_lo = split_banks(nc, sem, jobs, bank, identF, name)

        block = st.enter_context(nc.Block())

        @block.sync
        def _(sp):
            for dst, src in fetch:
                sp.dma_start(dst, src).then_inc(fetched, 16)
            if rms:
                sp.dma_start(wb[:], norm_w.partition_broadcast(P)).then_inc(w_in, 16)
                sp.wait_ge(w_in, 16)
            if out is not None:
                for i in range(NT):
                    sp.wait_ge(ln_done, i + 1)
                    sp.dma_start(out[i // TPB, (i % TPB) * P:(i % TPB + 1) * P, :], X[:, i, :]).then_inc(out_done, 16)
                sp.wait_ge(out_done, 16 * NT)
            if fetch:
                sp.wait_ge(fetched, 16 * len(fetch))

        @block.gpsimd
        def _(pool):
            nc.gpsimd.memset(half[:], -0.5).then_inc(half_done, 1)
            pool.wait_ge(half_done, 1)
            if rms:
                pool.wait_ge(w_in, 16)
            for i in range(NT + 4):
                if layer and i < NT:
                    pool.wait_ge(mv_done, i + 1)
                    nc.gpsimd.tensor_scalar(ve[:, i:i + 1], mv[:, i, 1:2], EPS, 1.0, ALU.add, ALU.mult).then_inc(ve_done, 1)
                    pool.wait_ge(ve_done, i + 1)
                    nc.gpsimd.tensor_tensor(rstd[:, i:i + 1], ve[:, i:i + 1], half[:], ALU.pow).then_inc(rstd_done, 1)
                n = i - 3
                if rms and 0 <= n < NT:
                    pool.wait_ge(ms_done, n + 1)
                    nc.gpsimd.tensor_scalar(me[:, n:n + 1], ms[:, n:n + 1], 1.0 / D, EPS, ALU.mult, ALU.add).then_inc(me_done, 1)
                    pool.wait_ge(me_done, n + 1)
                    nc.gpsimd.tensor_tensor(rr[:, n:n + 1], me[:, n:n + 1], half[:], ALU.pow).then_inc(rr_done, 1)
                n = i - 4
                if 0 <= n < NT and keep is not None:
                    nc.gpsimd.tensor_scalar(keep[:, n, :], X[:, n, :], 1.0, 1.0, ALU.mult, ALU.mult)
                if 0 <= n < NT and add is not None:
                    pool.wait_ge(xw_done, n + 1)
                    nc.gpsimd.tensor_tensor(X[:, n, :], X[:, n, :], add[:, n, :], ALU.add)

        @block.tensor
        def _(pe):
            for n in range(len(jobs)):
                tr_pe(pe, n)

        @block.scalar
        def _(act):
            if rms:
                for i in range(NT):
                    if layer:
                        act.wait_ge(ln_done, i + 1)
                    if i >= 2:
                        act.wait_ge(ms_done, i - 1)
                    nc.scalar.activation(sq[:, i % 2, :], X[:, i, :], ACT.Square, accum_out=ms[:, i:i + 1]).then_inc(ms_done, 1)
                    if i >= 3:
                        tr_act(act, i - 3)
                for i in range(NT - 3, NT):
                    tr_act(act, i)
            else:
                for i in range(len(jobs)):
                    tr_act(act, i)

        @block.vector
        def _(dve):
            if rms:
                dve.wait_ge(w_in, 16)
            for i in range(NT + 6):
                if layer and i < NT:
                    nc.vector.bn_stats(stats[:, i, :], X[:, i, :]).then_inc(stats_done, 1)
                    dve.wait_ge(stats_done, i + 1)
                    nc.vector.bn_aggr(mv[:, i, :], stats[:, i, :]).then_inc(mv_done, 1)
                n = i - 2
                if layer and 0 <= n < NT:
                    dve.wait_ge(rstd_done, n + 1)
                    dve.wait_ge(mv_done, n + 1)
                    nc.vector.tensor_scalar(X[:, n, :], X[:, n, :], mv[:, n, 0:1], rstd[:, n:n + 1], ALU.subtract,
                                            ALU.mult).then_inc(ln_done, 1)
                n = i - 4
                if rms and 0 <= n < NT:
                    dve.wait_ge(rr_done, n + 1)
                    if layer:
                        dve.wait_ge(ln_done, n + 1)
                    if n >= XR:
                        dve.wait_ge(tr_lo, n - XR + 1)
                    nc.vector.scalar_tensor_tensor(out=xw[:, n % XR, :], in0=X[:, n, :], scalar=rr[:, n:n + 1], in1=wb[:],
                                                   op0=ALU.mult, op1=ALU.mult).then_inc(xw_done, 1)
                n = i - 6
                if 0 <= n < len(jobs):
                    tr_dve(dve, n)


def attention(nc, name, X, XT, KVT, identF, Wq, Wk, Wv, Wo, kv_heads, groups, keys, mask_of, flag, rope):
    NS = groups * TPB
    NBLK = keys // P
    NB = -(-NBLK // 4)
    KC = KVT.shape[2]
    WQ, WKV = DC * groups * HD, KC * HD
    causal = rope is not None
    JP, JO = 6, TPB
    JT = JP + JO
    NJ = 2 if causal else 1
    TAIL = 4
    if causal:
        proj = [("q", g) for g in range(groups)] + [("k", 0), ("v", 0)]
        slots = {0: ([("proj", 0)], []), 1: ([("proj", 1)], []), 2: ([("proj", 2)], []), 4: ([("proj", 3)], []),
                 5: ([("proj", 4)], []), 6: ([("proj", 5)], []), 8: ([("wo", 0)], []), 10: ([("wo", 1)], []),
                 12: ([("wo", 2)], []), 14: ([("wo", 3)], [])}
    else:
        proj = [("q", 0), ("q", 1), ("k", 0), ("k", 1), ("v", 0), ("v", 1)]
        slots = {0: ([("proj", 0)], []), 1: ([("proj", 1)], []), 2: ([("proj", 2)], []),
                 3: ([("proj", 3)], [("proj", 4)]), 4: ([("proj", 5)], []), 5: ([("wo", 0)], []),
                 6: ([("wo", 1)], []), 7: ([("wo", 2)], [("wo", 3)])}
    assert len(proj) == JP
    last_proj_slot = max(j for j, l in slots.items() if any(k == "proj" for k, _ in l[0] + l[1]))
    first_piece = last_proj_slot + 1

    def jobs_before(h):
        return JP if isinstance(h, int) and h == 0 else 2 * JP + JT * (h - 1)

    def projections_before(h):
        return jobs_before(h) if isinstance(h, int) and h <= 1 else jobs_before(h) - JO

    def slot_jobs(h, j, first, last, late=None):
        out, k = [], 0
        for jj in range(NS):
            for place, jobs in enumerate(slots.get(jj, ([], []))):
                for kind, i in jobs:
                    if kind == "wo" and first or kind == "proj" and last:
                        continue
                    if jj == j and late in (None, place):
                        out.append((kind, i, jobs_before(h) + k, k % NJ))
                    k += 1
        return out

    with ExitStack() as st:
        sem = phase_semaphores(nc, st)

        def sb(n, shape, dt):
            return st.enter_context(nc.sbuf_tensor(f"{name}_{n}", shape, dt))

        def pb(n, shape):
            return st.enter_context(nc.psum_tensor(f"{name}_{n}", shape, F32))

        WPraw = sb("WPraw", [P, WQ + 2 * WKV], F32)
        WP = sb("WP", [P, 2, WQ + 2 * WKV], F16)
        WOraw = sb("WOraw", [P, groups, D], F32)
        WO = sb("WO", [P, 2, groups, D], F16)
        QT = [sb(f"QT{b}", [P, 2, groups, S], F16) for b in range(B)]
        KT = [sb(f"KT{b}", [P, 2, keys], F16) for b in range(B)]
        V = [sb(f"V{b}", [P, 2, NBLK, HD], F16) for b in range(B)]
        OT = [sb(f"OT{b}", [P, 2, groups, S], F16) for b in range(B)]
        SC = [sb(f"SC{i}", [P, keys], F32) for i in range(2)]
        PN = [sb(f"PN{i}", [P, keys], F32) for i in range(2)]
        PT = [sb(f"PT{i}", [P, 2, NBLK, S], F16) for i in range(2)]
        mn = sb("mn", [P, 4], F32)
        sm = sb("sm", [P, 4], F32)
        rc = sb("rc", [P, 4], F32)
        rA = [sb(f"rA{i}", [P, S if causal else 1], F32) for i in range(2)]
        rB = [sb(f"rB{i}", [P, S if causal else 1], F32) for i in range(2)]
        psS = [pb(f"psS{i}", [P, NB * 512]) for i in range(2)]
        psT = [pb(f"psT{i}", [P, 512]) for i in range(2)]
        psO = pb("psO", [P, 512])
        psJ = [pb(f"psJ{i}", [P, 512]) for i in range(NJ)]

        s = lambda n: sem(f"{name}_{n}")
        wp_in, wp_hi, wp_done = s("wp_in"), s("wp_hi"), s("wp_done")
        wo_in, wo_hi, wo_done = s("wo_in"), s("wo_hi"), s("wo_done")
        scores_ready, masked, exp_done, recip_done, norm_done = (
            s("scores_ready"), s("masked"), s("exp_done"), s("recip_done"), s("norm_done"))
        tr_ready, tr_hi, tr_lo = s("tr_ready"), s("tr_hi"), s("tr_lo")
        pv_ready, o_hi, o_lo = s("pv_ready"), s("o_hi"), s("o_lo")
        job_ready, job_hi, job_free = s("job_ready"), s("job_hi"), s("job_free")
        rope_added, rope_hi, rope_done = s("rope_added"), s("rope_hi"), s("rope_done")

        pool_passed, dve_passed = s("pool_passed"), s("dve_passed")
        wp_pieces = [(WP[:, :, c:c + 512], WPraw[:, c:c + 512]) for c in range(0, WQ + 2 * WKV, 512)]
        wo_pieces = [(WO[:, :, g, :], WOraw[:, g, :]) for g in range(groups)]
        NWP, NWO = len(wp_pieces), len(wo_pieces)

        def step_pieces(kv, b, j, last_kv):
            i = j - first_piece
            if b == 0 and not last_kv and 0 <= i < NWP:
                return "wp", i, (kv + 1) * NWP + i
            if b == 1 and j < NWO:
                return "wo", j, kv * NWO + j
            return None

        wq_v = WP[:, :, 0:WQ].rearrange("p l (k g c) -> p l k g c", k=DC, g=groups)
        wk_v = WP[:, :, WQ:WQ + WKV].rearrange("p l (k c) -> p l k c", k=KC)
        wv_v = WP[:, :, WQ + WKV:].rearrange("p l (k c) -> p l k c", k=KC)

        def width(t):
            return (t + 1) * P if causal else keys

        def blocks(t, i):
            return range(4 * i, min(4 * i + 4, width(t) // P))

        block = st.enter_context(nc.Block())

        def halves(emit):
            for b in range(B):
                emit(b, 0, b, b == 0, False)
            yield 1, kv_heads - 1
            for b in range(B):
                emit(2 * (kv_heads - 1) + b, kv_heads - 1, b, False, b == B - 1)

        @block.sync
        def _(sp):
            def load_kv(kv):
                wait_from(sp, wp_done, kv * NWP)
                sp.dma_start(WPraw[:, 0:WQ].rearrange("p (k c) -> p k c", k=DC),
                             Wq[:, bass.ds(kv * (groups * HD), groups * HD)].rearrange("(k p) c -> p k c", p=P)).then_inc(wp_in, 16)
                sp.dma_start(WPraw[:, WQ:WQ + WKV].rearrange("p (k c) -> p k c", k=KC),
                             Wk[:, bass.ds(kv * HD, HD)].rearrange("(k p) c -> p k c", p=P)).then_inc(wp_in, 16)
                sp.dma_start(WPraw[:, WQ + WKV:].rearrange("p (k c) -> p k c", k=KC),
                             Wv[:, bass.ds(kv * HD, HD)].rearrange("(k p) c -> p k c", p=P)).then_inc(wp_in, 16)
                wait_from(sp, wo_done, kv * NWO)
                sp.dma_start(WOraw[:], Wo[bass.ds(kv * (groups * HD), groups * HD), :].rearrange(
                    "(g p) d -> p g d", p=P)).then_inc(wo_in, 16)

            load_kv(0)
            with sp.Fori(1, kv_heads) as kv:
                load_kv(kv)

        @block.gpsimd
        def _(pool):
            def piece_low(what, i, n):
                (dst, src), hi_done, done = ((wp_pieces[i], wp_hi, wp_done) if what == "wp" else
                                             (wo_pieces[i], wo_hi, wo_done))
                pool.wait_ge(hi_done, n + 1)
                nc.gpsimd.tensor_tensor(dst[:, 1], src, dst[:, 0], ALU.subtract).then_inc(done, 1)

            def rope_sum(h, b, i, job):
                par = (b * (JP - 1) + i) % 2
                pool.wait_ge(job_free, job + 1)
                nc.gpsimd.tensor_tensor(rA[par][:], rA[par][:], rB[par][:], ALU.add).then_inc(rope_added, 1)

            def rope_low(h, b, i):
                r = (JP - 1) * h + i
                par = (b * (JP - 1) + i) % 2
                pool.wait_ge(rope_hi, r + 1)
                dst = QT[b][:, :, i, :] if proj[i][0] == "q" else KT[b][:, :, :]
                nc.gpsimd.tensor_tensor(dst[:, 1, :], rA[par][:], dst[:, 0, :], ALU.subtract).then_inc(rope_done, 1)

            def half(h, kv, b, first, last):
                for j in range(NS):
                    n = h * NS + j
                    pool.wait_ge(recip_done, n + 1)
                    wait_from(pool, tr_ready, (n - 1) * NB)
                    w = width(j % TPB)
                    stand_apart(pool, pool_passed)
                    nc.gpsimd.tensor_scalar(PN[j % 2][:, 0:w], SC[j % 2][:, 0:w], rc[:, j % 4:j % 4 + 1],
                                            PSCALE if flag is None else flag[:, b:b + 1], ALU.mult,
                                            ALU.mult).then_inc(norm_done, 1)
                    turned = [(i, job) for kind, i, job, _ in slot_jobs(h, j, first, last)
                              if causal and kind == "proj" and proj[i][0] != "v"]
                    for i, job in turned:
                        rope_sum(h + 1, 1 - b, i, job)
                    piece = step_pieces(kv, b, j, isinstance(kv, int) and kv == kv_heads - 1)
                    if piece:
                        piece_low(*piece)
                    for i, job in turned:
                        rope_low(h + 1, 1 - b, i)

            if causal:
                for i in range(JP - 1):
                    rope_sum(0, 0, i, i)
                    rope_low(0, 0, i)
            mid = halves(half)
            lo, hi = next(mid)
            with pool.Fori(lo, hi) as kv:
                for b in range(B):
                    half(kv * 2 + b, kv, b, False, False)
            for _ in mid:
                pass

        @block.tensor
        def _(pe):
            def project(h, b, i, job, bank):
                kind, a = proj[i]
                wait_from(pe, job_free, job - NJ + 1)
                if kind == "q":
                    for q, (hw, hx) in enumerate(PAIRS):
                        for k in range(DC):
                            last = nc.tensor.matmul(psJ[bank][:, :], wq_v[:, hw, k, a, :], XT[:, hx, k, b * S:(b + 1) * S],
                                                    start=(q + k == 0), stop=(q == 2 and k == DC - 1))
                elif kind == "k":
                    for q, (hw, hx) in enumerate(PAIRS):
                        for k in range(KC):
                            last = nc.tensor.matmul(psJ[bank][:, :], wk_v[:, hw, k, :],
                                                    KVT[:, hx, k, b * keys + a * 512:b * keys + a * 512 + 512],
                                                    start=(q + k == 0), stop=(q == 2 and k == KC - 1))
                else:
                    for m in range(4):
                        at = b * keys + (4 * a + m) * P
                        for q, (hw, hx) in enumerate(PAIRS):
                            for k in range(KC):
                                last = nc.tensor.matmul(psJ[bank][:, m * P:(m + 1) * P], KVT[:, hx, k, at:at + P],
                                                        wv_v[:, hw, k, :], start=(q + k == 0),
                                                        stop=(q == 2 and k == KC - 1))
                last.then_inc(job_ready, 1)

            def output(h, b, t, job, bank):
                pe.wait_ge(o_lo, (h + 1) * groups)
                wait_from(pe, job_free, job - NJ + 1)
                for g in range(groups):
                    for q, (ho, hw) in enumerate(PAIRS):
                        last = nc.tensor.matmul(psJ[bank][:, :], OT[b][:, ho, g, t * P:(t + 1) * P], WO[:, hw, g, :],
                                                start=(g + q == 0), stop=(g == groups - 1 and q == 2))
                last.then_inc(job_ready, 1)

            def scores(n, b, g, t, j):
                wait_from(pe, masked, n - 1)
                w = width(t)
                for c in range(0, w, 512):
                    cw = min(512, w - c)
                    for q, (hq, hk) in enumerate(PAIRS):
                        last = nc.tensor.matmul(psS[j % 2][:, c:c + cw], QT[b][:, hq, g, t * P:(t + 1) * P],
                                                KT[b][:, hk, c:c + cw], start=(q == 0), stop=(q == 2))
                last.then_inc(scores_ready, 1)

            def transposes(m, t, j):
                pe.wait_ge(norm_done, m + 1)
                for i in range(NB):
                    u = m * NB + i
                    wait_from(pe, tr_lo, u - 1)
                    for blk in blocks(t, i):
                        last = nc.tensor.transpose(psT[(j * NB + i) % 2][:, (blk % 4) * P:(blk % 4 + 1) * P],
                                                   PN[j % 2][:, blk * P:(blk + 1) * P], identF[:])
                    last.then_inc(tr_ready, 1)

            def values(head, steps, b, g):
                pe.wait_ge(tr_lo, steps * NB)
                wait_from(pe, o_lo, head)
                for blk in range(NBLK):
                    c = blk * P if causal else 0
                    for q, (hv, hp) in enumerate(PAIRS):
                        last = nc.tensor.matmul(psO[:, c:], V[b][:, hv, blk, :], PT[g % 2][:, hp, blk, c:],
                                                start=(blk + q == 0), stop=(blk == NBLK - 1 and q == 2))
                last.then_inc(pv_ready, 1)

            def jobs(h, kv, b, j, first, last, late):
                for kind, i, job, bank in slot_jobs(h, j, first, last, late):
                    if kind == "proj":
                        if b == 1 and i == 0:
                            pe.wait_ge(wp_done, (kv + 2) * NWP)
                        project(h + 1, 1 - b, i, job, bank)
                    else:
                        pe.wait_ge(wo_done, (kv + b) * NWO)
                        output(h - 1, 1 - b, i, job, bank)

            def half(h, kv, b, first, last):
                for j in range(NS + (TAIL if last else 0)):
                    n = h * NS + j
                    if j == 0:
                        pe.wait_ge(job_free, projections_before(h))
                        if causal:
                            pe.wait_ge(rope_done, (h + 1) * (JP - 1))
                    if j < NS:
                        scores(n, b, j // TPB, j % TPB, j)
                    jobs(h, kv, b, j, first, last, 0)
                    m = j - TAIL
                    if m % TPB == TPB - 1 and (m >= 0 or not first):
                        values(h * groups + m // TPB, n - TAIL + 1, b if m >= 0 else 1 - b, (m % NS) // TPB)
                    jobs(h, kv, b, j, first, last, 1)
                    m = j - 2
                    if m < NS and (m >= 0 or not first):
                        mj = m % NS
                        transposes(n - 2, mj % TPB, mj)

            pe.wait_ge(wp_done, NWP)
            for i in range(JP):
                project(0, 0, i, i, i % NJ)
            mid = halves(half)
            lo, hi = next(mid)
            with pe.Fori(lo, hi) as kv:
                for b in range(B):
                    half(kv * 2 + b, kv, b, False, False)
            for _ in mid:
                pass
            pe.wait_ge(wo_done, kv_heads * NWO)
            for t in range(TPB):
                h = 2 * kv_heads - 1
                output(h, 1, t, jobs_before(h) + JO + t, t % NJ)

        def job_view(i):
            kind, a = proj[i]
            if kind == "q":
                return lambda b, hl: QT[b][:, hl, a, :]
            if kind == "k":
                return lambda b, hl: KT[b][:, hl, a * 512:(a + 1) * 512]
            return lambda b, hl: V[b][:, hl, 4 * a:4 * a + 4, :].rearrange("p m c -> p (m c)")

        def plain(i):
            return not causal or proj[i][0] == "v"

        def plain_count(h, i):
            return h + 1 if causal else JP * h + i + 1

        @block.scalar
        def _(act):
            def job_high(h, b, i, job, bank):
                act.wait_ge(job_ready, job + 1)
                nc.scalar.copy(job_view(i)(b, 0), psJ[bank][:, :]).then_inc(job_hi, 1)

            def rope_high(h, b, i):
                r = (JP - 1) * h + i
                par = (b * (JP - 1) + i) % 2
                dst = QT[b][:, :, i, :] if proj[i][0] == "q" else KT[b][:, :, :]
                act.wait_ge(rope_added, r + 1)
                nc.scalar.copy(dst[:, 0, :], rA[par][:]).then_inc(rope_hi, 1)

            short = [] if causal else [j for j, l in slots.items() if l[0][0][0] == "proj" and proj[l[0][0][1]][0] != "q"]

            def piece_high(what, i):
                (dst, src), hi_done = (wp_pieces[i], wp_hi) if what == "wp" else (wo_pieces[i], wo_hi)
                nc.scalar.copy(dst[:, 0], src).then_inc(hi_done, 1)

            def jobs(h, b, j, first, last, late):
                for kind, i, job, bank in slot_jobs(h, j, first, last, late):
                    if kind == "proj" and plain(i):
                        job_high(h + 1, 1 - b, i, job, bank)

            def half(h, kv, b, first, last):
                for j in range(NS + (TAIL if last else 0)):
                    n = h * NS + j
                    if j in short:
                        jobs(h, b, j, first, last, 0)
                    if j < NS:
                        w = width(j % TPB)
                        act.wait_ge(masked, n + 1)
                        nc.scalar.activation(SC[j % 2][:, 0:w], SC[j % 2][:, 0:w], ACT.Exp,
                                             bias=mn[:, j % 4:j % 4 + 1], scale=-1.0,
                                             accum_out=sm[:, j % 4:j % 4 + 1]).then_inc(exp_done, 1)
                    if j not in short:
                        jobs(h, b, j, first, last, 0)
                    m = j - TAIL
                    if m % TPB == TPB - 1 and (m >= 0 or not first):
                        mb, mg = (b if m >= 0 else 1 - b), (m % NS) // TPB
                        act.wait_ge(pv_ready, h * groups + m // TPB + 1)
                        nc.scalar.activation(OT[mb][:, 0, mg, :], psO[:, :], ACT.Copy, scale=1.0 / PSCALE).then_inc(o_hi, 1)
                    jobs(h, b, j, first, last, 1)
                    m = j - 2
                    if m < NS and (m >= 0 or not first):
                        mj = m % NS
                        mt, mg = mj % TPB, mj // TPB
                        for i in range(NB):
                            u = (n - 2) * NB + i
                            bl = blocks(mt, i)
                            act.wait_ge(tr_ready, u + 1)
                            nc.scalar.copy(PT[mg % 2][:, 0, bl[0]:bl[-1] + 1, mt * P:(mt + 1) * P],
                                           psT[(mj * NB + i) % 2][:, 0:len(bl) * P].rearrange("p (k t) -> p k t", t=P)
                                           ).then_inc(tr_hi, 1)
                    piece = step_pieces(kv, b, j, last or isinstance(kv, int) and kv == kv_heads - 1)
                    if piece and piece[0] == "wp":
                        if piece[1] == 0:
                            act.wait_ge(wp_in, 48 * (kv + 2))
                            act.wait_ge(job_ready, jobs_before(h + 1) - (0 if first else JO))
                        piece_high(*piece[:2])
                    elif piece:
                        if piece[1] == 0:
                            act.wait_ge(wo_in, 16 * (kv + 1))
                            act.wait_ge(job_ready, jobs_before(h))
                        piece_high(*piece[:2])
                    for kind, i, job, _ in slot_jobs(h, j, first, last):
                        if causal and kind == "proj" and proj[i][0] != "v":
                            rope_high(h + 1, 1 - b, i)

            act.wait_ge(wp_in, 48)
            for i in range(NWP):
                piece_high("wp", i)
            for i in range(JP):
                if plain(i):
                    job_high(0, 0, i, i, i % NJ)
                else:
                    rope_high(0, 0, i)
            mid = halves(half)
            lo, hi = next(mid)
            with act.Fori(lo, hi) as kv:
                for b in range(B):
                    half(kv * 2 + b, kv, b, False, False)
            for _ in mid:
                pass

        @block.vector
        def _(dve):
            def job_low(h, b, i, job, bank):
                if plain(i):
                    dve.wait_ge(job_hi, plain_count(h, i))
                    dve.wait_ge(job_ready, job + 1)
                    nc.vector.tensor_tensor(job_view(i)(b, 1), psJ[bank][:, :], job_view(i)(b, 0),
                                            ALU.subtract).then_inc(job_free, 1)
                    return
                r = (JP - 1) * h + i
                par = (b * (JP - 1) + i) % 2
                dve.wait_ge(job_ready, job + 1)
                wait_from(dve, rope_done, r - 1)
                ropeC, ropeS = rope
                nc.vector.tensor_tensor(rA[par][:], psJ[bank][:, :], ropeC[:], ALU.mult)
                nc.vector.tensor_tensor(rB[par][64:128, :], psJ[bank][0:64, :], ropeS[0:64, :], ALU.mult)
                nc.vector.tensor_tensor(rB[par][0:64, :], psJ[bank][64:128, :], ropeS[64:128, :],
                                        ALU.mult).then_inc(job_free, 1)

            def output_add(h, b, t, job, bank):
                dve.wait_ge(job_ready, job + 1)
                nc.vector.tensor_tensor(X[:, b * TPB + t, :], psJ[bank][:, :], X[:, b * TPB + t, :], ALU.add).then_inc(job_free, 1)

            def jobs(h, b, j, first, last, late):
                for kind, i, job, bank in slot_jobs(h, j, first, last, late):
                    if kind == "proj":
                        job_low(h + 1, 1 - b, i, job, bank)
                    else:
                        output_add(h - 1, 1 - b, i, job, bank)

            def half(h, kv, b, first, last):
                for j in range(NS + (TAIL if last else 0)):
                    n = h * NS + j
                    if j < NS:
                        w = width(j % TPB)
                        dve.wait_ge(scores_ready, n + 1)
                        wait_from(dve, norm_done, n - 1)
                        stand_apart(dve, dve_passed)
                        nc.vector.tensor_tensor_reduce(out=SC[j % 2][:, 0:w], in0=psS[j % 2][:, 0:w],
                                                       in1=mask_of(b, j % TPB), scale=-SCORE_SCALE, scalar=3e38,
                                                       op0=ALU.add, op1=ALU.min,
                                                       accum_out=mn[:, j % 4:j % 4 + 1]).then_inc(masked, 1)
                    jobs(h, b, j, first, last, 0)
                    if j < NS:
                        dve.wait_ge(exp_done, n + 1)
                        nc.vector.reciprocal(rc[:, j % 4:j % 4 + 1], sm[:, j % 4:j % 4 + 1]).then_inc(recip_done, 1)
                    m = j - TAIL
                    if m % TPB == TPB - 1 and (m >= 0 or not first):
                        mb, mg = (b if m >= 0 else 1 - b), (m % NS) // TPB
                        dve.wait_ge(o_hi, h * groups + m // TPB + 1)
                        nc.vector.scalar_tensor_tensor(out=OT[mb][:, 1, mg, :], in0=psO[:, :], scalar=1.0 / PSCALE,
                                                       in1=OT[mb][:, 0, mg, :], op0=ALU.mult,
                                                       op1=ALU.subtract).then_inc(o_lo, 1)
                    jobs(h, b, j, first, last, 1)
                    m = j - 2
                    if m < NS and (m >= 0 or not first):
                        mj = m % NS
                        mt, mg = mj % TPB, mj // TPB
                        for i in range(NB):
                            u = (n - 2) * NB + i
                            bl = blocks(mt, i)
                            dve.wait_ge(tr_hi, u + 1)
                            dst = (slice(bl[0], bl[-1] + 1), slice(mt * P, (mt + 1) * P))
                            nc.vector.tensor_tensor(PT[mg % 2][:, 1, dst[0], dst[1]],
                                                    psT[(mj * NB + i) % 2][:, 0:len(bl) * P].rearrange("p (k t) -> p k t", t=P),
                                                    PT[mg % 2][:, 0, dst[0], dst[1]], ALU.subtract).then_inc(tr_lo, 1)

            for i, (dst, src) in enumerate(wp_pieces):
                dve.wait_ge(wp_hi, i + 1)
                nc.vector.tensor_tensor(dst[:, 1], src, dst[:, 0], ALU.subtract).then_inc(wp_done, 1)
            for i in range(JP):
                job_low(0, 0, i, i, i % NJ)
            mid = halves(half)
            lo, hi = next(mid)
            with dve.Fori(lo, hi) as kv:
                for b in range(B):
                    half(kv * 2 + b, kv, b, False, False)
            for _ in mid:
                pass
            for t in range(TPB):
                h = 2 * kv_heads - 1
                output_add(h, 1, t, jobs_before(h) + JO + t, t % NJ)


def w13_split_pieces(W13, W13raw):
    return [(W13[:, :, :, i // 2, (i % 2) * 512:(i % 2) * 512 + 512], W13raw[:, :, i // 2, (i % 2) * 512:(i % 2) * 512 + 512])
            for i in range(8)]


def phase_route(nc, XT, gate_w, W13, W13raw, wts, p12, slots, over):
    with ExitStack() as st:
        named = phase_semaphores(nc, st)
        sem = lambda n: named(f"route_{n}")

        def sb(n, shape, dt):
            return st.enter_context(nc.sbuf_tensor(f"route_{n}", shape, dt))

        GW = sb("GW", [P, DC, E], F32)
        GWP = sb("GWP", [P, 2, DC, E], F16)
        lg = sb("lg", [P, NT, E], F32)
        top = sb("top", [P, NT, 8], F32)
        idx = sb("idx", [P, NT, 8], U32)
        idf = sb("idf", [P, NT, 8], F32)
        dlt = sb("dlt", [P, NT], F32)
        ex = sb("ex", [P, NT], F32)
        ex1 = sb("ex1", [P, NT], F32)
        expert = sb("expert", [P, E], F32)
        base = sb("base", [P, E], F32)
        onehot = sb("onehot", [P, 2, NT, E], F32)
        picks = sb("picks", [P, NT, E], F16)
        before = sb("before", [P, NT + 1, E], F16)
        part = sb("part", [P, 2, NT, E], F32)
        rank = sb("rank", [P, NT, E], F32)
        slotf = sb("slotf", [P, 2, NT], F32)
        counts = sb("counts", [P, 1], F32)
        zero = sb("zero", [P, P], F32)
        earlier = sb("earlier", [P, P], F32)
        earlier16 = sb("earlier16", [P, P], F16)
        ones16 = sb("ones16", [P, P], F16)
        psL = st.enter_context(nc.psum_tensor("route_psL", [P, 512], F32))
        psR = st.enter_context(nc.psum_tensor("route_psR", [P, 512], F32))
        psC = st.enter_context(nc.psum_tensor("route_psC", [P, 512], F32))

        gw_in, gw_hi, gw_done, iota_done, zero_done, tri_done, mats_done = (
            sem("gw_in"), sem("gw_hi"), sem("gw_done"), sem("iota_done"), sem("zero_done"), sem("tri_done"), sem("mats_done"))
        logits_ready, dlt_done, ex_done, chain = sem("logits_ready"), sem("dlt_done"), sem("ex_done"), sem("chain")
        picks_done, rank_ready, w13_hi, w13_done = sem("picks_done"), sem("rank_ready"), sem("w13_hi"), sem("w13_done")
        pieces = w13_split_pieces(W13, W13raw)
        block = st.enter_context(nc.Block())

        @block.sync
        def _(sp):
            sp.dma_start(GW[:], gate_w.rearrange("(k p) e -> p k e", p=P)).then_inc(gw_in, 16)

        @block.gpsimd
        def _(pool):
            nc.gpsimd.iota(expert[:], pattern=[[1, E]], base=0, channel_multiplier=0,
                           allow_small_or_imprecise_dtypes=True).then_inc(iota_done, 1)
            nc.gpsimd.iota(base[:], pattern=[[CAP, E]], base=0, channel_multiplier=0,
                           allow_small_or_imprecise_dtypes=True).then_inc(iota_done, 1)
            nc.gpsimd.memset(zero[:], 0.0).then_inc(zero_done, 1)
            nc.gpsimd.memset(ones16[:], 1.0).then_inc(mats_done, 1)
            pool.wait_ge(zero_done, 1)
            nc.gpsimd.affine_select(out=earlier[:], in_=zero[:], compare_op=ALU.is_ge, fill=1.0, base=0,
                                    pattern=[[-1, P]], channel_multiplier=1).then_inc(tri_done, 1)
            pool.wait_ge(tri_done, 1)
            nc.gpsimd.tensor_copy(earlier16[:], earlier[:]).then_inc(mats_done, 1)

        @block.tensor
        def _(pe):
            pe.wait_ge(gw_done, 1)
            for i in range(NT):
                for q, (hx, hw) in enumerate(PAIRS):
                    for k in range(DC):
                        last = nc.tensor.matmul(psL[:, i * E:(i + 1) * E], XT[:, hx, k, i * P:(i + 1) * P], GWP[:, hw, k, :],
                                                start=(q + k == 0), stop=(q == 2 and k == DC - 1))
            last.then_inc(logits_ready, 1)
            pe.wait_ge(picks_done, 1)
            pe.wait_ge(mats_done, 2)
            nc.tensor.matmul(psR[:, 0:NT * E], earlier16[:], picks[:].rearrange("p t e -> p (t e)"), start=True, stop=False)
            nc.tensor.matmul(psR[:, 0:NT * E], ones16[:], before[:, 0:NT, :].rearrange("p t e -> p (t e)"),
                             start=False, stop=True)
            nc.tensor.matmul(psC[:, 0:E], ones16[:], before[:, NT, :], start=True, stop=True).then_inc(rank_ready, 1)

        @block.scalar
        def _(act):
            for dst, src in pieces:
                nc.scalar.copy(dst[:, 0], src).then_inc(w13_hi, 1)
            act.wait_ge(dlt_done, 1)
            nc.scalar.activation(ex[:], dlt[:], ACT.Exp).then_inc(ex_done, 1)

        @block.vector
        def _(dve):
            steps = [0]

            def chained(ins):
                steps[0] += 1
                ins.then_inc(chain, 1)
                dve.wait_ge(chain, steps[0])

            dve.wait_ge(gw_in, 16)
            nc.vector.tensor_copy(GWP[:, 0, :, :], GW[:]).then_inc(gw_hi, 1)
            dve.wait_ge(gw_hi, 1)
            nc.vector.tensor_tensor(GWP[:, 1, :, :], GW[:], GWP[:, 0, :, :], ALU.subtract).then_inc(gw_done, 1)
            dve.wait_ge(logits_ready, 1)
            chained(nc.vector.tensor_copy(lg[:].rearrange("p t e -> p (t e)"), psL[:, 0:NT * E]))
            for i in range(NT):
                last = nc.vector.max(top[:, i, :], lg[:, i, :])
            chained(last)
            for i in range(NT):
                last = nc.vector.max_index(idx[:, i, :], top[:, i, :], lg[:, i, :])
            chained(last)
            nc.vector.tensor_tensor(dlt[:], top[:, :, 1], top[:, :, 0], ALU.subtract).then_inc(dlt_done, 1)
            chained(nc.vector.tensor_copy(idf[:], idx[:]))
            dve.wait_ge(iota_done, 2)
            wide = [P, NT, E]
            for k in range(2):
                last = nc.vector.tensor_tensor(onehot[:, k], expert[:].unsqueeze(1).broadcast_to(wide),
                                               idf[:, :, k:k + 1].broadcast_to(wide), ALU.is_equal)
            chained(last)
            chained(nc.vector.tensor_tensor(picks[:], onehot[:, 0], onehot[:, 1], ALU.add))
            chained(nc.vector.memset(before[:, 0, :], 0.0))
            for i in range(NT):
                chained(nc.vector.tensor_tensor(before[:, i + 1, :], before[:, i, :], picks[:, i, :], ALU.add))
            nc.vector.tensor_copy(counts[:], expert[:, 0:1]).then_inc(picks_done, 1)
            dve.wait_ge(ex_done, 1)
            chained(nc.vector.tensor_scalar(ex1[:], ex[:], 1.0, None, ALU.add))
            chained(nc.vector.reciprocal(p12[:, 0, :], ex1[:]))
            chained(nc.vector.tensor_tensor(p12[:, 1, :], ex[:], p12[:, 0, :], ALU.mult))
            for k in range(2):
                last = nc.vector.tensor_tensor(part[:, k], onehot[:, k], p12[:, k, :].unsqueeze(2).broadcast_to(wide), ALU.mult)
            chained(last)
            chained(nc.vector.tensor_tensor(wts[:], part[:, 0], part[:, 1], ALU.add))
            dve.wait_ge(rank_ready, 1)
            chained(nc.vector.tensor_tensor(rank[:], psR[:, 0:NT * E].rearrange("p (t e) -> p t e", e=E),
                                            base[:].unsqueeze(1).broadcast_to(wide), ALU.add))
            for k in range(2):
                last = nc.vector.tensor_tensor(part[:, k], onehot[:, k], rank[:], ALU.mult)
            chained(last)
            chained(nc.vector.tensor_reduce(slotf[:], part[:], AX_X, ALU.add))
            chained(nc.vector.tensor_copy(slots[:], slotf[:]))
            chained(nc.vector.tensor_reduce(counts[:], psC[:, 0:E], AX_X, ALU.max))
            chained(nc.vector.tensor_scalar(over[:], counts[:], float(CAP), None, ALU.is_gt))
            for i, (dst, src) in enumerate(pieces):
                dve.wait_ge(w13_hi, i + 1)
                nc.vector.tensor_tensor(dst[:, 1], src, dst[:, 0], ALU.subtract).then_inc(w13_done, 1)


def phase_moe_routed(nc, X, XT, XW, scratch, XG, YG, w1, w3, w2, W13raw, W13, W2raw, W2, p12, slots):
    with ExitStack() as st:
        named = phase_semaphores(nc, st)
        sem = lambda n: named(f"rmoe_{n}")

        def sb(n, shape, dt):
            return st.enter_context(nc.sbuf_tensor(f"rmoe_{n}", shape, dt))

        def pb(n):
            return st.enter_context(nc.psum_tensor(f"rmoe_{n}", [P, 512], F32))

        XR = scratch[:, 0:CTL, :]
        YR = scratch[:, CTL:2 * CTL, :]
        XGT = sb("XGT", [P, 2, DC, CAP], F16)
        SG = [sb(f"SG{i}", [P, CAP], F32) for i in range(2)]
        HF = [sb(f"HF{i}", [P, CAP], F32) for i in range(2)]
        HT = sb("HT", [P, 2, FC, CAP], F16)
        ident = sb("ident", [P, P], F32)
        psG = [pb(f"psG{i}") for i in range(2)]
        psU = [pb(f"psU{i}") for i in range(2)]
        psY = [pb(f"psY{i}") for i in range(2)]
        psT = [pb(f"psT{i}") for i in range(2)]
        Y1, Y2 = XW, XT[:].rearrange("p l k t -> p (l k t)").bitcast(F32).rearrange("p (t d) -> p t d", d=D)

        ident_zero, ident_done = sem("ident_zero"), sem("ident_done")
        scattered, x_in = sem("scattered"), sem("x_in")
        w13_in, w2_in, w13_hi, w13_done, w2_hi, w2_done = (
            sem("w13_in"), sem("w2_in"), sem("w13_hi"), sem("w13_done"), sem("w2_hi"), sem("w2_done"))
        tr_ready, tr_hi, tr_lo = sem("tr_ready"), sem("tr_hi"), sem("tr_lo")
        up_ready, silu_done, h_done, h_hi, h_lo = (
            sem("up_ready"), sem("silu_done"), sem("h_done"), sem("h_hi"), sem("h_lo"))
        down_ready, y_copied = sem("down_ready"), sem("y_copied")
        y_stored = [sem(f"y_stored{r}") for r in range(CTL)]
        gathered = [sem(f"gathered{t}") for t in range(NT)]
        combined = sem("combined")
        w13_pieces = w13_split_pieces(W13, W13raw)
        w2_pieces = [(W2[:, :, i, :], W2raw[:, i, :]) for i in range(FC)]
        xg_v = XG.rearrange("(e r p) d -> e p r d", r=CTL, p=P)
        yg_v = YG.rearrange("(e r p) d -> e r p d", r=CTL, p=P)
        block = st.enter_context(nc.Block())

        def over_experts(eng, emit):
            emit(0, True, False)
            with eng.Fori(1, E - 1) as e:
                emit(e, False, False)
            emit(E - 1, False, True)

        @block.sync
        def _(sp):
            def load_rows(e):
                wait_from(sp, tr_ready, DC * e)
                sp.dma_start(XR, xg_v[bass.ds(e, 1)].rearrange("o p r d -> p (o r) d")).then_inc(x_in, 16)

            sp.wait_ge(scattered, 16 * 2 * NT)
            load_rows(0)

            def step(e, first, last):
                if not last:
                    load_rows(e + 1)
                    wait_from(sp, w13_done, 8 * e)
                    for i, w in enumerate((w1, w3)):
                        sp.dma_start(W13raw[:, i, :, :], w[bass.ds(e + 1, 1)].rearrange("o (k p) f -> p (o k) f", p=P)).then_inc(w13_in, 16)
                    sp.wait_ge(w2_done, FC * (e + 1))
                    sp.dma_start(W2raw[:], w2[bass.ds(e + 1, 1)].rearrange("o (k p) d -> p (o k) d", p=P)).then_inc(w2_in, 16)
                for r in range(CTL):
                    sp.wait_ge(y_copied, CTL * e + r + 1)
                    sp.dma_start(yg_v[bass.ds(e, 1), r].rearrange("o p d -> p (o d)"), YR[:, r, :]).then_inc(y_stored[r], 16)

            over_experts(sp, step)
            for r in range(CTL):
                sp.wait_ge(y_stored[r], 16 * E)

        @block.gpsimd
        def _(pool):
            for t in range(NT):
                for k in range(2):
                    pool.indirect_dma_start(out=XG, out_offset=bass.IndirectOffsetOnAxis(ap=slots[:, k, t:t + 1], axis=0),
                                            in_=XW[:, t, :], in_offset=None).then_inc(scattered, 16)
            nc.gpsimd.memset(ident[:], 0.0).then_inc(ident_zero, 1)
            pool.wait_ge(ident_zero, 1)
            nc.gpsimd.affine_select(out=ident[:], in_=ident[:], compare_op=ALU.not_equal, fill=1.0, base=0,
                                    pattern=[[-1, P]], channel_multiplier=1).then_inc(ident_done, 1)
            for r in range(CTL):
                pool.wait_ge(y_stored[r], 16 * E)
            pool.wait_ge(scattered, 16 * 2 * NT)
            for t in range(NT):
                for k, dst in enumerate((Y1, Y2)):
                    pool.indirect_dma_start(out=dst[:, t, :], out_offset=None, in_=YG,
                                            in_offset=bass.IndirectOffsetOnAxis(ap=slots[:, k, t:t + 1], axis=0)
                                            ).then_inc(gathered[t], 16)

        @block.tensor
        def _(pe):
            def transposes(e):
                pe.wait_ge(x_in, 16 * (e + 1))
                for k in range(DC):
                    wait_from(pe, tr_lo, DC * e + k - 1)
                    for r in range(CTL):
                        last = nc.tensor.transpose(psT[k % 2][:, r * P:(r + 1) * P], XR[:, r, k * P:(k + 1) * P], ident[:])
                    last.then_inc(tr_ready, 1)

            def step(e, first, last_e):
                if not first:
                    pe.wait_ge(w13_done, 8 * e)
                pe.wait_ge(tr_lo, DC * (e + 1))
                for f in range(FC):
                    n = e * FC + f
                    wait_from(pe, h_done, n - 1)
                    for w, bank in ((0, psG), (1, psU)):
                        for i, (hw, hx) in enumerate(PAIRS):
                            for k in range(DC):
                                last = nc.tensor.matmul(bank[f % 2][:, 0:CAP], W13[:, hw, w, k, f * P:(f + 1) * P],
                                                        XGT[:, hx, k, :], start=(i + k == 0),
                                                        stop=(i == 2 and k == DC - 1))
                    last.then_inc(up_ready, 1)
                if not last_e:
                    transposes(e + 1)
                pe.wait_ge(w2_done, (e + 1) * FC)
                pe.wait_ge(h_lo, (e + 1) * FC)
                for r in range(CTL):
                    y = r % 2
                    wait_from(pe, y_copied, e * CTL + r - 1 if r else e * CTL)
                    for i, (hh, hw) in enumerate(PAIRS):
                        for k in range(FC):
                            last = nc.tensor.matmul(psY[y][:, :], HT[:, hh, k, r * P:(r + 1) * P], W2[:, hw, k, :],
                                                    start=(i + k == 0), stop=(i == 2 and k == FC - 1))
                    last.then_inc(down_ready, 1)

            pe.wait_ge(ident_done, 1)
            transposes(0)
            over_experts(pe, step)

        @block.scalar
        def _(act):
            def rows_high(e):
                for k in range(DC):
                    act.wait_ge(tr_ready, DC * e + k + 1)
                    if k == 0:
                        wait_from(act, up_ready, FC * e)
                    nc.scalar.copy(XGT[:, 0, k, :], psT[k % 2][:, 0:CAP]).then_inc(tr_hi, 1)

            def step(e, first, last):
                wait_from(act, w2_in, 16 * e)
                wait_from(act, down_ready, CTL * e)
                for f in range(FC):
                    n = e * FC + f
                    act.wait_ge(up_ready, n + 1)
                    nc.scalar.activation(SG[f % 2][:], psG[f % 2][:, 0:CAP], ACT.Silu).then_inc(silu_done, 1)
                    dst, src = w2_pieces[f]
                    nc.scalar.copy(dst[:, 0], src).then_inc(w2_hi, 1)
                    act.wait_ge(h_done, n + 1)
                    nc.scalar.copy(HT[:, 0, f, :], HF[f % 2][:]).then_inc(h_hi, 1)
                if not last:
                    rows_high(e + 1)
                    act.wait_ge(w13_in, 32 * (e + 1))
                    for dst, src in w13_pieces:
                        nc.scalar.copy(dst[:, 0], src).then_inc(w13_hi, 1)

            rows_high(0)
            over_experts(act, step)

        @block.vector
        def _(dve):
            def rows_low(e):
                for k in range(DC):
                    dve.wait_ge(tr_hi, DC * e + k + 1)
                    nc.vector.tensor_tensor(XGT[:, 1, k, :], psT[k % 2][:, 0:CAP], XGT[:, 0, k, :], ALU.subtract).then_inc(tr_lo, 1)

            def step(e, first, last):
                for f in range(FC):
                    n = e * FC + f
                    dve.wait_ge(silu_done, n + 1)
                    wait_from(dve, h_lo, n - 1)
                    nc.vector.tensor_tensor(HF[f % 2][:], psU[f % 2][:, 0:CAP], SG[f % 2][:], ALU.mult).then_inc(h_done, 1)
                    dst, src = w2_pieces[f]
                    dve.wait_ge(w2_hi, n + 1)
                    nc.vector.tensor_tensor(dst[:, 1], src, dst[:, 0], ALU.subtract).then_inc(w2_done, 1)
                    dve.wait_ge(h_hi, n + 1)
                    nc.vector.tensor_tensor(HT[:, 1, f, :], HF[f % 2][:], HT[:, 0, f, :], ALU.subtract).then_inc(h_lo, 1)
                if not last:
                    rows_low(e + 1)
                for r in range(CTL):
                    if not last:
                        for i in range(3 * r, min(3 * r + 3, 8)):
                            dst, src = w13_pieces[i]
                            dve.wait_ge(w13_hi, 8 * e + i + 1)
                            nc.vector.tensor_tensor(dst[:, 1], src, dst[:, 0], ALU.subtract).then_inc(w13_done, 1)
                    dve.wait_ge(down_ready, CTL * e + r + 1)
                    wait_from(dve, y_stored[r], 16 * e)
                    nc.vector.tensor_copy(YR[:, r, :], psY[r % 2][:, :]).then_inc(y_copied, 1)

            rows_low(0)
            over_experts(dve, step)
            for t in range(NT):
                dve.wait_ge(gathered[t], 32)
                nc.vector.scalar_tensor_tensor(out=X[:, t, :], in0=Y1[:, t, :], scalar=p12[:, 0, t:t + 1],
                                               in1=X[:, t, :], op0=ALU.mult, op1=ALU.add).then_inc(combined, 1)
                dve.wait_ge(combined, 2 * t + 1)
                nc.vector.scalar_tensor_tensor(out=X[:, t, :], in0=Y2[:, t, :], scalar=p12[:, 1, t:t + 1],
                                               in1=X[:, t, :], op0=ALU.mult, op1=ALU.add).then_inc(combined, 1)


def phase_moe_dense(nc, X, XT, wts, w1, w3, w2, W13raw, W13, W2raw, W2, scratch):
    with ExitStack() as st:
        sem = phase_semaphores(nc, st)

        def sb(n, shape, dt):
            return st.enter_context(nc.sbuf_tensor(f"moe_{n}", shape, dt))

        def pb(n, shape):
            return st.enter_context(nc.psum_tensor(f"moe_{n}", shape, F32))

        SG = [sb(f"SG{i}", [P, S], F32) for i in range(2)]
        HF = [sb(f"HF{i}", [P, S], F32) for i in range(4)]
        HT = scratch[:].rearrange("p l t d -> p (l t d)").bitcast(F16).rearrange("p (l f t) -> p l f t", l=2, f=FC)
        psG = [pb(f"psG{i}", [P, 512]) for i in range(2)]
        psU = [pb(f"psU{i}", [P, 512]) for i in range(2)]
        psY = [pb(f"psY{i}", [P, 512]) for i in range(2)]

        s = lambda n: sem(f"moe_{n}")
        pool_passed = s("pool_passed")
        w13_in, w2_in = s("w13_in"), s("w2_in")
        w13_hi, w13_done, w2_hi, w2_done = s("w13_hi"), s("w13_done"), s("w2_hi"), s("w2_done")
        up_ready, silu_done, h_done, h_hi, h_split = s("up_ready"), s("silu_done"), s("h_done"), s("h_hi"), s("h_split")
        down_ready, added = s("down_ready"), s("added")
        UP = B * FC
        block = st.enter_context(nc.Block())

        def over_experts(eng, emit):
            emit(0, True, False)
            with eng.Fori(1, E - 1) as e:
                emit(e, False, False)
            emit(E - 1, False, True)

        @block.sync
        def _(sp):
            def load(e):
                wait_from(sp, w13_done, e * 8)
                for i, w in enumerate((w1, w3)):
                    sp.dma_start(W13raw[:, i, :, :], w[bass.ds(e, 1)].rearrange("o (k p) f -> p (o k) f", p=P)).then_inc(w13_in, 16)
                wait_from(sp, w2_done, e * 8)
                sp.dma_start(W2raw[:], w2[bass.ds(e, 1)].rearrange("o (k p) d -> p (o k) d", p=P)).then_inc(w2_in, 16)

            load(0)
            with sp.Fori(1, E) as e:
                load(e)

        @block.gpsimd
        def _(pool):
            def split_w13(e, i):
                at = (i // 2, slice((i % 2) * 512, (i % 2) * 512 + 512))
                stand_apart(pool, pool_passed)
                nc.gpsimd.tensor_copy(W13[:, 0, :, at[0], at[1]], W13raw[:, :, at[0], at[1]]).then_inc(w13_hi, 1)
                pool.wait_ge(w13_hi, e * 8 + i + 1)
                nc.gpsimd.tensor_tensor(W13[:, 1, :, at[0], at[1]], W13raw[:, :, at[0], at[1]],
                                        W13[:, 0, :, at[0], at[1]], ALU.subtract).then_inc(w13_done, 1)

            def split_w2(e, i):
                stand_apart(pool, pool_passed)
                nc.gpsimd.tensor_copy(W2[:, 0, i, :], W2raw[:, i, :]).then_inc(w2_hi, 1)
                pool.wait_ge(w2_hi, e * 8 + i + 1)
                nc.gpsimd.tensor_tensor(W2[:, 1, i, :], W2raw[:, i, :], W2[:, 0, i, :], ALU.subtract).then_inc(w2_done, 1)

            def expert_steps(e, first, last):
                for q in range(UP):
                    b, f = q // FC, q % FC
                    if q == 0:
                        pool.wait_ge(w2_in, 16 * (e + 1))
                        wait_from(pool, down_ready, e * NT)
                    if q < 8:
                        split_w2(e, q)
                    n = e * UP + q
                    pool.wait_ge(h_done, n + 1)
                    stand_apart(pool, pool_passed)
                    nc.gpsimd.tensor_copy(HT[:, 0, f, b * S:(b + 1) * S], HF[q % 4][:]).then_inc(h_hi, 1)
                    pool.wait_ge(h_hi, n + 1)
                    nc.gpsimd.tensor_tensor(HT[:, 1, f, b * S:(b + 1) * S], HF[q % 4][:], HT[:, 0, f, b * S:(b + 1) * S],
                                            ALU.subtract).then_inc(h_split, 1)
                if not last:
                    pool.wait_ge(w13_in, 32 * (e + 2))
                    pool.wait_ge(up_ready, (e + 1) * UP)
                    for i in range(8):
                        split_w13(e + 1, i)

            pool.wait_ge(w13_in, 32)
            for i in range(8):
                split_w13(0, i)
            over_experts(pool, expert_steps)

        @block.tensor
        def _(pe):
            def expert_steps(e, first, last_e):
                pe.wait_ge(w13_done, (e + 1) * 8)
                for q in range(UP):
                    n = e * UP + q
                    b, f = q // FC, q % FC
                    wait_from(pe, h_done, n - 1)
                    for w, bank in ((0, psG), (1, psU)):
                        for i, (hw, hx) in enumerate(PAIRS):
                            for k in range(DC):
                                last = nc.tensor.matmul(bank[q % 2][:, :], W13[:, hw, w, k, f * P:(f + 1) * P],
                                                        XT[:, hx, k, b * S:(b + 1) * S], start=(i + k == 0),
                                                        stop=(i == 2 and k == DC - 1))
                    last.then_inc(up_ready, 1)
                pe.wait_ge(w2_done, (e + 1) * 8)
                for t in range(NT):
                    if t % TPB == 0:
                        pe.wait_ge(h_split, e * UP + (t // TPB + 1) * FC)
                    wait_from(pe, added, e * NT + t - 1)
                    for i, (hh, hw) in enumerate(PAIRS):
                        for k in range(FC):
                            last = nc.tensor.matmul(psY[t % 2][:, :], HT[:, hh, k, t * P:(t + 1) * P], W2[:, hw, k, :],
                                                    start=(i + k == 0), stop=(i == 2 and k == FC - 1))
                    last.then_inc(down_ready, 1)

            over_experts(pe, expert_steps)

        @block.scalar
        def _(act):
            def expert_steps(e, first, last):
                for q in range(UP):
                    n = e * UP + q
                    act.wait_ge(up_ready, n + 1)
                    wait_from(act, h_done, n - 1)
                    nc.scalar.activation(SG[q % 2][:], psG[q % 2][:, :], ACT.Silu).then_inc(silu_done, 1)

            over_experts(act, expert_steps)

        @block.vector
        def _(dve):
            def expert_steps(e, first, last):
                for q in range(UP):
                    n = e * UP + q
                    dve.wait_ge(silu_done, n + 1)
                    wait_from(dve, h_split, n - 3)
                    nc.vector.tensor_tensor(HF[q % 4][:], psU[q % 2][:, :], SG[q % 2][:], ALU.mult).then_inc(h_done, 1)
                for t in range(NT):
                    dve.wait_ge(down_ready, e * NT + t + 1)
                    wait_from(dve, added, (e - 1) * NT + t + 1)
                    nc.vector.scalar_tensor_tensor(out=X[:, t, :], in0=psY[t % 2][:, :], scalar=wts[:, t, bass.ds(e, 1)],
                                                   in1=X[:, t, :], op0=ALU.mult, op1=ALU.add).then_inc(added, 1)

            over_experts(dve, expert_steps)


def decoder_layer(nc, x, ctxt, mask, W_in, W_out, log_A, W_dt, b_dt, xWq, xWk, xWv, xWo, norm1_w, norm2_w, wq, wk, wv, wo,
                  gate_w, w1, w3, w2, rope_in, XG, YG, out):
    with ExitStack() as st:
        def sb(name, shape, dt):
            return st.enter_context(nc.sbuf_tensor(name, shape, dt))

        X = sb("X", [P, NT, D], F32)
        XT = sb("XT", [P, 2, DC, T], F16)
        identF = sb("identF", [P, P], F32)
        causal = sb("causal", [P, S], F32)
        flag = sb("flag", [P, B], F32)
        ropeC = sb("ropeC", [P, S], F32)
        ropeS = sb("ropeS", [P, S], F32)

        with ExitStack() as cross:
            CT = cross.enter_context(nc.sbuf_tensor("CT", [P, 2, DCTX // P, B * S2], F16))
            maskb = cross.enter_context(nc.sbuf_tensor("maskb", [P, B, S2], F32))
            phase_ssm(nc, X, XT, CT, XG, x, ctxt, mask, W_in, W_out, log_A, W_dt, b_dt,
                      (identF, causal, maskb, flag, ropeC, ropeS), rope_in)
            attention(nc, "xa", X, XT, CT, identF, xWq, xWk, xWv, xWo, 8, 2, S2,
                      lambda b, t: maskb[:, b, :], flag, None)
        rows = sb("rows", [P, 2, NT, D], F32)
        XW = rows[:, 0]
        X2 = rows[:, 1]
        phase_norm(nc, "n2", X, identF, XT=XT, norm_w=norm1_w, keep=X2)
        attention(nc, "sa", X, XT, XT, identF, wq, wk, wv, wo, 4, 4, S,
                  lambda b, t: causal[:, S - (t + 1) * P:S], None, (ropeC, ropeS))
        W13raw = sb("W13raw", [P, 2, DC, F], F32)
        W13 = sb("W13", [P, 2, 2, DC, F], F16)
        W2raw = sb("W2raw", [P, FC, D], F32)
        W2 = sb("W2", [P, 2, FC, D], F16)
        wts = sb("wts", [P, NT, E], F32)
        p12 = sb("p12", [P, 2, NT], F32)
        slots = sb("slots", [P, 2, NT], U32)
        over = sb("over", [P, 1], I32)
        phase_norm(nc, "n3", X, identF, XT=XT, norm_w=norm2_w, layer=False, add=X2, rows=XW,
                   fetch=[(W13raw[:, 0], w1[0].rearrange("(k p) f -> p k f", p=P)),
                          (W13raw[:, 1], w3[0].rearrange("(k p) f -> p k f", p=P)),
                          (W2raw[:], w2[0].rearrange("(k p) d -> p k d", p=P))])
        phase_route(nc, XT, gate_w, W13, W13raw, wts, p12, slots, over)
        overfull = nc.values_load(over[0:1, 0:1], min_val=0, max_val=1)
        with nc.If(overfull < 1):
            phase_moe_routed(nc, X, XT, XW, X2, XG, YG, w1, w3, w2, W13raw, W13, W2raw, W2, p12, slots)
        with nc.Else():
            phase_moe_dense(nc, X, XT, wts, w1, w3, w2, W13raw, W13, W2raw, W2, rows)
        phase_norm(nc, "n4", X, identF, out=out)


def rope_tables():
    inv = (1.0 / np.float32(1e6) ** (np.arange(0, HD, 2, dtype=np.float32) / np.float32(HD))).astype(np.float32)
    ang = inv[:, None] * np.arange(S, dtype=np.float32)[None, :]
    c, s = np.cos(ang).astype(np.float32), np.sin(ang).astype(np.float32)
    return np.stack([np.concatenate([c, c]), np.concatenate([s, -s])])


_INS = ['x', 'ctx_1024', 'mask_BxS2_bf1', 'L0_attn_W_in', 'L0_attn_W_out', 'L0_attn_log_A', 'L0_attn_W_dt', 'L0_attn_b_dt',
        'L0_xattn_Wq', 'L0_xattn_Wk', 'L0_xattn_Wv', 'L0_xattn_Wo', 'L0_ffn_norm1_w', 'L0_ffn_norm2_w', 'L0_ffn_wq',
        'L0_ffn_wk', 'L0_ffn_wv', 'L0_ffn_wo', 'L0_ffn_gate_w', 'L0_ffn_w1', 'L0_ffn_w3', 'L0_ffn_w2']


def kernel(**inputs):
    import numpy as _np
    import concourse.bacc as _bacc
    from concourse import mybir as _mybir
    from concourse.bass_utils import run_bass_kernel_spmd as _run

    nc = _bacc.Bacc("TRN2", target_bir_lowering=False, num_devices=1)
    arrays, args = {}, []
    for name in _INS:
        a = _np.ascontiguousarray(inputs[name])
        arrays[f"in_{name}_dram"] = a
        args.append(nc.dram_tensor(f"in_{name}_dram", a.shape, _mybir.dt.from_np(a.dtype), kind="ExternalInput").ap())
    arrays["rope_dram"] = rope_tables()
    args.append(nc.dram_tensor("rope_dram", (2, HD, S), F32, kind="ExternalInput").ap())
    for name in ("expert_rows_dram", "expert_out_dram"):
        args.append(nc.dram_tensor(name, (E * CAP, D), F32).ap())
    args.append(nc.dram_tensor("out_0_dram", (B, S, D), F32, kind="ExternalOutput").ap())
    decoder_layer(nc, *args)
    r = _run(nc, [arrays], core_ids=[0])
    return r.results[0]["out_0_dram"]
```

```python
from contextlib import ExitStack

import concourse.bass as bass
import numpy as np
from concourse import mybir

F32 = mybir.dt.float32
F16 = mybir.dt.float16
U8 = mybir.dt.uint8
U32 = mybir.dt.uint32
I32 = mybir.dt.int32
ALU = mybir.AluOpType
ACT = mybir.ActivationFunctionType
AX_X = mybir.AxisListType.X

P = 128
B, S, D = 2, 512, 512
T = B * S
NT = T // P
TPB = S // P
DC = D // P
S2, DCTX = 1024, 256
HD = 128
EPS = 1e-5
NEG = -1e30
PSCALE = 1024.0
SCORE_SCALE = float(1.0 / np.sqrt(HD))
E, F = 8, 1024
FC = F // P
CAP = 352
CTL = -(-CAP // P)
PAIRS = ((0, 0), (0, 1), (1, 0))


def wait_from(eng, sem, count):
    if isinstance(count, int) and count <= 0:
        return
    eng.wait_ge(sem, count)


def phase_semaphores(nc, phase):
    held = []

    def end():
        nc.clear_and_free_semaphores(held)
        nc.all_engine_barrier()

    phase.callback(end)

    def sem(name):
        held.append(nc.alloc_semaphore(name=name))
        return held[-1]

    return sem


def stand_apart(eng, passed):
    eng.sem_inc(passed, 1)


def split_banks(nc, sem, jobs, bank, ident, name):
    tr_done, hi_done, lo_done = sem(name + "_tr_done"), sem(name + "_hi_done"), sem(name + "_lo_done")
    nb = len(bank)

    def pe_job(pe, n):
        wait, blocks, _, _ = jobs[n]
        pe.wait_ge(*wait)
        if n >= nb:
            pe.wait_ge(lo_done, n - nb + 1)
        for src, off, rows, cols in blocks:
            last = nc.tensor.transpose(bank[n % nb][0:cols, off:off + rows], src, ident[0:rows, 0:rows])
        last.then_inc(tr_done, 1)

    def act_job(act, n):
        _, _, hi, _ = jobs[n]
        act.wait_ge(tr_done, n + 1)
        nc.scalar.copy(hi[0], hi[1](bank[n % nb])).then_inc(hi_done, 1)

    def dve_job(dve, n):
        _, _, hi, lo = jobs[n]
        dve.wait_ge(hi_done, n + 1)
        nc.vector.tensor_tensor(lo[0], lo[1](bank[n % nb]), hi[0], ALU.subtract).then_inc(lo_done, 1)

    return pe_job, act_job, dve_job, lo_done


def phase_ssm(nc, X, XT, CT, XG, x, ctxt, mask, W_in, W_out, log_A, W_dt, b_dt, consts, rope_in,
              fetch):
    identF, causal, maskb, flag, ropeC, ropeS = consts
    with ExitStack() as st:
        sem = phase_semaphores(nc, st)

        def sb(name, shape, dt):
            return st.enter_context(nc.sbuf_tensor(name, shape, dt))

        def pb(name, shape):
            return st.enter_context(nc.psum_tensor(name, shape, F32))

        win = sb("win", [P, DC, D], F32)
        wout = sb("wout", [P, DC, D], F32)
        wdt = sb("wdt", [32, D], F32)
        winT = sb("winT", [P, 2, DC, D], F16)
        woutT = sb("woutT", [P, 2, DC, D], F16)
        wdtT = sb("wdtT", [P, 2, DC, 32], F16)
        wdtR = sb("wdtR", [P, 2, DC, 32, 16], F16)
        ctx_in = [win[:].rearrange("p m (r d) -> p (m r) d", d=DCTX), sb("ctx_in1", [P, 8, DCTX], F32)[:]]
        xp = sb("xp", [P, DC, T], F32)
        XPT = sb("XPT", [P, 2, DC, T], F16)
        logA = sb("logA", [P, DC], F32)
        negA = sb("negA", [P, DC], F32)
        bdt = sb("bdt", [P, DC], F32)
        zb = sb("zb", [P, 2 * DC, S], F32)
        za = sb("za", [P, 2 * DC, S], F32)
        ys = sb("ys", [P, DC, S], F32)
        stats = sb("stats", [P, NT, 6], F32)
        mv = sb("mv", [P, NT, 2], F32)
        ve = sb("ve", [P, NT], F32)
        half = sb("half", [P, 1], F32)
        rstd = sb("rstd", [P, NT], F32)
        mask_in = sb("mask_in", [P, B * S2], U8)
        anyv = sb("anyv", [P, B], F32)
        zeros = sb("zeros", [P, D], F32)
        zeros_done, zeroed = sem("zeros_done"), sem("zeroed")
        bank = [pb(f"bank{i}", [P, 512]) for i in range(8)]

        x_in = [sem(f"x_in{b}") for b in range(B)]
        tables_in, mask_done, w_in, small_in = sem("tables_in"), sem("mask_done"), sem("w_in"), sem("small_in")
        c_in = [sem(f"c_in{b}") for b in range(B)]
        ident_zero, ident_done, causal_zero, causal_done = (sem("ident_zero"), sem("ident_done"),
                                                            sem("causal_zero"), sem("causal_done"))
        maskb_done, any_done, flag_done = sem("maskb_done"), sem("any_done"), sem("flag_done")
        rep_hi, rep_lo, expA_done, negA_done = sem("rep_hi"), sem("rep_lo"), sem("expA_done"), sem("negA_done")
        xp_ready, xp_hi, xp_f32, xp_lo = sem("xp_ready"), sem("xp_hi"), sem("xp_f32"), sem("xp_lo")
        z_ready, zb_done, za_abs, za_exp, za_ln = (sem("z_ready"), sem("zb_done"), sem("za_abs"),
                                                   sem("za_exp"), sem("za_ln"))
        dt_done, dec_done, scan_done, ys_hi, ys_lo = (sem("dt_done"), sem("dec_done"), sem("scan_done"),
                                                      sem("ys_hi"), sem("ys_lo"))
        y_ready, y_added = sem("y_ready"), sem("y_added")
        half_done, stats_done, mv_done, ve_done, rstd_done, ln_done = (
            sem("half_done"), sem("stats_done"), sem("mv_done"), sem("ve_done"), sem("rstd_done"), sem("ln_done"))

        YST = XT
        whole = lambda ap: ap[:, :]

        jobs = []
        as4 = lambda ap: ap[:, :].rearrange("p (k t) -> p k t", k=DC)

        def rows_job(i, wait):
            return (wait, [(X[:, i, k * P:(k + 1) * P], k * P, P, P) for k in range(DC)],
                    (XT[:, 0, :, i * P:(i + 1) * P], as4), (XT[:, 1, :, i * P:(i + 1) * P], as4))

        for k in range(DC):
            jobs.append(((w_in, 16), [(win[:, m, k * P:(k + 1) * P], m * P, P, P) for m in range(DC)],
                         (winT[:, 0, k, :], whole), (winT[:, 1, k, :], whole)))
        jobs += [rows_job(i, (x_in[0], 16)) for i in range(TPB)]
        as_dt = lambda ap: ap[:, 0:DC * 32].rearrange("p (k h) -> p k h", k=DC)
        jobs.append(((w_in, 32), [(wdt[:, k * P:(k + 1) * P], k * 32, 32, P) for k in range(DC)],
                     (wdtT[:, 0, :, :], as_dt), (wdtT[:, 1, :, :], as_dt)))
        first_jobs = len(jobs)
        jobs += [rows_job(i, (x_in[1], 16)) for i in range(TPB, NT)]
        late = []
        for k in range(DC):
            late.append(((w_in, 48), [(wout[:, m, k * P:(k + 1) * P], m * P, P, P) for m in range(DC)],
                         (woutT[:, 0, k, :], whole), (woutT[:, 1, k, :], whole)))
        for i in range(8):
            pair = lambda ap: ap[:, :].rearrange("p (c t) -> p c t", c=2)
            late.append(((c_in[i // 4], 16),
                         [(ctx_in[i // 4][:, 2 * (i % 4) + j, c * P:(c + 1) * P], c * 2 * P + j * P, P, P)
                          for c in range(2) for j in range(2)],
                         (CT[:, 0, :, i * 2 * P:(i + 1) * 2 * P], pair), (CT[:, 1, :, i * 2 * P:(i + 1) * 2 * P], pair)))
        norm_jobs = [rows_job(i, (ln_done, i + 1)) for i in range(NT)]
        tr_pe, tr_act, tr_dve, tr_lo = split_banks(nc, sem, jobs, bank[0:4], identF, "first")
        late_pe, late_act, late_dve, late_lo = split_banks(nc, sem, late, bank[0:2], identF, "late")
        norm_pe, norm_act, norm_dve, norm_lo = split_banks(nc, sem, norm_jobs, bank[4:8], identF, "norm")

        block = st.enter_context(nc.Block())

        @block.sync
        def _(sp):
            sp.dma_start(win[:], W_in.rearrange("(m p) d -> p m d", p=P)).then_inc(w_in, 16)
            sp.dma_start(X[:, 0:TPB, :], x[0].rearrange("(t p) d -> p t d", p=P)).then_inc(x_in[0], 16)
            sp.wait_ge(w_in, 16)
            sp.dma_start(wdt[:], W_dt).then_inc(w_in, 16)
            sp.dma_start(X[:, TPB:NT, :], x[1].rearrange("(t p) d -> p t d", p=P)).then_inc(x_in[1], 16)
            sp.wait_ge(w_in, 32)
            sp.dma_start(wout[:], W_out.rearrange("(m p) d -> p m d", p=P)).then_inc(w_in, 16)
            sp.dma_start(mask_in[:], mask.rearrange("b s -> (b s)").partition_broadcast(P)).then_inc(mask_done, 16)
            sp.dma_start(ropeC[:], rope_in[0]).then_inc(tables_in, 16)
            sp.dma_start(ropeS[:], rope_in[1]).then_inc(tables_in, 16)
            sp.wait_ge(tr_lo, DC)
            for b in range(B):
                sp.dma_start(ctx_in[b], ctxt[b].rearrange("(t p) d -> p t d", p=P)).then_inc(c_in[b], 16)
            for dst, src, arrived in fetch:
                sp.dma_start(dst, src).then_inc(arrived, 16)
            sp.wait_ge(zeros_done, 1)
            xg = XG.rearrange("(n p r) d -> n p r d", p=P, r=2)
            for i in range(E * CAP // (2 * P)):
                sp.dma_start(xg[i], zeros[:].unsqueeze(1).broadcast_to([P, 2, D])).then_inc(zeroed, 16)
            sp.wait_ge(zeroed, 16 * (E * CAP // (2 * P)))
            sp.wait_ge(tables_in, 32)

        @block.gpsimd
        def _(pool):
            nc.gpsimd.memset(identF[:], 0.0).then_inc(ident_zero, 1)
            pool.wait_ge(ident_zero, 1)
            nc.gpsimd.affine_select(out=identF[:], in_=identF[:], compare_op=ALU.not_equal, fill=1.0, base=0,
                                    pattern=[[-1, P]], channel_multiplier=1).then_inc(ident_done, 1)
            nc.gpsimd.memset(zeros[:], 0.0).then_inc(zeros_done, 1)
            nc.gpsimd.memset(causal[:], 0.0).then_inc(causal_zero, 1)
            pool.wait_ge(causal_zero, 1)
            nc.gpsimd.affine_select(out=causal[:, S - P:S], in_=causal[:, S - P:S], compare_op=ALU.is_ge, fill=NEG,
                                    base=0, pattern=[[-1, P]], channel_multiplier=1).then_inc(causal_done, 1)
            nc.gpsimd.memset(half[:], -0.5).then_inc(half_done, 1)
            pool.wait_ge(half_done, 1)
            for i in range(NT):
                pool.wait_ge(mv_done, i + 1)
                nc.gpsimd.tensor_scalar(ve[:, i:i + 1], mv[:, i, 1:2], EPS, 1.0, ALU.add, ALU.mult).then_inc(ve_done, 1)
                pool.wait_ge(ve_done, i + 1)
                nc.gpsimd.tensor_tensor(rstd[:, i:i + 1], ve[:, i:i + 1], half[:], ALU.pow).then_inc(rstd_done, 1)

        @block.tensor
        def _(pe):
            def project(b):
                for m in range(DC):
                    n = b * DC + m
                    if n >= 2:
                        pe.wait_ge(xp_lo, n - 1)
                    for i, (hw, hx) in enumerate(PAIRS):
                        for k in range(DC):
                            last = nc.tensor.matmul(bank[6 + n % 2][:, :], winT[:, hw, k, m * P:(m + 1) * P],
                                                    XT[:, hx, k, b * S:(b + 1) * S], start=(i + k == 0),
                                                    stop=(i == 2 and k == DC - 1))
                    last.then_inc(xp_ready, 1)

            def gates(b):
                pe.wait_ge(xp_lo, DC * (b + 1))
                for m in range(DC):
                    for i, (hw, hx) in enumerate(PAIRS):
                        for k in range(DC):
                            last = nc.tensor.matmul(bank[b * DC + m][:, :],
                                                    wdtR[:, hw, k, m * 8:(m + 1) * 8, :].rearrange("p h c -> p (h c)"),
                                                    XPT[:, hx, k, b * S:(b + 1) * S], start=(i + k == 0),
                                                    stop=(i == 2 and k == DC - 1))
                    last.then_inc(z_ready, 1)

            def output(i):
                pe.wait_ge(ys_lo, DC * (i // TPB + 1))
                if i >= 2:
                    pe.wait_ge(y_added, i - 1)
                for q, (hy, hw) in enumerate(PAIRS):
                    for k in range(DC):
                        last = nc.tensor.matmul(bank[2 + i % 2][:, :], YST[:, hy, k, i * P:(i + 1) * P],
                                                woutT[:, hw, k, :], start=(q + k == 0), stop=(q == 2 and k == DC - 1))
                last.then_inc(y_ready, 1)

            pe.wait_ge(ident_done, 1)
            for n in range(first_jobs):
                tr_pe(pe, n)
            pe.wait_ge(tr_lo, 2 * TPB)
            project(0)
            for n in range(first_jobs, len(jobs)):
                tr_pe(pe, n)
            pe.wait_ge(rep_hi, 1)
            pe.wait_ge(rep_lo, 1)
            pe.wait_ge(tr_lo, len(jobs))
            gates(0)
            project(1)
            gates(1)
            pe.wait_ge(za_abs, DC)
            pe.wait_ge(zb_done, DC)
            for n in range(DC):
                late_pe(pe, n)
            pe.wait_ge(late_lo, DC)
            for i in range(TPB):
                output(i)
            for n in range(DC, len(late)):
                late_pe(pe, n)
            pe.wait_ge(za_abs, 2 * DC)
            pe.wait_ge(zb_done, 2 * DC)
            for i in range(TPB, NT):
                output(i)
                norm_pe(pe, i - TPB)
            for n in range(TPB, NT):
                norm_pe(pe, n)

        @block.scalar
        def _(act):
            def split_xp(n):
                m, b = n % DC, n // DC
                act.wait_ge(xp_ready, n + 1)
                nc.scalar.copy(XPT[:, 0, m, b * S:(b + 1) * S], bank[6 + n % 2][:, :]).then_inc(xp_hi, 1)
                nc.scalar.copy(xp[:, m, b * S:(b + 1) * S], bank[6 + n % 2][:, :]).then_inc(xp_f32, 1)

            def gate_exp(n):
                act.wait_ge(z_ready, n + 1)
                act.wait_ge(zb_done, n + 1)
                nc.scalar.activation(za[:, n, :], bank[n][:, :], ACT.Abs, bias=bdt[:, n % DC:n % DC + 1]).then_inc(za_abs, 1)
                act.wait_ge(za_abs, n + 1)
                nc.scalar.activation(za[:, n, :], za[:, n, :], ACT.Exp, scale=-1.0).then_inc(za_exp, 1)

            def gate_ln(n):
                act.wait_ge(za_exp, n + 1)
                nc.scalar.activation(za[:, n, :], za[:, n, :], ACT.Ln, bias=1.0).then_inc(za_ln, 1)

            def decay(n):
                act.wait_ge(dt_done, n + 1)
                nc.scalar.activation(za[:, n, :], zb[:, n, :], ACT.Exp, scale=negA[:, n % DC:n % DC + 1]).then_inc(dec_done, 1)

            def scan_high(n):
                act.wait_ge(scan_done, n + 1)
                nc.scalar.copy(YST[:, 0, n % DC, (n // DC) * S:(n // DC + 1) * S], ys[:, n % DC, :]).then_inc(ys_hi, 1)

            act.dma_start(logA[:], log_A.rearrange("(m h) c -> (h c) m", m=DC), allow_slow_non_contiguous=True).then_inc(small_in, 16)
            for h in range(8):
                act.dma_start(bdt[h * 16:(h + 1) * 16, :],
                              b_dt.rearrange("(m h) -> h m", h=8)[h].partition_broadcast(16),
                              allow_slow_non_contiguous=True).then_inc(small_in, 16)
            for n in range(first_jobs):
                tr_act(act, n)
            act.wait_ge(tr_lo, first_jobs)
            nc.scalar.copy(wdtR[:, 0], wdtT[:, 0, :, :].unsqueeze(3).broadcast_to([P, DC, 32, 16])).then_inc(rep_hi, 1)
            for n in range(DC):
                split_xp(n)
            for n in range(first_jobs, len(jobs)):
                tr_act(act, n)
            act.wait_ge(small_in, 144)
            nc.scalar.activation(logA[:], logA[:], ACT.Exp).then_inc(expA_done, 1)
            act.wait_ge(negA_done, 1)
            for n in range(DC):
                gate_exp(n)
            for n in range(DC, DC + 2):
                split_xp(n)
            for n in range(DC):
                gate_ln(n)
            for n in range(DC + 2, 2 * DC):
                split_xp(n)
            for n in range(DC):
                decay(n)
            for n in range(DC):
                scan_high(n)
            for n in range(DC, 2 * DC):
                gate_exp(n)
            for n in range(DC):
                late_act(act, n)
            for n in range(DC, 2 * DC):
                gate_ln(n)
            for n in range(DC, 2 * DC):
                decay(n)
            for n in range(DC, 2 * DC):
                scan_high(n)
            for n in range(DC, len(late)):
                late_act(act, n)
            for n in range(NT):
                norm_act(act, n)

        @block.vector
        def _(dve):
            def xp_low(n):
                m, b = n % DC, n // DC
                dve.wait_ge(xp_hi, n + 1)
                dve.wait_ge(xp_f32, n + 1)
                nc.vector.tensor_tensor(XPT[:, 1, m, b * S:(b + 1) * S], xp[:, m, b * S:(b + 1) * S],
                                        XPT[:, 0, m, b * S:(b + 1) * S], ALU.subtract).then_inc(xp_lo, 1)

            def gate_max(n):
                dve.wait_ge(z_ready, n + 1)
                nc.vector.tensor_scalar(zb[:, n, :], bank[n][:, :], bdt[:, n % DC:n % DC + 1], 0.0, ALU.add,
                                        ALU.max).then_inc(zb_done, 1)

            def softplus(n):
                dve.wait_ge(zb_done, n + 1)
                dve.wait_ge(za_ln, n + 1)
                nc.vector.tensor_tensor(zb[:, n, :], zb[:, n, :], za[:, n, :], ALU.add).then_inc(dt_done, 1)

            def scan(n):
                m, b = n % DC, n // DC
                dve.wait_ge(dec_done, n + 1)
                if b:
                    dve.wait_ge(ys_hi, n - DC + 1)
                    dve.wait_ge(ys_lo, n - DC + 1)
                nc.vector.tensor_tensor_scan(ys[:, m, :], za[:, n, :], xp[:, m, b * S:(b + 1) * S], 0.0,
                                             ALU.mult, ALU.add).then_inc(scan_done, 1)

            def scan_low(n):
                m, b = n % DC, n // DC
                dve.wait_ge(ys_hi, n + 1)
                nc.vector.tensor_tensor(YST[:, 1, m, b * S:(b + 1) * S], ys[:, m, :],
                                        YST[:, 0, m, b * S:(b + 1) * S], ALU.subtract).then_inc(ys_lo, 1)

            def add(i):
                dve.wait_ge(y_ready, i + 1)
                nc.vector.tensor_tensor(X[:, i, :], bank[2 + i % 2][:, :], X[:, i, :], ALU.add).then_inc(y_added, 1)
                dve.wait_ge(y_added, i + 1)
                nc.vector.bn_stats(stats[:, i, :], X[:, i, :]).then_inc(stats_done, 1)
                dve.wait_ge(stats_done, i + 1)
                nc.vector.bn_aggr(mv[:, i, :], stats[:, i, :]).then_inc(mv_done, 1)

            def layer_norm(i):
                dve.wait_ge(rstd_done, i + 1)
                dve.wait_ge(mv_done, i + 1)
                nc.vector.tensor_scalar(X[:, i, :], X[:, i, :], mv[:, i, 0:1], rstd[:, i:i + 1], ALU.subtract,
                                        ALU.mult).then_inc(ln_done, 1)

            for n in range(first_jobs):
                tr_dve(dve, n)
            dve.wait_ge(tr_lo, first_jobs)
            nc.vector.tensor_copy(wdtR[:, 1], wdtT[:, 1, :, :].unsqueeze(3).broadcast_to([P, DC, 32, 16])).then_inc(rep_lo, 1)
            for n in range(DC):
                xp_low(n)
            for n in range(first_jobs, len(jobs)):
                tr_dve(dve, n)
            dve.wait_ge(expA_done, 1)
            nc.vector.tensor_scalar(negA[:], logA[:], -1.0, None, ALU.mult).then_inc(negA_done, 1)
            for n in range(DC):
                gate_max(n)
            dve.wait_ge(mask_done, 16)
            nc.vector.tensor_scalar(maskb[:].rearrange("p b s -> p (b s)"), mask_in[:], -1.0, -NEG, ALU.add,
                                    ALU.mult).then_inc(maskb_done, 1)
            for b in range(B):
                last = nc.vector.tensor_reduce(anyv[:, b:b + 1], mask_in[:, b * S2:(b + 1) * S2], AX_X, ALU.max)
            last.then_inc(any_done, 1)
            dve.wait_ge(any_done, 1)
            nc.vector.tensor_scalar(flag[:], anyv[:], PSCALE, None, ALU.mult).then_inc(flag_done, 1)
            for n in range(DC, DC + 2):
                xp_low(n)
            for n in range(DC):
                softplus(n)
            for n in range(DC + 2, 2 * DC):
                xp_low(n)
            for n in range(DC):
                scan(n)
            for n in range(DC):
                scan_low(n)
            for n in range(DC, 2 * DC):
                gate_max(n)
            for n in range(DC):
                late_dve(dve, n)
            for n in range(DC, 2 * DC):
                softplus(n)
            for n in range(DC, 2 * DC):
                scan(n)
            for n in range(DC, 2 * DC):
                scan_low(n)
            for i in range(TPB):
                add(i)
            for n in range(DC, len(late)):
                late_dve(dve, n)
            for i in range(TPB):
                layer_norm(i)
            for i in range(TPB, NT):
                add(i)
                if i > TPB:
                    layer_norm(i - 1)
                norm_dve(dve, i - TPB)
            layer_norm(NT - 1)
            for n in range(TPB, NT):
                norm_dve(dve, n)


def phase_norm(nc, name, X, identF, XT=None, norm_w=None, layer=True, out=None, keep=None, add=None,
               rows=None, fetch=()):
    with ExitStack() as st:
        sem = phase_semaphores(nc, st)

        def sb(n, shape, dt):
            return st.enter_context(nc.sbuf_tensor(f"{name}_{n}", shape, dt))

        stats = sb("stats", [P, NT, 6], F32)
        mv = sb("mv", [P, NT, 2], F32)
        ve = sb("ve", [P, NT], F32)
        half = sb("half", [P, 1], F32)
        rstd = sb("rstd", [P, NT], F32)
        sq = sb("sq", [P, 2, D], F32)
        ms = sb("ms", [P, NT], F32)
        me = sb("me", [P, NT], F32)
        rr = sb("rr", [P, NT], F32)
        wb = sb("wb", [P, D], F32)
        XR = 4 if rows is None else NT
        xw = sb("xw", [P, 4, D], F32) if rows is None else rows
        bank = [st.enter_context(nc.psum_tensor(f"{name}_bank{i}", [P, 512], F32)) for i in range(4)]

        s = lambda n: sem(f"{name}_{n}")
        half_done, w_in, stats_done, mv_done, ve_done, rstd_done, ln_done = (
            s("half_done"), s("w_in"), s("stats_done"), s("mv_done"), s("ve_done"), s("rstd_done"), s("ln_done"))
        ms_done, me_done, rr_done, xw_done, out_done = (
            s("ms_done"), s("me_done"), s("rr_done"), s("xw_done"), s("out_done"))
        rms = norm_w is not None
        jobs = []
        if XT is not None:
            for i in range(NT):
                src = xw[:, i % XR] if rms else X[:, i]
                as4 = lambda ap: ap[:, :].rearrange("p (k t) -> p k t", k=DC)
                jobs.append(((xw_done if rms else ln_done, i + 1),
                             [(src[:, k * P:(k + 1) * P], k * P, P, P) for k in range(DC)],
                             (XT[:, 0, :, i * P:(i + 1) * P], as4), (XT[:, 1, :, i * P:(i + 1) * P], as4)))
        tr_pe, tr_act, tr_dve, tr_lo = split_banks(nc, sem, jobs, bank, identF, name)

        block = st.enter_context(nc.Block())

        @block.sync
        def _(sp):
            if rms:
                sp.dma_start(wb[:], norm_w.partition_broadcast(P)).then_inc(w_in, 16)
                sp.wait_ge(w_in, 16)
            for dst, src, arrived in fetch:
                sp.dma_start(dst, src).then_inc(arrived, 16)
            if out is not None:
                for i in range(NT):
                    sp.wait_ge(ln_done, i + 1)
                    sp.dma_start(out[i // TPB, (i % TPB) * P:(i % TPB + 1) * P, :], X[:, i, :]).then_inc(out_done, 16)
                sp.wait_ge(out_done, 16 * NT)

        @block.gpsimd
        def _(pool):
            nc.gpsimd.memset(half[:], -0.5).then_inc(half_done, 1)
            pool.wait_ge(half_done, 1)
            for i in range(NT + 4):
                if layer and i < NT:
                    pool.wait_ge(mv_done, i + 1)
                    nc.gpsimd.tensor_scalar(ve[:, i:i + 1], mv[:, i, 1:2], EPS, 1.0, ALU.add, ALU.mult).then_inc(ve_done, 1)
                    pool.wait_ge(ve_done, i + 1)
                    nc.gpsimd.tensor_tensor(rstd[:, i:i + 1], ve[:, i:i + 1], half[:], ALU.pow).then_inc(rstd_done, 1)
                n = i - 3
                if rms and 0 <= n < NT:
                    pool.wait_ge(ms_done, n + 1)
                    nc.gpsimd.tensor_scalar(me[:, n:n + 1], ms[:, n:n + 1], 1.0 / D, EPS, ALU.mult, ALU.add).then_inc(me_done, 1)
                    pool.wait_ge(me_done, n + 1)
                    nc.gpsimd.tensor_tensor(rr[:, n:n + 1], me[:, n:n + 1], half[:], ALU.pow).then_inc(rr_done, 1)
                n = i - 4
                if 0 <= n < NT and keep is not None:
                    nc.gpsimd.tensor_scalar(keep[:, n, :], X[:, n, :], 1.0, 1.0, ALU.mult, ALU.mult)
                if 0 <= n < NT and add is not None:
                    pool.wait_ge(xw_done, n + 1)
                    nc.gpsimd.tensor_tensor(X[:, n, :], X[:, n, :], add[:, n, :], ALU.add)

        @block.tensor
        def _(pe):
            for n in range(len(jobs)):
                tr_pe(pe, n)

        @block.scalar
        def _(act):
            if rms:
                for i in range(NT):
                    if layer:
                        act.wait_ge(ln_done, i + 1)
                    if i >= 2:
                        act.wait_ge(ms_done, i - 1)
                    nc.scalar.activation(sq[:, i % 2, :], X[:, i, :], ACT.Square, accum_out=ms[:, i:i + 1]).then_inc(ms_done, 1)
                    if i >= 3:
                        tr_act(act, i - 3)
                for i in range(NT - 3, NT):
                    tr_act(act, i)
            else:
                for i in range(len(jobs)):
                    tr_act(act, i)

        @block.vector
        def _(dve):
            for i in range(NT + 6):
                if layer and i < NT:
                    nc.vector.bn_stats(stats[:, i, :], X[:, i, :]).then_inc(stats_done, 1)
                    dve.wait_ge(stats_done, i + 1)
                    nc.vector.bn_aggr(mv[:, i, :], stats[:, i, :]).then_inc(mv_done, 1)
                n = i - 2
                if layer and 0 <= n < NT:
                    dve.wait_ge(rstd_done, n + 1)
                    dve.wait_ge(mv_done, n + 1)
                    nc.vector.tensor_scalar(X[:, n, :], X[:, n, :], mv[:, n, 0:1], rstd[:, n:n + 1], ALU.subtract,
                                            ALU.mult).then_inc(ln_done, 1)
                n = i - 4
                if rms and 0 <= n < NT:
                    if n == 0:
                        dve.wait_ge(w_in, 16)
                    dve.wait_ge(rr_done, n + 1)
                    if layer:
                        dve.wait_ge(ln_done, n + 1)
                    if n >= XR:
                        dve.wait_ge(tr_lo, n - XR + 1)
                    nc.vector.scalar_tensor_tensor(out=xw[:, n % XR, :], in0=X[:, n, :], scalar=rr[:, n:n + 1], in1=wb[:],
                                                   op0=ALU.mult, op1=ALU.mult).then_inc(xw_done, 1)
                n = i - 6
                if 0 <= n < len(jobs):
                    tr_dve(dve, n)


def attention_weights(nc, st, name, groups, KC, Wq, Wk, Wv):
    WQ, WKV = DC * groups * HD, KC * HD
    WPraw = st.enter_context(nc.sbuf_tensor(f"{name}_WPraw", [P, WQ + 2 * WKV], F32))
    WP = st.enter_context(nc.sbuf_tensor(f"{name}_WP", [P, 2, WQ + 2 * WKV], F16))
    arrived = nc.alloc_semaphore(name=f"{name}_first_in")
    loads = [(dst, src, arrived) for dst, src in head_loads(WPraw, WQ, WKV, KC, groups, Wq, Wk, Wv, 0)]
    return (WPraw, WP, arrived), loads


def head_loads(WPraw, WQ, WKV, KC, groups, Wq, Wk, Wv, kv):
    return [(WPraw[:, 0:WQ].rearrange("p (k c) -> p k c", k=DC),
             Wq[:, bass.ds(kv * (groups * HD), groups * HD)].rearrange("(k p) c -> p k c", p=P)),
            (WPraw[:, WQ:WQ + WKV].rearrange("p (k c) -> p k c", k=KC),
             Wk[:, bass.ds(kv * HD, HD)].rearrange("(k p) c -> p k c", p=P)),
            (WPraw[:, WQ + WKV:].rearrange("p (k c) -> p k c", k=KC),
             Wv[:, bass.ds(kv * HD, HD)].rearrange("(k p) c -> p k c", p=P))]


def attention(nc, name, X, XT, KVT, identF, weights, Wq, Wk, Wv, Wo, kv_heads, groups, keys, mask_of, flag, rope):
    NS = groups * TPB
    NBLK = keys // P
    NB = -(-NBLK // 4)
    KC = KVT.shape[2]
    WQ, WKV = DC * groups * HD, KC * HD
    causal = rope is not None
    JP, JO = 6, TPB
    JT = JP + JO
    NJ = 3 if causal else 1
    DEPTH = 2 if causal else 2
    NPN = 2 if causal else 2
    TAIL = DEPTH + 2
    LAG = 1 if causal else 0
    if causal:
        proj = [("q", g) for g in range(groups)] + [("k", 0), ("v", 0)]
        slots = {0: ([("proj", 0)], []), 1: ([("proj", 1)], []), 2: ([("proj", 2)], []), 4: ([("proj", 3)], []),
                 5: ([("proj", 4)], []), 6: ([("proj", 5)], []), 8: ([("wo", 0)], []), 10: ([("wo", 1)], []),
                 12: ([("wo", 2)], []), 14: ([("wo", 3)], [])}
    else:
        proj = [("q", 0), ("q", 1), ("k", 0), ("k", 1), ("v", 0), ("v", 1)]
        slots = {0: ([("proj", 0)], []), 1: ([("proj", 1)], []), 2: ([("proj", 2)], []),
                 3: ([("proj", 3)], [("proj", 4)]), 4: ([("proj", 5)], []), 5: ([("wo", 0)], []),
                 6: ([("wo", 1)], []), 7: ([("wo", 2)], [("wo", 3)])}
    assert len(proj) == JP and (not LAG or NS - 1 not in slots)
    last_proj_slot = max(j for j, l in slots.items() if any(k == "proj" for k, _ in l[0] + l[1]))
    first_piece = last_proj_slot + 1

    def jobs_before(h):
        return JP if isinstance(h, int) and h == 0 else 2 * JP + JT * (h - 1)

    def projections_before(h):
        return jobs_before(h) if isinstance(h, int) and h <= 1 else jobs_before(h) - JO

    def slot_jobs(h, j, first, last, late=None):
        out, k = [], 0
        for jj in range(NS):
            for place, jobs in enumerate(slots.get(jj, ([], []))):
                for kind, i in jobs:
                    if kind == "wo" and first or kind == "proj" and last:
                        continue
                    if jj == j and late in (None, place):
                        out.append((kind, i, jobs_before(h) + k, k))
                    k += 1
        return out

    with ExitStack() as st:
        sem = phase_semaphores(nc, st)

        def sb(n, shape, dt):
            return st.enter_context(nc.sbuf_tensor(f"{name}_{n}", shape, dt))

        def pb(n, shape):
            return st.enter_context(nc.psum_tensor(f"{name}_{n}", shape, F32))

        WPraw, WP, first_in = weights
        WOraw = sb("WOraw", [P, groups, D], F32)
        WO = sb("WO", [P, 2, groups, D], F16)
        QT = [sb(f"QT{b}", [P, 2, groups, S], F16) for b in range(B)]
        KT = [sb(f"KT{b}", [P, 2, keys], F16) for b in range(B)]
        V = [sb(f"V{b}", [P, 2, NBLK, HD], F16) for b in range(B)]
        OT = [sb(f"OT{b}", [P, 2, groups, S], F16) for b in range(B)]
        SC = [sb(f"SC{i}", [P, keys], F32) for i in range(2)]
        PN = [sb(f"PN{i}", [P, keys], F32) for i in range(NPN)]
        PT = [sb(f"PT{i}", [P, 2, NBLK, S], F16) for i in range(2)]
        mn = sb("mn", [P, 4], F32)
        sm = sb("sm", [P, 4], F32)
        rc = sb("rc", [P, 4], F32)
        rA = [sb(f"rA{i}", [P, S if causal else 1], F32) for i in range(3)]
        rB = [sb(f"rB{i}", [P, S if causal else 1], F32) for i in range(3)]
        psS = [pb(f"psS{i}", [P, NB * 512]) for i in range(2)]
        psT = [pb(f"psT{i}", [P, 512]) for i in range(2)]
        psO = pb("psO", [P, 512])
        psJ = [pb(f"psJ{i}", [P, 512]) for i in range(NJ)]
        ring = psJ if causal else [psJ[0], psO]

        s = lambda n: sem(f"{name}_{n}")
        wp_in, wp_hi, wp_done = s("wp_in"), s("wp_hi"), s("wp_done")
        wo_in, wo_hi, wo_done = s("wo_in"), s("wo_hi"), s("wo_done")
        scores_ready, masked, exp_done, recip_done, norm_done = (
            s("scores_ready"), s("masked"), s("exp_done"), s("recip_done"), s("norm_done"))
        tr_ready, tr_hi, tr_lo = s("tr_ready"), s("tr_hi"), s("tr_lo")
        pv_ready, o_hi, o_lo = s("pv_ready"), s("o_hi"), s("o_lo")
        job_ready, job_hi, job_free = s("job_ready"), s("job_hi"), s("job_free")
        rope_added, rope_hi, rope_done = s("rope_added"), s("rope_hi"), s("rope_done")

        pool_passed, dve_passed = s("pool_passed"), s("dve_passed")
        wp_pieces = [(WP[:, :, c:c + 512], WPraw[:, c:c + 512]) for c in range(0, WQ + 2 * WKV, 512)]
        wo_pieces = [(WO[:, :, g, :], WOraw[:, g, :]) for g in range(groups)]
        NWP, NWO = len(wp_pieces), len(wo_pieces)

        def step_pieces(kv, b, j, last_kv):
            i = j - first_piece
            if b == 0 and not last_kv and 0 <= i < NWP:
                return "wp", i, (kv + 1) * NWP + i
            if b == 1 and j < NWO:
                return "wo", j, kv * NWO + j
            return None

        wq_v = WP[:, :, 0:WQ].rearrange("p l (k g c) -> p l k g c", k=DC, g=groups)
        wk_v = WP[:, :, WQ:WQ + WKV].rearrange("p l (k c) -> p l k c", k=KC)
        wv_v = WP[:, :, WQ + WKV:].rearrange("p l (k c) -> p l k c", k=KC)

        def width(t):
            return (t + 1) * P if causal else keys

        def blocks(t, i):
            return range(4 * i, min(4 * i + 4, width(t) // P))

        block = st.enter_context(nc.Block())

        def halves(emit):
            for b in range(B):
                emit(b, 0, b, b == 0, False)
            yield 1, kv_heads - 1
            for b in range(B):
                emit(2 * (kv_heads - 1) + b, kv_heads - 1, b, False, b == B - 1)

        @block.sync
        def _(sp):
            def load_wp(kv):
                sp.wait_ge(wp_done, kv * NWP)
                for dst, src in head_loads(WPraw, WQ, WKV, KC, groups, Wq, Wk, Wv, kv):
                    sp.dma_start(dst, src).then_inc(wp_in, 16)

            def load_wo(kv):
                wait_from(sp, wo_done, kv * NWO)
                sp.dma_start(WOraw[:], Wo[bass.ds(kv * (groups * HD), groups * HD), :].rearrange(
                    "(g p) d -> p g d", p=P)).then_inc(wo_in, 16)

            load_wo(0)
            with sp.Fori(1, kv_heads) as kv:
                load_wp(kv)
                load_wo(kv)

        @block.gpsimd
        def _(pool):
            def piece_low(what, i, n):
                (dst, src), hi_done, done = ((wp_pieces[i], wp_hi, wp_done) if what == "wp" else
                                             (wo_pieces[i], wo_hi, wo_done))
                pool.wait_ge(hi_done, n + 1)
                nc.gpsimd.tensor_tensor(dst[:, 1], src, dst[:, 0], ALU.subtract).then_inc(done, 1)

            def rope_sum(h, b, i, job):
                par = i % 3
                pool.wait_ge(job_free, job + 1)
                nc.gpsimd.tensor_tensor(rA[par][:], rA[par][:], rB[par][:], ALU.add).then_inc(rope_added, 1)

            def rope_low(h, b, i):
                r = (JP - 1) * h + i
                par = i % 3
                pool.wait_ge(rope_hi, r + 1)
                dst = QT[b][:, :, i, :] if proj[i][0] == "q" else KT[b][:, :, :]
                nc.gpsimd.tensor_tensor(dst[:, 1, :], rA[par][:], dst[:, 0, :], ALU.subtract).then_inc(rope_done, 1)

            def half(h, kv, b, first, last):
                for j in range(NS):
                    n = h * NS + j
                    turned = [(i, job) for kind, i, job, _ in slot_jobs(h, j - 2, first, last)
                              if causal and kind == "proj" and proj[i][0] != "v"]
                    for i, job in turned:
                        rope_sum(h + 1, 1 - b, i, job)
                    pool.wait_ge(recip_done, n + 1)
                    wait_from(pool, tr_ready, (n - NPN + 1) * NB)
                    w = width(j % TPB)
                    stand_apart(pool, pool_passed)
                    nc.gpsimd.tensor_scalar(PN[j % NPN][:, 0:w], SC[j % 2][:, 0:w], rc[:, j % 4:j % 4 + 1],
                                            PSCALE if flag is None else flag[:, b:b + 1], ALU.mult,
                                            ALU.mult).then_inc(norm_done, 1)
                    piece = step_pieces(kv, b, j, isinstance(kv, int) and kv == kv_heads - 1)
                    if piece:
                        piece_low(*piece)
                    for kind, i, job, _ in slot_jobs(h, j - 3, first, last):
                        if causal and kind == "proj" and proj[i][0] != "v":
                            rope_low(h + 1, 1 - b, i)

            if causal:
                for i in range(JP - 1):
                    rope_sum(0, 0, i, i)
                    rope_low(0, 0, i)
            mid = halves(half)
            lo, hi = next(mid)
            with pool.Fori(lo, hi) as kv:
                for b in range(B):
                    half(kv * 2 + b, kv, b, False, False)
            for _ in mid:
                pass

        @block.tensor
        def _(pe):
            def project(h, b, i, job, bank, back=NJ):
                kind, a = proj[i]
                wait_from(pe, job_free, job - back + 1)
                if kind == "q":
                    for q, (hw, hx) in enumerate(PAIRS):
                        for k in range(DC):
                            last = nc.tensor.matmul(bank[:, :], wq_v[:, hw, k, a, :], XT[:, hx, k, b * S:(b + 1) * S],
                                                    start=(q + k == 0), stop=(q == 2 and k == DC - 1))
                elif kind == "k":
                    for q, (hw, hx) in enumerate(PAIRS):
                        for k in range(KC):
                            last = nc.tensor.matmul(bank[:, :], wk_v[:, hw, k, :],
                                                    KVT[:, hx, k, b * keys + a * 512:b * keys + a * 512 + 512],
                                                    start=(q + k == 0), stop=(q == 2 and k == KC - 1))
                else:
                    for m in range(4):
                        at = b * keys + (4 * a + m) * P
                        for q, (hw, hx) in enumerate(PAIRS):
                            for k in range(KC):
                                last = nc.tensor.matmul(bank[:, m * P:(m + 1) * P], KVT[:, hx, k, at:at + P],
                                                        wv_v[:, hw, k, :], start=(q + k == 0),
                                                        stop=(q == 2 and k == KC - 1))
                last.then_inc(job_ready, 1)

            def output(h, b, t, job, bank, back=NJ):
                pe.wait_ge(o_lo, (h + 1) * groups)
                wait_from(pe, job_free, job - back + 1)
                for g in range(groups):
                    for q, (ho, hw) in enumerate(PAIRS):
                        last = nc.tensor.matmul(bank[:, :], OT[b][:, ho, g, t * P:(t + 1) * P], WO[:, hw, g, :],
                                                start=(g + q == 0), stop=(g == groups - 1 and q == 2))
                last.then_inc(job_ready, 1)

            def scores(n, b, g, t, j):
                wait_from(pe, masked, n - 1)
                w = width(t)
                for c in range(0, w, 512):
                    cw = min(512, w - c)
                    for q, (hq, hk) in enumerate(PAIRS):
                        last = nc.tensor.matmul(psS[j % 2][:, c:c + cw], QT[b][:, hq, g, t * P:(t + 1) * P],
                                                KT[b][:, hk, c:c + cw], start=(q == 0), stop=(q == 2))
                last.then_inc(scores_ready, 1)

            def transposes(m, t, j):
                pe.wait_ge(norm_done, m + 1)
                for i in range(NB):
                    u = m * NB + i
                    wait_from(pe, tr_lo, u - 1)
                    for blk in blocks(t, i):
                        last = nc.tensor.transpose(psT[(j * NB + i) % 2][:, (blk % 4) * P:(blk % 4 + 1) * P],
                                                   PN[j % NPN][:, blk * P:(blk + 1) * P], identF[:])
                    last.then_inc(tr_ready, 1)

            def values(head, steps, b, g):
                pe.wait_ge(tr_lo, steps * NB)
                wait_from(pe, o_lo, head)
                for blk in range(NBLK):
                    c = blk * P if causal else 0
                    for q, (hv, hp) in enumerate(PAIRS):
                        last = nc.tensor.matmul(psO[:, c:], V[b][:, hv, blk, :], PT[g % 2][:, hp, blk, c:],
                                                start=(blk + q == 0), stop=(blk == NBLK - 1 and q == 2))
                last.then_inc(pv_ready, 1)

            def jobs(h, kv, b, j, first, last, late):
                for kind, i, job, k in slot_jobs(h, j, first, last, late):
                    back = NJ if k else 1
                    if kind == "proj":
                        if b == 1 and i == 0:
                            pe.wait_ge(wp_done, (kv + 2) * NWP)
                        project(h + 1, 1 - b, i, job, psJ[k % NJ], back)
                    else:
                        pe.wait_ge(wo_done, (kv + b) * NWO)
                        output(h - 1, 1 - b, i, job, psJ[k % NJ], back)

            def half(h, kv, b, first, last):
                for j in range(NS + (TAIL if last else 0)):
                    n = h * NS + j
                    if j == 0:
                        pe.wait_ge(job_free, projections_before(h))
                        if causal:
                            pe.wait_ge(rope_done, (h + 1) * (JP - 1))
                    if j < NS:
                        scores(n, b, j // TPB, j % TPB, j)
                    jobs(h, kv, b, j, first, last, 0)
                    m = j - TAIL
                    if m % TPB == TPB - 1 and (m >= 0 or not first):
                        values(h * groups + m // TPB, n - TAIL + 1, b if m >= 0 else 1 - b, (m % NS) // TPB)
                    jobs(h, kv, b, j, first, last, 1)
                    m = j - DEPTH
                    if m < NS and (m >= 0 or not first):
                        mj = m % NS
                        transposes(n - DEPTH, mj % TPB, mj)

            pe.wait_ge(wp_done, WQ // 512)
            for i in range(JP):
                if i == min(i for i, (kind, _) in enumerate(proj) if kind != "q"):
                    pe.wait_ge(wp_done, NWP)
                project(0, 0, i, i, ring[i % len(ring)], len(ring))
            mid = halves(half)
            lo, hi = next(mid)
            with pe.Fori(lo, hi) as kv:
                for b in range(B):
                    half(kv * 2 + b, kv, b, False, False)
            for _ in mid:
                pass
            pe.wait_ge(wo_done, kv_heads * NWO)
            for t in range(TPB):
                h = 2 * kv_heads - 1
                output(h, 1, t, jobs_before(h) + JO + t, ring[(t + LAG) % len(ring)],
                       len(ring) if t or causal else NJ)

        def job_view(i):
            kind, a = proj[i]
            if kind == "q":
                return lambda b, hl: QT[b][:, hl, a, :]
            if kind == "k":
                return lambda b, hl: KT[b][:, hl, a * 512:(a + 1) * 512]
            return lambda b, hl: V[b][:, hl, 4 * a:4 * a + 4, :].rearrange("p m c -> p (m c)")

        def plain(i):
            return not causal or proj[i][0] == "v"

        def plain_count(h, i):
            return h + 1 if causal else JP * h + i + 1

        @block.scalar
        def _(act):
            def job_high(h, b, i, job, bank):
                act.wait_ge(job_ready, job + 1)
                nc.scalar.copy(job_view(i)(b, 0), bank[:, :]).then_inc(job_hi, 1)

            def rope_high(h, b, i):
                r = (JP - 1) * h + i
                par = i % 3
                dst = QT[b][:, :, i, :] if proj[i][0] == "q" else KT[b][:, :, :]
                act.wait_ge(rope_added, r + 1)
                nc.scalar.copy(dst[:, 0, :], rA[par][:]).then_inc(rope_hi, 1)

            short = [] if causal else [j for j, l in slots.items() if l[0][0][0] == "proj" and proj[l[0][0][1]][0] != "q"]

            def piece_high(what, i):
                (dst, src), hi_done = (wp_pieces[i], wp_hi) if what == "wp" else (wo_pieces[i], wo_hi)
                nc.scalar.copy(dst[:, 0], src).then_inc(hi_done, 1)

            def jobs(h, b, j, first, last, late):
                for kind, i, job, k in slot_jobs(h, j, first, last, late):
                    if kind == "proj" and plain(i):
                        job_high(h + 1, 1 - b, i, job, psJ[k % NJ])

            def half(h, kv, b, first, last):
                for j in range(NS + (TAIL if last else 0)):
                    n = h * NS + j
                    if j in short:
                        jobs(h, b, j, first, last, 0)
                    if j < NS:
                        w = width(j % TPB)
                        act.wait_ge(masked, n + 1)
                        nc.scalar.activation(SC[j % 2][:, 0:w], SC[j % 2][:, 0:w], ACT.Exp,
                                             bias=mn[:, j % 4:j % 4 + 1], scale=-1.0,
                                             accum_out=sm[:, j % 4:j % 4 + 1]).then_inc(exp_done, 1)
                    if j not in short:
                        jobs(h, b, j - LAG, first, last, 0)
                    for kind, i, job, _ in slot_jobs(h, j - 3, first, last):
                        if causal and kind == "proj" and proj[i][0] != "v":
                            rope_high(h + 1, 1 - b, i)
                    m = j - TAIL
                    if m % TPB == TPB - 1 and (m >= 0 or not first):
                        mb, mg = (b if m >= 0 else 1 - b), (m % NS) // TPB
                        act.wait_ge(pv_ready, h * groups + m // TPB + 1)
                        nc.scalar.activation(OT[mb][:, 0, mg, :], psO[:, :], ACT.Copy, scale=1.0 / PSCALE).then_inc(o_hi, 1)
                    jobs(h, b, j, first, last, 1)
                    m = j - DEPTH
                    if m < NS and (m >= 0 or not first):
                        mj = m % NS
                        mt, mg = mj % TPB, mj // TPB
                        for i in range(NB):
                            u = (n - DEPTH) * NB + i
                            bl = blocks(mt, i)
                            act.wait_ge(tr_ready, u + 1)
                            nc.scalar.copy(PT[mg % 2][:, 0, bl[0]:bl[-1] + 1, mt * P:(mt + 1) * P],
                                           psT[(mj * NB + i) % 2][:, 0:len(bl) * P].rearrange("p (k t) -> p k t", t=P)
                                           ).then_inc(tr_hi, 1)
                    piece = step_pieces(kv, b, j, last or isinstance(kv, int) and kv == kv_heads - 1)
                    if piece and piece[0] == "wp":
                        if piece[1] == 0:
                            act.wait_ge(wp_in, 48 * (kv + 1))
                            act.wait_ge(job_ready, jobs_before(h + 1) - (0 if first else JO))
                        piece_high(*piece[:2])
                    elif piece:
                        if piece[1] == 0:
                            act.wait_ge(wo_in, 16 * (kv + 1))
                            act.wait_ge(job_ready, jobs_before(h))
                        piece_high(*piece[:2])

            act.wait_ge(first_in, 48)
            for i in range(NWP):
                piece_high("wp", i)
            for i in range(JP):
                if plain(i):
                    job_high(0, 0, i, i, ring[i % len(ring)])
                else:
                    rope_high(0, 0, i)
            mid = halves(half)
            lo, hi = next(mid)
            with act.Fori(lo, hi) as kv:
                for b in range(B):
                    half(kv * 2 + b, kv, b, False, False)
            for _ in mid:
                pass

        @block.vector
        def _(dve):
            def job_low(h, b, i, job, bank):
                if plain(i):
                    dve.wait_ge(job_hi, plain_count(h, i))
                    dve.wait_ge(job_ready, job + 1)
                    nc.vector.tensor_tensor(job_view(i)(b, 1), bank[:, :], job_view(i)(b, 0),
                                            ALU.subtract).then_inc(job_free, 1)
                    return
                r = (JP - 1) * h + i
                par = i % 3
                dve.wait_ge(job_ready, job + 1)
                if i != 2:
                    wait_from(dve, rope_done, r - 1 if i < 2 else r - 2)
                else:
                    wait_from(dve, rope_done, r - 4)
                ropeC, ropeS = rope
                nc.vector.tensor_tensor(rA[par][:], bank[:, :], ropeC[:], ALU.mult)
                nc.vector.tensor_tensor(rB[par][64:128, :], bank[0:64, :], ropeS[0:64, :], ALU.mult)
                nc.vector.tensor_tensor(rB[par][0:64, :], bank[64:128, :], ropeS[64:128, :],
                                        ALU.mult).then_inc(job_free, 1)

            def output_add(h, b, t, job, bank):
                dve.wait_ge(job_ready, job + 1)
                nc.vector.tensor_tensor(X[:, b * TPB + t, :], bank[:, :], X[:, b * TPB + t, :], ALU.add).then_inc(job_free, 1)

            def jobs(h, b, j, first, last, late):
                for kind, i, job, k in slot_jobs(h, j, first, last, late):
                    if kind == "proj":
                        job_low(h + 1, 1 - b, i, job, psJ[k % NJ])
                    else:
                        output_add(h - 1, 1 - b, i, job, psJ[k % NJ])

            def half(h, kv, b, first, last):
                for j in range(NS + (TAIL if last else 0)):
                    n = h * NS + j
                    if j < NS:
                        w = width(j % TPB)
                        dve.wait_ge(scores_ready, n + 1)
                        wait_from(dve, norm_done, n - 1)
                        stand_apart(dve, dve_passed)
                        nc.vector.tensor_tensor_reduce(out=SC[j % 2][:, 0:w], in0=psS[j % 2][:, 0:w],
                                                       in1=mask_of(b, j % TPB), scale=-SCORE_SCALE, scalar=3e38,
                                                       op0=ALU.add, op1=ALU.min,
                                                       accum_out=mn[:, j % 4:j % 4 + 1]).then_inc(masked, 1)
                    jobs(h, b, j - LAG, first, last, 0)
                    if j < NS:
                        dve.wait_ge(exp_done, n + 1)
                        nc.vector.reciprocal(rc[:, j % 4:j % 4 + 1], sm[:, j % 4:j % 4 + 1]).then_inc(recip_done, 1)
                    m = j - TAIL
                    if m % TPB == TPB - 1 and (m >= 0 or not first):
                        mb, mg = (b if m >= 0 else 1 - b), (m % NS) // TPB
                        dve.wait_ge(o_hi, h * groups + m // TPB + 1)
                        nc.vector.scalar_tensor_tensor(out=OT[mb][:, 1, mg, :], in0=psO[:, :], scalar=1.0 / PSCALE,
                                                       in1=OT[mb][:, 0, mg, :], op0=ALU.mult,
                                                       op1=ALU.subtract).then_inc(o_lo, 1)
                    jobs(h, b, j, first, last, 1)
                    m = j - DEPTH
                    if m < NS and (m >= 0 or not first):
                        mj = m % NS
                        mt, mg = mj % TPB, mj // TPB
                        for i in range(NB):
                            u = (n - DEPTH) * NB + i
                            bl = blocks(mt, i)
                            dve.wait_ge(tr_hi, u + 1)
                            dst = (slice(bl[0], bl[-1] + 1), slice(mt * P, (mt + 1) * P))
                            nc.vector.tensor_tensor(PT[mg % 2][:, 1, dst[0], dst[1]],
                                                    psT[(mj * NB + i) % 2][:, 0:len(bl) * P].rearrange("p (k t) -> p k t", t=P),
                                                    PT[mg % 2][:, 0, dst[0], dst[1]], ALU.subtract).then_inc(tr_lo, 1)

            for i, (dst, src) in enumerate(wp_pieces):
                dve.wait_ge(wp_hi, i + 1)
                nc.vector.tensor_tensor(dst[:, 1], src, dst[:, 0], ALU.subtract).then_inc(wp_done, 1)
            for i in range(JP):
                job_low(0, 0, i, i, ring[i % len(ring)])
            mid = halves(half)
            lo, hi = next(mid)
            with dve.Fori(lo, hi) as kv:
                for b in range(B):
                    half(kv * 2 + b, kv, b, False, False)
            for _ in mid:
                pass
            for t in range(TPB):
                h = 2 * kv_heads - 1
                output_add(h, 1, t, jobs_before(h) + JO + t, ring[(t + LAG) % len(ring)])


def w13_split_pieces(W13, W13raw):
    return [(W13[:, :, :, i // 2, (i % 2) * 512:(i % 2) * 512 + 512], W13raw[:, :, i // 2, (i % 2) * 512:(i % 2) * 512 + 512])
            for i in range(8)]


def phase_route(nc, XT, gate_w, wts, p12, slots, over):
    with ExitStack() as st:
        named = phase_semaphores(nc, st)
        sem = lambda n: named(f"route_{n}")

        def sb(n, shape, dt):
            return st.enter_context(nc.sbuf_tensor(f"route_{n}", shape, dt))

        GW = sb("GW", [P, DC, E], F32)
        GWP = sb("GWP", [P, 2, DC, E], F16)
        lg = sb("lg", [P, NT, E], F32)
        top = sb("top", [P, NT, 8], F32)
        idx = sb("idx", [P, NT, 8], U32)
        idf = sb("idf", [P, NT, 8], F32)
        dlt = sb("dlt", [P, NT], F32)
        ex = sb("ex", [P, NT], F32)
        ex1 = sb("ex1", [P, NT], F32)
        expert = sb("expert", [P, E], F32)
        base = sb("base", [P, E], F32)
        onehot = sb("onehot", [P, 2, NT, E], F32)
        picks = sb("picks", [P, NT, E], F16)
        before = sb("before", [P, NT + 1, E], F16)
        part = sb("part", [P, 2, NT, E], F32)
        rank = sb("rank", [P, NT, E], F32)
        slotf = sb("slotf", [P, 2, NT], F32)
        counts = sb("counts", [P, 1], F32)
        zero = sb("zero", [P, P], F32)
        earlier = sb("earlier", [P, P], F32)
        earlier16 = sb("earlier16", [P, P], F16)
        ones16 = sb("ones16", [P, P], F16)
        psL = st.enter_context(nc.psum_tensor("route_psL", [P, 512], F32))
        psR = st.enter_context(nc.psum_tensor("route_psR", [P, 512], F32))
        psC = st.enter_context(nc.psum_tensor("route_psC", [P, 512], F32))

        gw_in, gw_hi, gw_done, iota_done, zero_done, tri_done, mats_done = (
            sem("gw_in"), sem("gw_hi"), sem("gw_done"), sem("iota_done"), sem("zero_done"), sem("tri_done"), sem("mats_done"))
        logits_ready, dlt_done, ex_done, chain = sem("logits_ready"), sem("dlt_done"), sem("ex_done"), sem("chain")
        picks_done, rank_ready = sem("picks_done"), sem("rank_ready")
        block = st.enter_context(nc.Block())

        @block.sync
        def _(sp):
            sp.dma_start(GW[:], gate_w.rearrange("(k p) e -> p k e", p=P)).then_inc(gw_in, 16)

        @block.gpsimd
        def _(pool):
            nc.gpsimd.iota(expert[:], pattern=[[1, E]], base=0, channel_multiplier=0,
                           allow_small_or_imprecise_dtypes=True).then_inc(iota_done, 1)
            nc.gpsimd.iota(base[:], pattern=[[CAP, E]], base=0, channel_multiplier=0,
                           allow_small_or_imprecise_dtypes=True).then_inc(iota_done, 1)
            nc.gpsimd.memset(zero[:], 0.0).then_inc(zero_done, 1)
            nc.gpsimd.memset(ones16[:], 1.0).then_inc(mats_done, 1)
            pool.wait_ge(zero_done, 1)
            nc.gpsimd.affine_select(out=earlier[:], in_=zero[:], compare_op=ALU.is_ge, fill=1.0, base=0,
                                    pattern=[[-1, P]], channel_multiplier=1).then_inc(tri_done, 1)
            pool.wait_ge(tri_done, 1)
            nc.gpsimd.tensor_copy(earlier16[:], earlier[:]).then_inc(mats_done, 1)

        @block.tensor
        def _(pe):
            pe.wait_ge(gw_done, 1)
            for i in range(NT):
                for q, (hx, hw) in enumerate(PAIRS):
                    for k in range(DC):
                        last = nc.tensor.matmul(psL[:, i * E:(i + 1) * E], XT[:, hx, k, i * P:(i + 1) * P], GWP[:, hw, k, :],
                                                start=(q + k == 0), stop=(q == 2 and k == DC - 1))
            last.then_inc(logits_ready, 1)
            pe.wait_ge(picks_done, 1)
            pe.wait_ge(mats_done, 2)
            nc.tensor.matmul(psR[:, 0:NT * E], earlier16[:], picks[:].rearrange("p t e -> p (t e)"), start=True, stop=False)
            nc.tensor.matmul(psR[:, 0:NT * E], ones16[:], before[:, 0:NT, :].rearrange("p t e -> p (t e)"),
                             start=False, stop=True)
            nc.tensor.matmul(psC[:, 0:E], ones16[:], before[:, NT, :], start=True, stop=True).then_inc(rank_ready, 1)

        @block.scalar
        def _(act):
            act.wait_ge(dlt_done, 1)
            nc.scalar.activation(ex[:], dlt[:], ACT.Exp).then_inc(ex_done, 1)

        @block.vector
        def _(dve):
            steps = [0]

            def chained(ins):
                steps[0] += 1
                ins.then_inc(chain, 1)
                dve.wait_ge(chain, steps[0])

            dve.wait_ge(gw_in, 16)
            nc.vector.tensor_copy(GWP[:, 0, :, :], GW[:]).then_inc(gw_hi, 1)
            dve.wait_ge(gw_hi, 1)
            nc.vector.tensor_tensor(GWP[:, 1, :, :], GW[:], GWP[:, 0, :, :], ALU.subtract).then_inc(gw_done, 1)
            dve.wait_ge(logits_ready, 1)
            chained(nc.vector.tensor_copy(lg[:].rearrange("p t e -> p (t e)"), psL[:, 0:NT * E]))
            for i in range(NT):
                last = nc.vector.max(top[:, i, :], lg[:, i, :])
            chained(last)
            for i in range(NT):
                last = nc.vector.max_index(idx[:, i, :], top[:, i, :], lg[:, i, :])
            chained(last)
            nc.vector.tensor_tensor(dlt[:], top[:, :, 1], top[:, :, 0], ALU.subtract).then_inc(dlt_done, 1)
            chained(nc.vector.tensor_copy(idf[:], idx[:]))
            dve.wait_ge(iota_done, 2)
            wide = [P, NT, E]
            for k in range(2):
                last = nc.vector.tensor_tensor(onehot[:, k], expert[:].unsqueeze(1).broadcast_to(wide),
                                               idf[:, :, k:k + 1].broadcast_to(wide), ALU.is_equal)
            chained(last)
            chained(nc.vector.tensor_tensor(picks[:], onehot[:, 0], onehot[:, 1], ALU.add))
            chained(nc.vector.memset(before[:, 0, :], 0.0))
            for i in range(NT):
                chained(nc.vector.tensor_tensor(before[:, i + 1, :], before[:, i, :], picks[:, i, :], ALU.add))
            nc.vector.tensor_copy(counts[:], expert[:, 0:1]).then_inc(picks_done, 1)
            dve.wait_ge(ex_done, 1)
            chained(nc.vector.tensor_scalar(ex1[:], ex[:], 1.0, None, ALU.add))
            chained(nc.vector.reciprocal(p12[:, 0, :], ex1[:]))
            chained(nc.vector.tensor_tensor(p12[:, 1, :], ex[:], p12[:, 0, :], ALU.mult))
            for k in range(2):
                last = nc.vector.tensor_tensor(part[:, k], onehot[:, k], p12[:, k, :].unsqueeze(2).broadcast_to(wide), ALU.mult)
            chained(last)
            chained(nc.vector.tensor_tensor(wts[:], part[:, 0], part[:, 1], ALU.add))
            dve.wait_ge(rank_ready, 1)
            chained(nc.vector.tensor_tensor(rank[:], psR[:, 0:NT * E].rearrange("p (t e) -> p t e", e=E),
                                            base[:].unsqueeze(1).broadcast_to(wide), ALU.add))
            for k in range(2):
                last = nc.vector.tensor_tensor(part[:, k], onehot[:, k], rank[:], ALU.mult)
            chained(last)
            chained(nc.vector.tensor_reduce(slotf[:], part[:], AX_X, ALU.add))
            chained(nc.vector.tensor_copy(slots[:], slotf[:]))
            chained(nc.vector.tensor_reduce(counts[:], psC[:, 0:E], AX_X, ALU.max))
            chained(nc.vector.tensor_scalar(over[:], counts[:], float(CAP), None, ALU.is_gt))


def phase_moe_routed(nc, X, XT, XW, scratch, XG, YG, w1, w3, w2, W13raw, W13, W2raw, W2, p12, slots, arrived, out):
    with ExitStack() as st:
        named = phase_semaphores(nc, st)
        sem = lambda n: named(f"rmoe_{n}")

        def sb(n, shape, dt):
            return st.enter_context(nc.sbuf_tensor(f"rmoe_{n}", shape, dt))

        def pb(n):
            return st.enter_context(nc.psum_tensor(f"rmoe_{n}", [P, 512], F32))

        XR = scratch[:, 0:CTL, :]
        YR = scratch[:, CTL:2 * CTL, :]
        XGT = sb("XGT", [P, 2, DC, CAP], F16)
        SG = [sb(f"SG{i}", [P, CAP], F32) for i in range(2)]
        HF = [sb(f"HF{i}", [P, CAP], F32) for i in range(2)]
        HT = sb("HT", [P, 2, FC, CAP], F16)
        ident = sb("ident", [P, P], F32)
        stats = sb("stats", [P, NT, 6], F32)
        mv = sb("mv", [P, NT, 2], F32)
        ve = sb("ve", [P, NT], F32)
        half = sb("half", [P, 1], F32)
        rstd = sb("rstd", [P, NT], F32)
        psG = [pb(f"psG{i}") for i in range(2)]
        psU = [pb(f"psU{i}") for i in range(2)]
        psY = [pb(f"psY{i}") for i in range(2)]
        psT = [pb(f"psT{i}") for i in range(2)]
        Y1, Y2 = XW, XT[:].rearrange("p l k t -> p (l k t)").bitcast(F32).rearrange("p (t d) -> p t d", d=D)

        ident_zero, ident_done = sem("ident_zero"), sem("ident_done")
        scattered, x_in = sem("scattered"), sem("x_in")
        w13_in, w2_in, w13_hi, w13_done, w2_hi, w2_done = (
            sem("w13_in"), sem("w2_in"), sem("w13_hi"), sem("w13_done"), sem("w2_hi"), sem("w2_done"))
        tr_ready, tr_hi, tr_lo = sem("tr_ready"), sem("tr_hi"), sem("tr_lo")
        up_ready, silu_done, h_done, h_hi, h_lo = (
            sem("up_ready"), sem("silu_done"), sem("h_done"), sem("h_hi"), sem("h_lo"))
        down_ready, y_copied = sem("down_ready"), sem("y_copied")
        y_stored = [sem(f"y_stored{r}") for r in range(CTL)]
        gathered = [sem(f"gathered{t}") for t in range(NT)]
        combined = sem("combined")
        half_done, stats_done, mv_done, ve_done, rstd_done, ln_done, out_done = (
            sem("half_done"), sem("stats_done"), sem("mv_done"), sem("ve_done"), sem("rstd_done"), sem("ln_done"),
            sem("out_done"))
        w13_pieces = w13_split_pieces(W13, W13raw)
        w2_pieces = [(W2[:, :, i, :], W2raw[:, i, :]) for i in range(FC)]
        xg_v, yg_v = (g.rearrange("(e c) d -> e c d", c=CAP) for g in (XG, YG))

        def width(r):
            return min(P, CAP - r * P)

        block = st.enter_context(nc.Block())

        def over_experts(eng, emit):
            emit(0, True, False)
            with eng.Fori(1, E - 1) as e:
                emit(e, False, False)
            emit(E - 1, False, True)

        @block.sync
        def _(sp):
            def load_rows(e):
                wait_from(sp, tr_ready, DC * e)
                whole = CAP // P
                sp.dma_start(XR[:, 0:whole, :], xg_v[bass.ds(e, 1), 0:whole * P].rearrange(
                    "o (r p) d -> p (o r) d", p=P)).then_inc(x_in, 16)
                sp.dma_start(XR[0:CAP % P, whole, :], xg_v[bass.ds(e, 1), whole * P:CAP].rearrange(
                    "o p d -> p (o d)")).then_inc(x_in, 16)

            sp.wait_ge(scattered, 16 * 2 * NT)
            load_rows(0)

            def step(e, first, last):
                if not last:
                    load_rows(e + 1)
                    sp.wait_ge(w13_done, 8 * (e + 1))
                    for i, w in enumerate((w1, w3)):
                        sp.dma_start(W13raw[:, i, :, :], w[bass.ds(e + 1, 1)].rearrange("o (k p) f -> p (o k) f", p=P)).then_inc(w13_in, 16)
                    sp.wait_ge(w2_done, FC * (e + 1))
                    sp.dma_start(W2raw[:], w2[bass.ds(e + 1, 1)].rearrange("o (k p) d -> p (o k) d", p=P)).then_inc(w2_in, 16)
                for r in range(CTL):
                    sp.wait_ge(y_copied, CTL * e + r + 1)
                    sp.dma_start(yg_v[bass.ds(e, 1), r * P:r * P + width(r)].rearrange("o p d -> p (o d)"), YR[0:width(r), r, :]).then_inc(y_stored[r], 16)

            over_experts(sp, step)
            for r in range(CTL):
                sp.wait_ge(y_stored[r], 16 * E)
            for i in range(NT):
                sp.wait_ge(ln_done, i + 1)
                sp.dma_start(out[i // TPB, (i % TPB) * P:(i % TPB + 1) * P, :], X[:, i, :]).then_inc(out_done, 16)
            sp.wait_ge(out_done, 16 * NT)

        @block.gpsimd
        def _(pool):
            for t in range(NT):
                for k in range(2):
                    pool.indirect_dma_start(out=XG, out_offset=bass.IndirectOffsetOnAxis(ap=slots[:, k, t:t + 1], axis=0),
                                            in_=XW[:, t, :], in_offset=None).then_inc(scattered, 16)
            nc.gpsimd.memset(ident[:], 0.0).then_inc(ident_zero, 1)
            pool.wait_ge(ident_zero, 1)
            nc.gpsimd.affine_select(out=ident[:], in_=ident[:], compare_op=ALU.not_equal, fill=1.0, base=0,
                                    pattern=[[-1, P]], channel_multiplier=1).then_inc(ident_done, 1)
            nc.gpsimd.memset(half[:], -0.5).then_inc(half_done, 1)
            pool.wait_ge(half_done, 1)
            for r in range(CTL):
                pool.wait_ge(y_stored[r], 16 * E)
            pool.wait_ge(scattered, 16 * 2 * NT)
            for t in range(NT + 4):
                for k, dst in enumerate((Y1, Y2) if t < NT else ()):
                    pool.indirect_dma_start(out=dst[:, t, :], out_offset=None, in_=YG,
                                            in_offset=bass.IndirectOffsetOnAxis(ap=slots[:, k, t:t + 1], axis=0)
                                            ).then_inc(gathered[t], 16)
                i = t - 4
                if i >= 0:
                    pool.wait_ge(mv_done, i + 1)
                    nc.gpsimd.tensor_scalar(ve[:, i:i + 1], mv[:, i, 1:2], EPS, 1.0, ALU.add, ALU.mult).then_inc(ve_done, 1)
                    pool.wait_ge(ve_done, i + 1)
                    nc.gpsimd.tensor_tensor(rstd[:, i:i + 1], ve[:, i:i + 1], half[:], ALU.pow).then_inc(rstd_done, 1)

        @block.tensor
        def _(pe):
            def transposes(e, ks):
                pe.wait_ge(x_in, 32 * (e + 1))
                for k in ks:
                    wait_from(pe, tr_lo, DC * e + k - 1)
                    for r in range(CTL):
                        w = width(r)
                        last = nc.tensor.transpose(psT[k % 2][:, r * P:r * P + w], XR[0:w, r, k * P:(k + 1) * P], ident[0:w, 0:w])
                    last.then_inc(tr_ready, 1)

            def step(e, first, last_e):
                pe.wait_ge(w13_done, 8 * (e + 1))
                pe.wait_ge(tr_lo, DC * (e + 1))
                for f in range(FC):
                    n = e * FC + f
                    wait_from(pe, h_done, n - 1)
                    for w, bank in ((0, psG), (1, psU)):
                        for i, (hw, hx) in enumerate(PAIRS):
                            for k in range(DC):
                                last = nc.tensor.matmul(bank[f % 2][:, 0:CAP], W13[:, hw, w, k, f * P:(f + 1) * P],
                                                        XGT[:, hx, k, :], start=(i + k == 0),
                                                        stop=(i == 2 and k == DC - 1))
                    last.then_inc(up_ready, 1)
                if not last_e:
                    transposes(e + 1, (0, 1))
                for r in range(CTL):
                    y = r % 2
                    wait_from(pe, y_copied, e * CTL + r - 1 if r else e * CTL)
                    w = width(r)
                    for k in range(FC):
                        if r == 0:
                            pe.wait_ge(w2_done, e * FC + k + 1)
                            pe.wait_ge(h_lo, e * FC + k + 1)
                        for i, (hh, hw) in enumerate(PAIRS):
                            last = nc.tensor.matmul(psY[y][0:w, :], HT[:, hh, k, r * P:r * P + w], W2[:, hw, k, :],
                                                    start=(i + k == 0), stop=(i == 2 and k == FC - 1))
                    last.then_inc(down_ready, 1)
                    if r == 0 and not last_e:
                        transposes(e + 1, (2, 3))

            pe.wait_ge(ident_done, 1)
            transposes(0, range(DC))
            over_experts(pe, step)

        @block.scalar
        def _(act):
            def rows_high(e, ks):
                for k in ks:
                    act.wait_ge(tr_ready, DC * e + k + 1)
                    if k == 0:
                        wait_from(act, up_ready, FC * e)
                    nc.scalar.copy(XGT[:, 0, k, :], psT[k % 2][:, 0:CAP]).then_inc(tr_hi, 1)

            def w13_high(pieces):
                for dst, src in pieces:
                    nc.scalar.copy(dst[:, 0], src).then_inc(w13_hi, 1)

            def step(e, first, last):
                if first:
                    act.wait_ge(arrived[1], 16)
                else:
                    act.wait_ge(w2_in, 16 * e)
                wait_from(act, down_ready, CTL * e)
                for f in range(FC):
                    n = e * FC + f
                    act.wait_ge(up_ready, n + 1)
                    nc.scalar.activation(SG[f % 2][:], psG[f % 2][:, 0:CAP], ACT.Silu).then_inc(silu_done, 1)
                    dst, src = w2_pieces[f]
                    nc.scalar.copy(dst[:, 0], src).then_inc(w2_hi, 1)
                    act.wait_ge(h_done, n + 1)
                    nc.scalar.copy(HT[:, 0, f, :], HF[f % 2][:]).then_inc(h_hi, 1)
                if not last:
                    rows_high(e + 1, (0, 1))
                    act.wait_ge(w13_in, 32 * (e + 1))
                    w13_high(w13_pieces[0:3])
                    rows_high(e + 1, (2, 3))
                    w13_high(w13_pieces[3:8])

            act.wait_ge(arrived[0], 32)
            w13_high(w13_pieces)
            rows_high(0, range(DC))
            over_experts(act, step)

        @block.vector
        def _(dve):
            def rows_low(e, ks):
                for k in ks:
                    dve.wait_ge(tr_hi, DC * e + k + 1)
                    nc.vector.tensor_tensor(XGT[:, 1, k, :], psT[k % 2][:, 0:CAP], XGT[:, 0, k, :], ALU.subtract).then_inc(tr_lo, 1)

            def w13_low(e, pieces):
                for i in pieces:
                    dst, src = w13_pieces[i]
                    dve.wait_ge(w13_hi, 8 * e + i + 1)
                    nc.vector.tensor_tensor(dst[:, 1], src, dst[:, 0], ALU.subtract).then_inc(w13_done, 1)

            def step(e, first, last):
                for f in range(FC):
                    n = e * FC + f
                    dve.wait_ge(silu_done, n + 1)
                    wait_from(dve, h_lo, n - 1)
                    nc.vector.tensor_tensor(HF[f % 2][:], psU[f % 2][:, 0:CAP], SG[f % 2][:], ALU.mult).then_inc(h_done, 1)
                    dst, src = w2_pieces[f]
                    dve.wait_ge(w2_hi, n + 1)
                    nc.vector.tensor_tensor(dst[:, 1], src, dst[:, 0], ALU.subtract).then_inc(w2_done, 1)
                    dve.wait_ge(h_hi, n + 1)
                    nc.vector.tensor_tensor(HT[:, 1, f, :], HF[f % 2][:], HT[:, 0, f, :], ALU.subtract).then_inc(h_lo, 1)
                for r in range(CTL):
                    if not last:
                        if r < 2:
                            rows_low(e + 1, (2 * r, 2 * r + 1))
                        w13_low(e + 1, range(3 * r, min(3 * r + 3, 8)))
                    dve.wait_ge(down_ready, CTL * e + r + 1)
                    wait_from(dve, y_stored[r], 16 * e)
                    nc.vector.tensor_copy(YR[0:width(r), r, :], psY[r % 2][0:width(r), :]).then_inc(y_copied, 1)

            def layer_norm(i):
                dve.wait_ge(rstd_done, i + 1)
                dve.wait_ge(mv_done, i + 1)
                nc.vector.tensor_scalar(X[:, i, :], X[:, i, :], mv[:, i, 0:1], rstd[:, i:i + 1], ALU.subtract,
                                        ALU.mult).then_inc(ln_done, 1)

            w13_low(0, range(8))
            rows_low(0, range(DC))
            over_experts(dve, step)
            for t in range(NT):
                dve.wait_ge(gathered[t], 32)
                nc.vector.scalar_tensor_tensor(out=X[:, t, :], in0=Y1[:, t, :], scalar=p12[:, 0, t:t + 1],
                                               in1=X[:, t, :], op0=ALU.mult, op1=ALU.add).then_inc(combined, 1)
                dve.wait_ge(combined, 2 * t + 1)
                nc.vector.scalar_tensor_tensor(out=X[:, t, :], in0=Y2[:, t, :], scalar=p12[:, 1, t:t + 1],
                                               in1=X[:, t, :], op0=ALU.mult, op1=ALU.add).then_inc(combined, 1)
                dve.wait_ge(combined, 2 * t + 2)
                nc.vector.bn_stats(stats[:, t, :], X[:, t, :]).then_inc(stats_done, 1)
                dve.wait_ge(stats_done, t + 1)
                nc.vector.bn_aggr(mv[:, t, :], stats[:, t, :]).then_inc(mv_done, 1)
                if t >= 3:
                    layer_norm(t - 3)
            for i in range(NT - 3, NT):
                layer_norm(i)


def phase_moe_dense(nc, X, XT, wts, w1, w3, w2, W13raw, W13, W2raw, W2, scratch,
                    arrived):
    with ExitStack() as st:
        sem = phase_semaphores(nc, st)

        def sb(n, shape, dt):
            return st.enter_context(nc.sbuf_tensor(f"moe_{n}", shape, dt))

        def pb(n, shape):
            return st.enter_context(nc.psum_tensor(f"moe_{n}", shape, F32))

        SG = [sb(f"SG{i}", [P, S], F32) for i in range(2)]
        HF = [sb(f"HF{i}", [P, S], F32) for i in range(4)]
        HT = scratch[:].rearrange("p l t d -> p (l t d)").bitcast(F16).rearrange("p (l f t) -> p l f t", l=2, f=FC)
        psG = [pb(f"psG{i}", [P, 512]) for i in range(2)]
        psU = [pb(f"psU{i}", [P, 512]) for i in range(2)]
        psY = [pb(f"psY{i}", [P, 512]) for i in range(2)]

        s = lambda n: sem(f"moe_{n}")
        pool_passed = s("pool_passed")
        w13_in, w2_in = s("w13_in"), s("w2_in")
        w13_hi, w13_done, w2_hi, w2_done = s("w13_hi"), s("w13_done"), s("w2_hi"), s("w2_done")
        up_ready, silu_done, h_done, h_hi, h_split = s("up_ready"), s("silu_done"), s("h_done"), s("h_hi"), s("h_split")
        down_ready, added = s("down_ready"), s("added")
        UP = B * FC
        block = st.enter_context(nc.Block())

        def over_experts(eng, emit):
            emit(0, True, False)
            with eng.Fori(1, E - 1) as e:
                emit(e, False, False)
            emit(E - 1, False, True)

        @block.sync
        def _(sp):
            def load(e):
                wait_from(sp, w13_done, e * 8)
                for i, w in enumerate((w1, w3)):
                    sp.dma_start(W13raw[:, i, :, :], w[bass.ds(e, 1)].rearrange("o (k p) f -> p (o k) f", p=P)).then_inc(w13_in, 16)
                wait_from(sp, w2_done, e * 8)
                sp.dma_start(W2raw[:], w2[bass.ds(e, 1)].rearrange("o (k p) d -> p (o k) d", p=P)).then_inc(w2_in, 16)

            sp.wait_ge(arrived[0], 32)
            sp.wait_ge(arrived[1], 16)
            load(0)
            with sp.Fori(1, E) as e:
                load(e)

        @block.gpsimd
        def _(pool):
            def split_w13(e, i):
                at = (i // 2, slice((i % 2) * 512, (i % 2) * 512 + 512))
                stand_apart(pool, pool_passed)
                nc.gpsimd.tensor_copy(W13[:, 0, :, at[0], at[1]], W13raw[:, :, at[0], at[1]]).then_inc(w13_hi, 1)
                pool.wait_ge(w13_hi, e * 8 + i + 1)
                nc.gpsimd.tensor_tensor(W13[:, 1, :, at[0], at[1]], W13raw[:, :, at[0], at[1]],
                                        W13[:, 0, :, at[0], at[1]], ALU.subtract).then_inc(w13_done, 1)

            def split_w2(e, i):
                stand_apart(pool, pool_passed)
                nc.gpsimd.tensor_copy(W2[:, 0, i, :], W2raw[:, i, :]).then_inc(w2_hi, 1)
                pool.wait_ge(w2_hi, e * 8 + i + 1)
                nc.gpsimd.tensor_tensor(W2[:, 1, i, :], W2raw[:, i, :], W2[:, 0, i, :], ALU.subtract).then_inc(w2_done, 1)

            def expert_steps(e, first, last):
                for q in range(UP):
                    b, f = q // FC, q % FC
                    if q == 0:
                        pool.wait_ge(w2_in, 16 * (e + 1))
                        wait_from(pool, down_ready, e * NT)
                    if q < 8:
                        split_w2(e, q)
                    n = e * UP + q
                    pool.wait_ge(h_done, n + 1)
                    stand_apart(pool, pool_passed)
                    nc.gpsimd.tensor_copy(HT[:, 0, f, b * S:(b + 1) * S], HF[q % 4][:]).then_inc(h_hi, 1)
                    pool.wait_ge(h_hi, n + 1)
                    nc.gpsimd.tensor_tensor(HT[:, 1, f, b * S:(b + 1) * S], HF[q % 4][:], HT[:, 0, f, b * S:(b + 1) * S],
                                            ALU.subtract).then_inc(h_split, 1)
                if not last:
                    pool.wait_ge(w13_in, 32 * (e + 2))
                    pool.wait_ge(up_ready, (e + 1) * UP)
                    for i in range(8):
                        split_w13(e + 1, i)

            pool.wait_ge(w13_in, 32)
            for i in range(8):
                split_w13(0, i)
            over_experts(pool, expert_steps)

        @block.tensor
        def _(pe):
            def expert_steps(e, first, last_e):
                pe.wait_ge(w13_done, (e + 1) * 8)
                for q in range(UP):
                    n = e * UP + q
                    b, f = q // FC, q % FC
                    wait_from(pe, h_done, n - 1)
                    for w, bank in ((0, psG), (1, psU)):
                        for i, (hw, hx) in enumerate(PAIRS):
                            for k in range(DC):
                                last = nc.tensor.matmul(bank[q % 2][:, :], W13[:, hw, w, k, f * P:(f + 1) * P],
                                                        XT[:, hx, k, b * S:(b + 1) * S], start=(i + k == 0),
                                                        stop=(i == 2 and k == DC - 1))
                    last.then_inc(up_ready, 1)
                pe.wait_ge(w2_done, (e + 1) * 8)
                for t in range(NT):
                    if t % TPB == 0:
                        pe.wait_ge(h_split, e * UP + (t // TPB + 1) * FC)
                    wait_from(pe, added, e * NT + t - 1)
                    for i, (hh, hw) in enumerate(PAIRS):
                        for k in range(FC):
                            last = nc.tensor.matmul(psY[t % 2][:, :], HT[:, hh, k, t * P:(t + 1) * P], W2[:, hw, k, :],
                                                    start=(i + k == 0), stop=(i == 2 and k == FC - 1))
                    last.then_inc(down_ready, 1)

            over_experts(pe, expert_steps)

        @block.scalar
        def _(act):
            def expert_steps(e, first, last):
                for q in range(UP):
                    n = e * UP + q
                    act.wait_ge(up_ready, n + 1)
                    wait_from(act, h_done, n - 1)
                    nc.scalar.activation(SG[q % 2][:], psG[q % 2][:, :], ACT.Silu).then_inc(silu_done, 1)

            over_experts(act, expert_steps)

        @block.vector
        def _(dve):
            def expert_steps(e, first, last):
                for q in range(UP):
                    n = e * UP + q
                    dve.wait_ge(silu_done, n + 1)
                    wait_from(dve, h_split, n - 3)
                    nc.vector.tensor_tensor(HF[q % 4][:], psU[q % 2][:, :], SG[q % 2][:], ALU.mult).then_inc(h_done, 1)
                for t in range(NT):
                    dve.wait_ge(down_ready, e * NT + t + 1)
                    wait_from(dve, added, (e - 1) * NT + t + 1)
                    nc.vector.scalar_tensor_tensor(out=X[:, t, :], in0=psY[t % 2][:, :], scalar=wts[:, t, bass.ds(e, 1)],
                                                   in1=X[:, t, :], op0=ALU.mult, op1=ALU.add).then_inc(added, 1)

            over_experts(dve, expert_steps)


def decoder_layer(nc, x, ctxt, mask, W_in, W_out, log_A, W_dt, b_dt, xWq, xWk, xWv, xWo, norm1_w, norm2_w, wq, wk, wv, wo,
                  gate_w, w1, w3, w2, rope_in, XG, YG, out):
    with ExitStack() as st:
        def sb(name, shape, dt):
            return st.enter_context(nc.sbuf_tensor(name, shape, dt))

        X = sb("X", [P, NT, D], F32)
        XT = sb("XT", [P, 2, DC, T], F16)
        identF = sb("identF", [P, P], F32)
        causal = sb("causal", [P, S], F32)
        flag = sb("flag", [P, B], F32)
        ropeC = sb("ropeC", [P, S], F32)
        ropeS = sb("ropeS", [P, S], F32)

        with ExitStack() as cross:
            CT = cross.enter_context(nc.sbuf_tensor("CT", [P, 2, DCTX // P, B * S2], F16))
            maskb = cross.enter_context(nc.sbuf_tensor("maskb", [P, B, S2], F32))
            weights, loads = attention_weights(nc, cross, "xa", 2, DCTX // P, xWq, xWk, xWv)
            phase_ssm(nc, X, XT, CT, XG, x, ctxt, mask, W_in, W_out, log_A, W_dt, b_dt,
                      (identF, causal, maskb, flag, ropeC, ropeS), rope_in, loads)
            attention(nc, "xa", X, XT, CT, identF, weights, xWq, xWk, xWv, xWo, 8, 2, S2,
                      lambda b, t: maskb[:, b, :], flag, None)
        rows = sb("rows", [P, 2, NT, D], F32)
        XW = rows[:, 0]
        X2 = rows[:, 1]
        with ExitStack() as own:
            weights, loads = attention_weights(nc, own, "sa", 4, DC, wq, wk, wv)
            phase_norm(nc, "n2", X, identF, XT=XT, norm_w=norm1_w, keep=X2, fetch=loads)
            attention(nc, "sa", X, XT, XT, identF, weights, wq, wk, wv, wo, 4, 4, S,
                      lambda b, t: causal[:, S - (t + 1) * P:S], None, (ropeC, ropeS))
        W13raw = sb("W13raw", [P, 2, DC, F], F32)
        W13 = sb("W13", [P, 2, 2, DC, F], F16)
        W2raw = sb("W2raw", [P, FC, D], F32)
        W2 = sb("W2", [P, 2, FC, D], F16)
        wts = sb("wts", [P, NT, E], F32)
        p12 = sb("p12", [P, 2, NT], F32)
        slots = sb("slots", [P, 2, NT], U32)
        over = sb("over", [P, 1], I32)
        arrived = [nc.alloc_semaphore(name=f"first_{w}_in") for w in ("w13", "w2")]
        phase_norm(nc, "n3", X, identF, XT=XT, norm_w=norm2_w, layer=False, add=X2, rows=XW,
                   fetch=[(W13raw[:, 0], w1[0].rearrange("(k p) f -> p k f", p=P), arrived[0]),
                          (W13raw[:, 1], w3[0].rearrange("(k p) f -> p k f", p=P), arrived[0]),
                          (W2raw[:], w2[0].rearrange("(k p) d -> p k d", p=P), arrived[1])])
        phase_route(nc, XT, gate_w, wts, p12, slots, over)
        overfull = nc.values_load(over[0:1, 0:1], min_val=0, max_val=1)
        with nc.If(overfull < 1):
            phase_moe_routed(nc, X, XT, XW, X2, XG, YG, w1, w3, w2, W13raw, W13, W2raw, W2, p12, slots, arrived, out)
        with nc.Else():
            phase_moe_dense(nc, X, XT, wts, w1, w3, w2, W13raw, W13, W2raw, W2, rows, arrived)
            phase_norm(nc, "n4", X, identF, out=out)


def rope_tables():
    inv = (1.0 / np.float32(1e6) ** (np.arange(0, HD, 2, dtype=np.float32) / np.float32(HD))).astype(np.float32)
    ang = inv[:, None] * np.arange(S, dtype=np.float32)[None, :]
    c, s = np.cos(ang).astype(np.float32), np.sin(ang).astype(np.float32)
    return np.stack([np.concatenate([c, c]), np.concatenate([s, -s])])


_INS = ['x', 'ctx_1024', 'mask_BxS2_bf1', 'L0_attn_W_in', 'L0_attn_W_out', 'L0_attn_log_A', 'L0_attn_W_dt', 'L0_attn_b_dt',
        'L0_xattn_Wq', 'L0_xattn_Wk', 'L0_xattn_Wv', 'L0_xattn_Wo', 'L0_ffn_norm1_w', 'L0_ffn_norm2_w', 'L0_ffn_wq',
        'L0_ffn_wk', 'L0_ffn_wv', 'L0_ffn_wo', 'L0_ffn_gate_w', 'L0_ffn_w1', 'L0_ffn_w3', 'L0_ffn_w2']


def kernel(**inputs):
    import numpy as _np
    import concourse.bacc as _bacc
    from concourse import mybir as _mybir
    from concourse.bass_utils import run_bass_kernel_spmd as _run

    nc = _bacc.Bacc("TRN2", target_bir_lowering=False, num_devices=1)
    arrays, args = {}, []
    for name in _INS:
        a = _np.ascontiguousarray(inputs[name])
        arrays[f"in_{name}_dram"] = a
        args.append(nc.dram_tensor(f"in_{name}_dram", a.shape, _mybir.dt.from_np(a.dtype), kind="ExternalInput").ap())
    arrays["rope_dram"] = rope_tables()
    args.append(nc.dram_tensor("rope_dram", (2, HD, S), F32, kind="ExternalInput").ap())
    for name in ("expert_rows_dram", "expert_out_dram"):
        args.append(nc.dram_tensor(name, (E * CAP, D), F32).ap())
    args.append(nc.dram_tensor("out_0_dram", (B, S, D), F32, kind="ExternalOutput").ap())
    decoder_layer(nc, *args)
    r = _run(nc, [arrays], core_ids=[0])
    return r.results[0]["out_0_dram"]
```
